# Optimizing a Trainium2 kernel written in Bass

```python
import numpy as np
import jax
import jax.numpy as jnp

def _softmax(x, axis=-1):
    return jax.nn.softmax(x, axis=axis)

def _gelu(x):
    return jax.nn.gelu(x, approximate=True)

def _silu(x):
    return jax.nn.silu(x)

def _sigmoid(x):
    return jax.nn.sigmoid(x)

def _layernorm(x, axis=-1, eps=1e-05):
    m = jnp.mean(x, axis=axis, keepdims=True)
    v = jnp.var(x, axis=axis, keepdims=True)
    return (x - m) / jnp.sqrt(v + eps)

def _scatter_add(tgt, idx, src, axis=0):
    return tgt.at[idx].add(src)

def _segment_sum(src, seg, n):
    return jax.ops.segment_sum(src, seg, n)
kernel_name = 'mk_conv_preact_d4_conv_nhwc128_r4_915453'

def setup_inputs(seed: int=0):
    np.random.seed(seed)
    _w = jnp.asarray

    def _rec_inputs():
        import jax
        import jax.numpy as jnp
        _gk = jax.random.key(seed)
        x = -0.0002091 + 1 * jax.random.normal(jax.random.fold_in(_gk, 1), (16, 28, 28, 32), jnp.float32)
        return x
    x = _rec_inputs()

    def _L0_conv_setup():
        import jax, jax.numpy as jnp
        import numpy as np
        WS = 7
        NUM_HEADS = 4
        DIM = 32
        key = jax.random.key(seed)
        k1, k2, k3, k4, k5 = jax.random.split(key, 5)
        B, H, W, C = (16, 28, 28, DIM)
        x = jax.random.normal(k1, (B, H, W, C), dtype=jnp.float32)
        w_qkv = jax.random.normal(k2, (C, 3 * C), dtype=jnp.float32) * 0.02
        b_qkv = jax.random.normal(k3, (3 * C,), dtype=jnp.float32) * 0.02
        w_proj = jax.random.normal(k4, (C, C), dtype=jnp.float32) * 0.02
        b_proj = jax.random.normal(k5, (C,), dtype=jnp.float32) * 0.02
        return {'x': x, 'w_qkv': w_qkv, 'b_qkv': b_qkv, 'w_proj': w_proj, 'b_proj': b_proj}
    _L0_conv_all = _L0_conv_setup()
    _L0_conv_in = {k: v for k, v in _L0_conv_all.items() if k in ('w_qkv', 'b_qkv', 'w_proj', 'b_proj')}
    del _L0_conv_all

    def _L1_conv_setup():
        import jax, jax.numpy as jnp
        import numpy as np
        D_STATE = 8
        DT_RANK = 8

        def _grouped_1x1(x, w):
            B, H, W, _ = x.shape
            g, o, i = w.shape
            xg = x.reshape(B, H, W, g, i)
            return jnp.einsum('bhwgi,goi->bhwgo', xg, w).reshape(B, H, W, g * o)

        def _mamba(x_seq, in_proj_w, conv1d_w, conv1d_b, x_proj_w, dt_proj_w, dt_proj_b, A_log, D_param, out_proj_w):
            B, L, D = x_seq.shape
            N, R = (D_STATE, DT_RANK)
            xz = jnp.einsum('bld,ed->ble', x_seq, in_proj_w)
            u, z = (xz[..., :D], xz[..., D:])
            up = jnp.pad(u, ((0, 0), (2, 0), (0, 0)))
            u = up[:, 0:L] * conv1d_w[:, 0] + up[:, 1:L + 1] * conv1d_w[:, 1] + up[:, 2:L + 2] * conv1d_w[:, 2] + conv1d_b
            u = jax.nn.silu(u)
            x_dbl = jnp.einsum('bld,ed->ble', u, x_proj_w)
            dt = x_dbl[..., :R]
            Bm = x_dbl[..., R:R + N]
            Cm = x_dbl[..., R + N:]
            delta = jax.nn.softplus(jnp.einsum('blr,dr->bld', dt, dt_proj_w) + dt_proj_b)
            A = -jnp.exp(A_log)

            def step(h, inp):
                d_t, u_t, b_t, c_t = inp
                dA = jnp.exp(d_t[..., None] * A)
                h = dA * h + (d_t * u_t)[..., None] * b_t[:, None, :]
                y_t = jnp.einsum('bdn,bn->bd', h, c_t)
                return (h, y_t)
            h0 = jnp.zeros((B, D, N), dtype=x_seq.dtype)
            xs = (jnp.swapaxes(delta, 0, 1), jnp.swapaxes(u, 0, 1), jnp.swapaxes(Bm, 0, 1), jnp.swapaxes(Cm, 0, 1))
            _, ys = jax.lax.scan(step, h0, xs)
            y = jnp.swapaxes(ys, 0, 1) + u * D_param
            y = y * jax.nn.silu(z)
            return jnp.einsum('bld,ed->ble', y, out_proj_w)
        key = jax.random.key(seed)
        ks = jax.random.split(key, 16)
        B, H, W, C = (8, 16, 16, 32)
        g = 4
        D = 32
        N = D_STATE
        R = DT_RANK
        inp = {}
        inp['x'] = jax.random.normal(ks[0], (B, H, W, C), dtype=jnp.float32)
        inp['w1'] = jax.random.normal(ks[1], (g, D // g, C // g), dtype=jnp.float32) * 0.1
        inp['dw'] = jax.random.normal(ks[2], (3, 3, 1, D), dtype=jnp.float32) * 0.1
        inp['in_proj_w'] = jax.random.normal(ks[3], (2 * D, D), dtype=jnp.float32) * 0.05
        inp['conv1d_w'] = jax.random.normal(ks[4], (D, 3), dtype=jnp.float32) * 0.1
        inp['conv1d_b'] = jax.random.normal(ks[5], (D,), dtype=jnp.float32) * 0.05
        inp['x_proj_w'] = jax.random.normal(ks[6], (R + 2 * N, D), dtype=jnp.float32) * 0.05
        inp['dt_proj_w'] = jax.random.normal(ks[7], (D, R), dtype=jnp.float32) * 0.05
        inp['dt_proj_b'] = jax.random.normal(ks[8], (D,), dtype=jnp.float32) * 0.05
        inp['A_log'] = jnp.log(jnp.tile(jnp.arange(1, N + 1, dtype=jnp.float32)[None, :], (D, 1)))
        inp['D_param'] = jnp.ones((D,), dtype=jnp.float32)
        inp['out_proj_w'] = jax.random.normal(ks[9], (D, D), dtype=jnp.float32) * 0.05
        inp['gamma'] = jnp.ones((D,), dtype=jnp.float32)
        inp['beta'] = jnp.zeros((D,), dtype=jnp.float32)
        inp['w2'] = jax.random.normal(ks[10], (g, D // g, C // g), dtype=jnp.float32) * 0.1
        inp['wout'] = jax.random.normal(ks[11], (g, C // g, D // g), dtype=jnp.float32) * 0.1
        return inp
    _L1_conv_all = _L1_conv_setup()
    _L1_conv_in = {k: v for k, v in _L1_conv_all.items() if k in ('w1', 'dw', 'in_proj_w', 'conv1d_w', 'conv1d_b', 'x_proj_w', 'dt_proj_w', 'dt_proj_b', 'A_log', 'D_param', 'out_proj_w', 'gamma', 'beta', 'w2', 'wout')}
    del _L1_conv_all

    def _L2_conv_setup():
        import jax, jax.numpy as jnp
        import numpy as np
        EPS = 1e-05

        def _ln(x, g, b):
            m = jnp.mean(x, axis=-1, keepdims=True)
            v = jnp.var(x, axis=-1, keepdims=True)
            return (x - m) / jnp.sqrt(v + EPS) * g + b
        key = jax.random.key(seed)
        ks = jax.random.split(key, 16)
        B, N, CZ, C = (1, 128, 32, 16)
        s_cz = 1.0 / np.sqrt(CZ)
        s_c = 1.0 / np.sqrt(C)

        def lin(k, fan_in, shape):
            return jax.random.uniform(k, shape, jnp.float32, -1.0, 1.0) / np.sqrt(fan_in)
        return {'x': jax.random.normal(ks[0], (B, N, N, CZ), jnp.float32), 'Wa1': lin(ks[1], CZ, (CZ, C)), 'ba1': lin(ks[2], CZ, (C,)), 'Wa2': lin(ks[3], CZ, (CZ, C)), 'ba2': lin(ks[4], CZ, (C,)), 'Wb1': lin(ks[5], CZ, (CZ, C)), 'bb1': lin(ks[6], CZ, (C,)), 'Wb2': lin(ks[7], CZ, (CZ, C)), 'bb2': lin(ks[8], CZ, (C,)), 'ln2_g': jnp.ones((C,), jnp.float32), 'ln2_b': jnp.zeros((C,), jnp.float32), 'Wg': lin(ks[9], CZ, (CZ, CZ)), 'bg': lin(ks[10], CZ, (CZ,)), 'Wz': lin(ks[11], C, (C, CZ)), 'bz': lin(ks[12], C, (CZ,))}
    _L2_conv_all = _L2_conv_setup()
    _L2_conv_in = {k: v for k, v in _L2_conv_all.items() if k in ('Wa1', 'ba1', 'Wa2', 'ba2', 'Wb1', 'bb1', 'Wb2', 'bb2', 'ln2_g', 'ln2_b', 'Wg', 'bg', 'Wz', 'bz')}
    del _L2_conv_all

    def _L3_conv_setup():
        import jax, jax.numpy as jnp
        import numpy as np
        B, T, N, F, H = (16, 32, 64, 32, 32)

        def _gclstm(x, Wix, Wim, Wfx, Wfm, Wcx, Wcm, Wox, Wom, bi, bf, bc, bo):
            b_, t_, n_, f_ = x.shape
            h_ = Wix.shape[1]
            Wx = jnp.concatenate([Wix, Wfx, Wox, Wcx], axis=1)
            Wm = jnp.concatenate([Wim, Wfm, Wom, Wcm], axis=1)
            bias = jnp.concatenate([bi, bf, bo, bc], axis=1)
            xw = jnp.einsum('btnf,fg->tbng', x, Wx) + bias

            def step(carry, xw_t):
                h, c = carry
                z = xw_t + h @ Wm
                zi, zf, zo, zg = jnp.split(z, 4, axis=-1)
                i = jax.nn.sigmoid(zi)
                f = jax.nn.sigmoid(zf)
                o = jax.nn.sigmoid(zo)
                g = jnp.tanh(zg)
                c_new = f * c + i * g
                h_new = o * jnp.tanh(c_new)
                return ((h_new, c_new), h_new)
            init = (jnp.zeros((b_, n_, h_), x.dtype), jnp.zeros((b_, n_, h_), x.dtype))
            _, states = jax.lax.scan(step, init, xw)
            return states.reshape(b_, t_, n_, h_)
        key = jax.random.key(seed)
        ks = jax.random.split(key, 9)
        s_x = (2.0 / (F + H)) ** 0.5
        s_m = (2.0 / (H + H)) ** 0.5
        return {'x': jax.random.normal(ks[0], (B, T, N, F), dtype=jnp.float32), 'Wix': jax.random.normal(ks[1], (F, H), dtype=jnp.float32) * s_x, 'Wim': jax.random.normal(ks[2], (H, H), dtype=jnp.float32) * s_m, 'Wfx': jax.random.normal(ks[3], (F, H), dtype=jnp.float32) * s_x, 'Wfm': jax.random.normal(ks[4], (H, H), dtype=jnp.float32) * s_m, 'Wcx': jax.random.normal(ks[5], (F, H), dtype=jnp.float32) * s_x, 'Wcm': jax.random.normal(ks[6], (H, H), dtype=jnp.float32) * s_m, 'Wox': jax.random.normal(ks[7], (F, H), dtype=jnp.float32) * s_x, 'Wom': jax.random.normal(ks[8], (H, H), dtype=jnp.float32) * s_m, 'bi': jnp.zeros((1, H), dtype=jnp.float32), 'bf': jnp.zeros((1, H), dtype=jnp.float32), 'bc': jnp.zeros((1, H), dtype=jnp.float32), 'bo': jnp.zeros((1, H), dtype=jnp.float32)}
    _L3_conv_all = _L3_conv_setup()
    _L3_conv_in = {k: v for k, v in _L3_conv_all.items() if k in ('Wix', 'Wim', 'Wfx', 'Wfm', 'Wcx', 'Wcm', 'Wox', 'Wom', 'bi', 'bf', 'bc', 'bo')}
    del _L3_conv_all
    return {'x': x, 'L0_conv_w_qkv': _L0_conv_in['w_qkv'], 'L0_conv_b_qkv': _L0_conv_in['b_qkv'], 'L0_conv_w_proj': _L0_conv_in['w_proj'], 'L0_conv_b_proj': _L0_conv_in['b_proj'], 'L1_conv_w1': _L1_conv_in['w1'], 'L1_conv_dw': _L1_conv_in['dw'], 'L1_conv_in_proj_w': _L1_conv_in['in_proj_w'], 'L1_conv_conv1d_w': _L1_conv_in['conv1d_w'], 'L1_conv_conv1d_b': _L1_conv_in['conv1d_b'], 'L1_conv_x_proj_w': _L1_conv_in['x_proj_w'], 'L1_conv_dt_proj_w': _L1_conv_in['dt_proj_w'], 'L1_conv_dt_proj_b': _L1_conv_in['dt_proj_b'], 'L1_conv_A_log': _L1_conv_in['A_log'], 'L1_conv_D_param': _L1_conv_in['D_param'], 'L1_conv_out_proj_w': _L1_conv_in['out_proj_w'], 'L1_conv_gamma': _L1_conv_in['gamma'], 'L1_conv_beta': _L1_conv_in['beta'], 'L1_conv_w2': _L1_conv_in['w2'], 'L1_conv_wout': _L1_conv_in['wout'], 'L2_conv_Wa1': _L2_conv_in['Wa1'], 'L2_conv_ba1': _L2_conv_in['ba1'], 'L2_conv_Wa2': _L2_conv_in['Wa2'], 'L2_conv_ba2': _L2_conv_in['ba2'], 'L2_conv_Wb1': _L2_conv_in['Wb1'], 'L2_conv_bb1': _L2_conv_in['bb1'], 'L2_conv_Wb2': _L2_conv_in['Wb2'], 'L2_conv_bb2': _L2_conv_in['bb2'], 'L2_conv_ln2_g': _L2_conv_in['ln2_g'], 'L2_conv_ln2_b': _L2_conv_in['ln2_b'], 'L2_conv_Wg': _L2_conv_in['Wg'], 'L2_conv_bg': _L2_conv_in['bg'], 'L2_conv_Wz': _L2_conv_in['Wz'], 'L2_conv_bz': _L2_conv_in['bz'], 'L3_conv_Wix': _L3_conv_in['Wix'], 'L3_conv_Wim': _L3_conv_in['Wim'], 'L3_conv_Wfx': _L3_conv_in['Wfx'], 'L3_conv_Wfm': _L3_conv_in['Wfm'], 'L3_conv_Wcx': _L3_conv_in['Wcx'], 'L3_conv_Wcm': _L3_conv_in['Wcm'], 'L3_conv_Wox': _L3_conv_in['Wox'], 'L3_conv_Wom': _L3_conv_in['Wom'], 'L3_conv_bi': _L3_conv_in['bi'], 'L3_conv_bf': _L3_conv_in['bf'], 'L3_conv_bc': _L3_conv_in['bc'], 'L3_conv_bo': _L3_conv_in['bo']}

def reference(x, L0_conv_w_qkv, L0_conv_b_qkv, L0_conv_w_proj, L0_conv_b_proj, L1_conv_w1, L1_conv_dw, L1_conv_in_proj_w, L1_conv_conv1d_w, L1_conv_conv1d_b, L1_conv_x_proj_w, L1_conv_dt_proj_w, L1_conv_dt_proj_b, L1_conv_A_log, L1_conv_D_param, L1_conv_out_proj_w, L1_conv_gamma, L1_conv_beta, L1_conv_w2, L1_conv_wout, L2_conv_Wa1, L2_conv_ba1, L2_conv_Wa2, L2_conv_ba2, L2_conv_Wb1, L2_conv_bb1, L2_conv_Wb2, L2_conv_bb2, L2_conv_ln2_g, L2_conv_ln2_b, L2_conv_Wg, L2_conv_bg, L2_conv_Wz, L2_conv_bz, L3_conv_Wix, L3_conv_Wim, L3_conv_Wfx, L3_conv_Wfm, L3_conv_Wcx, L3_conv_Wcm, L3_conv_Wox, L3_conv_Wom, L3_conv_bi, L3_conv_bf, L3_conv_bc, L3_conv_bo):
    import jax
    import jax.numpy as jnp

    def _L0_conv_ref(x, w_qkv, b_qkv, w_proj, b_proj):
        import jax, jax.numpy as jnp
        import numpy as np
        WS = 7
        NUM_HEADS = 4
        DIM = 32
        B, H, W, C = x.shape
        nh, hd = (NUM_HEADS, C // NUM_HEADS)
        scale = hd ** (-0.5)
        pad_h = (WS - H % WS) % WS
        pad_w = (WS - W % WS) % WS
        if pad_h > 0 or pad_w > 0:
            x = jnp.pad(x, ((0, 0), (0, pad_h), (0, pad_w), (0, 0)))
        Hp, Wp = (H + pad_h, W + pad_w)
        nH, nW = (Hp // WS, Wp // WS)
        win = x.reshape(B, nH, WS, nW, WS, C).transpose(0, 1, 3, 2, 4, 5)
        win = win.reshape(-1, WS * WS, C)
        nwin, N = (win.shape[0], WS * WS)
        qkv = win @ w_qkv + b_qkv
        qkv = qkv.reshape(nwin, N, 3, nh, hd).transpose(2, 0, 3, 1, 4)
        q, k, v = (qkv[0], qkv[1], qkv[2])
        attn = jnp.einsum('whnd,whmd->whnm', q, k) * scale
        attn = jax.nn.softmax(attn, axis=-1)
        out = jnp.einsum('whnm,whmd->whnd', attn, v)
        out = out.transpose(0, 2, 1, 3).reshape(nwin, N, C)
        out = out @ w_proj + b_proj
        out = out.reshape(B, nH, nW, WS, WS, C).transpose(0, 1, 3, 2, 4, 5)
        out = out.reshape(B, Hp, Wp, C)
        if pad_h > 0 or pad_w > 0:
            out = out[:, :H, :W, :]
        return out

    def _L1_conv_ref(x, w1, dw, in_proj_w, conv1d_w, conv1d_b, x_proj_w, dt_proj_w, dt_proj_b, A_log, D_param, out_proj_w, gamma, beta, w2, wout):
        import jax, jax.numpy as jnp
        import numpy as np
        D_STATE = 8
        DT_RANK = 8

        def _grouped_1x1(x, w):
            B, H, W, _ = x.shape
            g, o, i = w.shape
            xg = x.reshape(B, H, W, g, i)
            return jnp.einsum('bhwgi,goi->bhwgo', xg, w).reshape(B, H, W, g * o)

        def _mamba(x_seq, in_proj_w, conv1d_w, conv1d_b, x_proj_w, dt_proj_w, dt_proj_b, A_log, D_param, out_proj_w):
            B, L, D = x_seq.shape
            N, R = (D_STATE, DT_RANK)
            xz = jnp.einsum('bld,ed->ble', x_seq, in_proj_w)
            u, z = (xz[..., :D], xz[..., D:])
            up = jnp.pad(u, ((0, 0), (2, 0), (0, 0)))
            u = up[:, 0:L] * conv1d_w[:, 0] + up[:, 1:L + 1] * conv1d_w[:, 1] + up[:, 2:L + 2] * conv1d_w[:, 2] + conv1d_b
            u = jax.nn.silu(u)
            x_dbl = jnp.einsum('bld,ed->ble', u, x_proj_w)
            dt = x_dbl[..., :R]
            Bm = x_dbl[..., R:R + N]
            Cm = x_dbl[..., R + N:]
            delta = jax.nn.softplus(jnp.einsum('blr,dr->bld', dt, dt_proj_w) + dt_proj_b)
            A = -jnp.exp(A_log)

            def step(h, inp):
                d_t, u_t, b_t, c_t = inp
                dA = jnp.exp(d_t[..., None] * A)
                h = dA * h + (d_t * u_t)[..., None] * b_t[:, None, :]
                y_t = jnp.einsum('bdn,bn->bd', h, c_t)
                return (h, y_t)
            h0 = jnp.zeros((B, D, N), dtype=x_seq.dtype)
            xs = (jnp.swapaxes(delta, 0, 1), jnp.swapaxes(u, 0, 1), jnp.swapaxes(Bm, 0, 1), jnp.swapaxes(Cm, 0, 1))
            _, ys = jax.lax.scan(step, h0, xs)
            y = jnp.swapaxes(ys, 0, 1) + u * D_param
            y = y * jax.nn.silu(z)
            return jnp.einsum('bld,ed->ble', y, out_proj_w)
        B, H, W, C = x.shape
        D = dw.shape[-1]
        x1 = _grouped_1x1(x, w1)
        x1 = jax.lax.conv_general_dilated(x1, dw, window_strides=(1, 1), padding='SAME', feature_group_count=D, dimension_numbers=('NHWC', 'HWIO', 'NHWC'))
        x1 = jax.nn.silu(x1)
        x1_seq = x1.reshape(B, H * W, D)
        x1_seq = _mamba(x1_seq, in_proj_w, conv1d_w, conv1d_b, x_proj_w, dt_proj_w, dt_proj_b, A_log, D_param, out_proj_w)
        x1 = x1_seq.reshape(B, H, W, D)
        mu = jnp.mean(x1, axis=-1, keepdims=True)
        var = jnp.mean(jnp.square(x1 - mu), axis=-1, keepdims=True)
        x1 = (x1 - mu) * jax.lax.rsqrt(var + 1e-05) * gamma + beta
        x2 = jax.nn.silu(_grouped_1x1(x, w2))
        x_fuse = x1 * x2
        return _grouped_1x1(x_fuse, wout)

    def _L2_conv_ref(x, Wa1, ba1, Wa2, ba2, Wb1, bb1, Wb2, bb2, ln2_g, ln2_b, Wg, bg, Wz, bz):
        import jax, jax.numpy as jnp
        import numpy as np
        EPS = 1e-05

        def _ln(x, g, b):
            m = jnp.mean(x, axis=-1, keepdims=True)
            v = jnp.var(x, axis=-1, keepdims=True)
            return (x - m) / jnp.sqrt(v + EPS) * g + b
        direction = 'outgoing'
        a = jax.nn.sigmoid((x @ Wa1 + ba1) * (x @ Wa2 + ba2))
        b = jax.nn.sigmoid((x @ Wb1 + bb1) * (x @ Wb2 + bb2))
        if direction == 'incoming':
            a = jnp.swapaxes(a, 1, 2)
            b = jnp.swapaxes(b, 1, 2)
        g = jax.nn.sigmoid(x @ Wg + bg)
        z = jnp.einsum('bikc,bkjc->bijc', a, b)
        return g * (_ln(z, ln2_g, ln2_b) @ Wz + bz)

    def _L3_conv_ref(x, Wix, Wim, Wfx, Wfm, Wcx, Wcm, Wox, Wom, bi, bf, bc, bo):
        import jax, jax.numpy as jnp
        import numpy as np
        B, T, N, F, H = (16, 32, 64, 32, 32)

        def _gclstm(x, Wix, Wim, Wfx, Wfm, Wcx, Wcm, Wox, Wom, bi, bf, bc, bo):
            b_, t_, n_, f_ = x.shape
            h_ = Wix.shape[1]
            Wx = jnp.concatenate([Wix, Wfx, Wox, Wcx], axis=1)
            Wm = jnp.concatenate([Wim, Wfm, Wom, Wcm], axis=1)
            bias = jnp.concatenate([bi, bf, bo, bc], axis=1)
            xw = jnp.einsum('btnf,fg->tbng', x, Wx) + bias

            def step(carry, xw_t):
                h, c = carry
                z = xw_t + h @ Wm
                zi, zf, zo, zg = jnp.split(z, 4, axis=-1)
                i = jax.nn.sigmoid(zi)
                f = jax.nn.sigmoid(zf)
                o = jax.nn.sigmoid(zo)
                g = jnp.tanh(zg)
                c_new = f * c + i * g
                h_new = o * jnp.tanh(c_new)
                return ((h_new, c_new), h_new)
            init = (jnp.zeros((b_, n_, h_), x.dtype), jnp.zeros((b_, n_, h_), x.dtype))
            _, states = jax.lax.scan(step, init, xw)
            return states.reshape(b_, t_, n_, h_)
        return _gclstm(x, Wix, Wim, Wfx, Wfm, Wcx, Wcm, Wox, Wom, bi, bf, bc, bo)

    def _gn(v, G=32, eps=1e-05):
        B_, H_, W_, C_ = v.shape
        g = v.reshape(B_, H_, W_, G, C_ // G)
        m = jnp.mean(g, axis=(1, 2, 4), keepdims=True)
        s = jnp.var(g, axis=(1, 2, 4), keepdims=True)
        return ((g - m) / jnp.sqrt(s + eps)).reshape(v.shape)

    def _ln_c(v, eps=1e-06):
        m = jnp.mean(v, axis=-1, keepdims=True)
        s = jnp.var(v, axis=-1, keepdims=True)
        return (v - m) / jnp.sqrt(s + eps)

    def _ln_t(v, eps=1e-05):
        m = jnp.mean(v, axis=-1, keepdims=True)
        s = jnp.var(v, axis=-1, keepdims=True)
        return (v - m) / jnp.sqrt(s + eps)

    def _to_tokens(v):
        B_, H_, W_, C_ = v.shape
        return v.reshape(B_, H_ * W_, C_)

    def _from_tokens(t, like):
        return t.reshape(like.shape)
    x = x + _L0_conv_ref(_gn(x), L0_conv_w_qkv, L0_conv_b_qkv, L0_conv_w_proj, L0_conv_b_proj)
    x = x + _L1_conv_ref(_gn(x), L1_conv_w1, L1_conv_dw, L1_conv_in_proj_w, L1_conv_conv1d_w, L1_conv_conv1d_b, L1_conv_x_proj_w, L1_conv_dt_proj_w, L1_conv_dt_proj_b, L1_conv_A_log, L1_conv_D_param, L1_conv_out_proj_w, L1_conv_gamma, L1_conv_beta, L1_conv_w2, L1_conv_wout)
    x = x + _L2_conv_ref(_gn(x), L2_conv_Wa1, L2_conv_ba1, L2_conv_Wa2, L2_conv_ba2, L2_conv_Wb1, L2_conv_bb1, L2_conv_Wb2, L2_conv_bb2, L2_conv_ln2_g, L2_conv_ln2_b, L2_conv_Wg, L2_conv_bg, L2_conv_Wz, L2_conv_bz)
    x = x + _L3_conv_ref(_gn(x), L3_conv_Wix, L3_conv_Wim, L3_conv_Wfx, L3_conv_Wfm, L3_conv_Wcx, L3_conv_Wcm, L3_conv_Wox, L3_conv_Wom, L3_conv_bi, L3_conv_bf, L3_conv_bc, L3_conv_bo)
    return x

_drawn_inputs = setup_inputs


def setup_inputs(seed=0):
    import zlib

    import numpy as np

    out = dict(_drawn_inputs(seed))
    spreads = {'L1_conv_D_param': (1.0, 0.6),
     'L1_conv_gamma': (1.0, 0.6),
     'L1_conv_beta': (0.0, 0.8),
     'L2_conv_ln2_g': (1.0, 0.6),
     'L2_conv_ln2_b': (0.0, 1.905),
     'L3_conv_bi': (0.0, 2.0),
     'L3_conv_bf': (0.0, 2.0),
     'L3_conv_bc': (0.0, 0.8),
     'L3_conv_bo': (0.0, 2.0)}
    factors = {'L0_conv_w_qkv': 8.0,
     'L0_conv_b_qkv': 8.0,
     'L0_conv_w_proj': 8.0,
     'L0_conv_b_proj': 19.037,
     'L1_conv_w1': 8.0,
     'L1_conv_dw': 8.0,
     'L1_conv_in_proj_w': 8.0,
     'L1_conv_conv1d_w': 8.0,
     'L1_conv_conv1d_b': 8.0,
     'L1_conv_x_proj_w': 8.0,
     'L1_conv_dt_proj_w': 8.0,
     'L1_conv_dt_proj_b': 8.0,
     'L1_conv_A_log': 8.0,
     'L1_conv_out_proj_w': 8.0,
     'L1_conv_w2': 8.0,
     'L1_conv_wout': 8.0,
     'L2_conv_bg': 19.407,
     'L3_conv_Wim': 22.39,
     'L3_conv_Wfm': 25.67,
     'L3_conv_Wom': 20.178,
     'L2_conv_ba1': 8.0,
     'L2_conv_ba2': 8.0,
     'L2_conv_bb1': 8.0,
     'L2_conv_bb2': 8.0,
     'L2_conv_Wg': 4.687,
     'L2_conv_bz': 5.359,
     'L3_conv_Wix': 3.896,
     'L3_conv_Wfx': 7.433,
     'L3_conv_Wcm': 4.852,
     'L3_conv_Wox': 4.859}
    for name, (base, spread) in spreads.items():
        noise = np.random.default_rng([zlib.crc32(name.encode()), seed]).standard_normal(out[name].shape)
        drawn = base * np.exp(spread * noise) if base else spread * noise
        out[name] = jnp.asarray(drawn.astype(out[name].dtype))
    for name, factor in factors.items():
        out[name] = (out[name] * factor).astype(out[name].dtype)
    return out
```

```python
import numpy as np

import concourse.bass as bass
from concourse import mybir
from contextlib import ExitStack

F32 = mybir.dt.float32
ALU = mybir.AluOpType
ACT = mybir.ActivationFunctionType
AX = mybir.AxisListType

P = 128
B, H, W, C = 16, 28, 28, 32
G = P // C
J = B // G
T = H * W
N = J * T
SP = 7
LP = T // SP
WS = 7
WT = WS * WS
WP = 64
NH, HD = 4, 8
NW = W // WS
ST = WS * W
NS = N // ST
R, DS = 8, 8
C2 = 16
HT = T // 2
EPS = 1e-5
SCALE = HD ** -0.5

(U_Q, U_K, U_V, U_P, U_A, U_B, U_G, U_X, U_M) = (0, 1, 2, 3, 4, 5, 6, 7, 11)
(U_Z, U_X2, U_WO, U_OUT, U_U, U_CV, U_DL, NU) = (15, 16, 17, 18, 19, 22, 31, 32)


def build(nc, a, out):
    ctx = ExitStack()
    with ctx:
        def sb(name, shape, stack=ctx):
            return stack.enter_context(nc.sbuf_tensor(name, shape, F32))

        def sem(name):
            return ctx.enter_context(nc.semaphore(name))

        X = sb("X", [P, N])
        XN = sb("XN", [P, J * 30 * 30])
        BD = sb("BD", [P, NU, P])
        BC = sb("BC", [P, 2 * DS, P])
        ident = sb("ident", [P, P])
        bd = sb("bd", [P, G])
        m16 = sb("m16", [P, 16])
        mask8 = sb("mask8", [P, NH])
        m8 = sb("m8", [P, 8])
        maskz = sb("maskz", [P, G])
        WZ = sb("WZ", [P, P])
        VB = sb("VB", [P, P])
        ones = sb("ones", [1, 512])
        rowA = sb("rowA", [1, 16, C])
        rowB = sb("rowB", [1, 16, C])
        BL = sb("BL", [4, G, C])
        half3 = sb("half3", [4, 1])
        smallr = sb("smallr", [1, 2, C])
        epsc = sb("epsc", [P, 1])
        vec = sb("vec", [P, 16])
        (V_BQ, V_BK, V_BV, V_BP, V_CB, V_DTB, V_D, V_GA, V_BE, V_BG, V_BZ, V_LG, V_BQS, V_BZF) = range(14)
        lnb = sb("lnb", [C2, 1])
        Aneg = sb("Aneg", [P, DS])
        stats = sb("stats", [P, J, 2, 6])
        mv = sb("mv", [P, J, 2])
        lnv = sb("lnv", [P, J])
        rstd = sb("rstd", [P, J])

        pairs = [ctx.enter_context(nc.psum_tensor(f"pair{i}", [P, 2, 512], F32)) for i in range(4)]
        banks = [pairs[i // 2][:, i % 2, :] for i in range(8)]
        TRB = 5

        setup = ExitStack()
        XT = sb("XT", [P, J, G, SP, C], setup)
        XS = sb("XS", [P, J, SP, G, C], setup)
        W4 = sb("W4", [P, NU, C], setup)
        NB = sb("NB", [P, 18, C], setup)
        TB = sb("TB", [P, 18, C], setup)
        W8 = sb("W8", [P, 3, 8], setup)
        W8X = sb("W8X", [P, C], setup)
        DW = sb("DW", [P, 9], setup)
        C1 = sb("C1", [P, 3], setup)
        AL = sb("AL", [P, DS], setup)
        AE = sb("AE", [P, DS], setup)
        WIN = sb("WIN", [P, 1, C], setup)
        wzraw = sb("wzraw", [P, C], setup)
        wzs = sb("wzs", [P, C], setup)
        wzn = sb("wzn", [C2, C], setup)
        omean = sb("omean", [P, 1], setup)
        setup.close()

        att = ExitStack()
        xw = sb("xw", [P, 2, NW, 2, WP], att)
        Qw = sb("Qw", [P, 2, NW, WP], att)
        Ks = sb("Ks", [P, 2, NW, WT], att)
        Km = sb("Km", [P, 2, NW, NH, WT], att)
        Vst = sb("Vst", [P, 2, NW, G, 2, C], att)
        Ts = sb("Ts", [P, G, 8, WT], att)
        Pr = sb("Pr", [P, 2, G, 8, WP], att)
        PT = sb("PT", [P, 2, 2, 2, P], att)
        AO = sb("AO", [P, 2, ST], att)
        mx = sb("mx", [P, G, 8], att)
        sm = sb("sm", [P, G, 8], att)
        rc = sb("rc", [P, G, 8], att)
        att.close()

        ssm = ExitStack()
        S1 = sb("S1", [P, J, T + 2], ssm)
        US = sb("US", [P, J, T], ssm)
        ZS = sb("ZS", [P, J, T], ssm)
        X2 = sb("X2", [P, J, T], ssm)
        YA = sb("YA", [P, T], ssm)
        DL = sb("DL", [P, T], ssm)
        DU = sb("DU", [P, T], ssm)
        dA = sb("dA", [P, 2, T], ssm)
        dBu = sb("dBu", [P, 2, T], ssm)
        Hs = sb("Hs", [P, 2, T], ssm)
        hC = sb("hC", [P, 2, T], ssm)
        sp = sb("sp", [P, 7, T], ssm)
        mxd = sb("mxd", [P, T], ssm)
        y1 = sb("y1", [P, T], ssm)
        y2 = sb("y2", [P, T], ssm)
        nt = sb("nt", [P, 3, T], ssm)
        sq = sb("sq", [P, 3, T], ssm)
        ssm.close()

        tri = ExitStack()
        XR = sb("XR", [P, 2, H, J, 32], tri)
        Ab = sb("Ab", [P, 2, 64, H], tri)
        p1 = sb("p1", [P, 2, 256], tri)
        pp = sb("pp", [P, 2, 256], tri)
        Zc = sb("Zc", [P, H, 64], tri)
        Zq = sb("Zq", [P, 2, 448], tri)
        zst = sb("zst", [P, G, 4, H], tri)
        ZT = sb("ZT", [P, 14 * P], tri)
        Gt = sb("Gt", [P, J, T], tri)
        Y = sb("Y", [P, J, T], tri)
        tri.close()

        rec = ExitStack()
        Rt = sb("Rt", [112, 112, C], rec)
        gates = sb("gates", [P, 2, 4, 112], rec)
        hst = sb("hst", [P, 2, 112], rec)
        cst = sb("cst", [P, 2, 112], rec)
        t1 = sb("t1", [P, 112], rec)
        t2 = sb("t2", [P, 112], rec)
        tcn = sb("tcn", [P, 112], rec)
        Os = sb("Os", [112, 2, G, C], rec)
        rec.close()

        s_x = [sem(f"s_x{j}") for j in range(J)]
        s_xs = [sem(f"s_xs{j}") for j in range(J)]
        s_wp = sem("s_wp")
        s_w = sem("s_w")
        s_z0 = sem("s_z0")
        s_mk = sem("s_mk")
        s_mk2 = sem("s_mk2")
        s_v = sem("s_v")
        s_a = sem("s_a")
        s_tr = sem("s_tr")
        s_ev = sem("s_ev")
        s_hf = sem("s_hf")
        s_ae = sem("s_ae")
        s_wd = sem("s_wd")
        s_mv = sem("s_mv")
        s_rs = sem("s_rs")
        s_xn = sem("s_xn")

        qk_d, q_r, k_r, km_r, xw_r, v_r, s_r, sub_r, exp_r, max_r, sum_r, rec_r, pn_r, t_r, ring_r, av_r, ao_r, pj_r, x1_r, = \
            [sem("a_" + n) for n in "qk q k km xw v s sub exp max sum rec pn t ring av ao pj x1".split()]
        pe_u, arel, drel, sp1, sp2, sp3, sp4, sp5, sp6, sp7, dl_r, du_r, da_r, db_r, sc_r, hc_r, ya_r, y1_r, y2_r, r1_r, rs_r, nt1, nt2, xf_r, x2_r, s1z = \
            [sem("m_" + n) for n in "peu arel drel sp1 sp2 sp3 sp4 sp5 sp6 sp7 dl du da db sc hc ya y1 y2 r1 rs nt1 nt2 xf x2 s1z".split()]
        t_pr, t_p1, t_pp, t_sg, t_z, t_zc, t_c, t_q, t_v, t_r1, t_r2, t_n, t_t, t_te, t_o, t_y, t_g, t_gd, t_x3, t_zz, t_xr = \
            [sem("t_" + n) for n in "pr p1 pp sg z zc c q v r1 r2 n t te o y g gd x3 zz xr".split()]
        r_t, r_te, r_z, r_g, r_1, r_2, r_c, r_th, r_h, r_o, r_os, r_in, r_1b = \
            [sem("r_" + n) for n in "t te z g 1 2 c th h o os in 1b".split()]
        s_out = [sem("s_out0"), sem("s_out1")]

        block = ctx.enter_context(nc.Block())

        def strip(s):
            return bass.ds(s * ST, ST)

        def windows(ap):
            return ap.rearrange("p (r w c) -> p w r c", r=WS, w=NW)

        def bcast(ap, axis, n):
            ap = ap.unsqueeze(axis)
            shape = list(ap.shape)
            shape[axis] = n
            return ap.broadcast_to(shape)

        def flat(buf):
            return buf[:, :, :].rearrange("p b t -> p (b t)")

        def col_of(buf, i):
            n = buf.shape[2]
            return flat(buf)[:, bass.ds(i * n, n)]

        def two_banks(k):
            return pairs[k % 4][:, :, 0:HT]

        def evac_in(eng, q):
            n, stop = 4 * q, 4 * q + 4
            while n < stop:
                j, s = divmod(n, SP)
                m = min(stop - n, SP - s)
                src = banks[q][:, LP * (n % 4):LP * (n % 4 + m)].rearrange("p (s t) -> p s t", s=m)
                dst = X[:, T * j:T * j + T].rearrange("p (t s) -> p s t", s=SP)[:, s:s + m]
                ins = (eng.activation(dst, src, ACT.Copy) if eng is nc.scalar else eng.tensor_copy(dst, src))
                n += m
            ins.then_inc(s_ev, 1)

        def halves(ap):
            return ap.rearrange("p (h t) -> p h t", h=2)

        USES = ["conv", "x2", "u", "z", "delta"] + [f"{m}{n}" for n in range(DS) for m in "BC"] + ["out", "var", "wout"]
        D_ORDER = ["delta", "B0"] + [x for n in range(1, DS) for x in (f"B{n}", f"C{n - 1}")] + [f"C{DS - 1}", "out", "wout"]
        A_ORDER = ["conv", "x2", "u", "z", "delta", "out", "var"]

        def used(k):
            b0, b1 = banks[2 * (k % 4)], banks[2 * (k % 4) + 1]
            return b0, b1

        def rep(dram, off, rows, cols, stride):
            return bass.AP(dram.tensor, off, [[0, G], [stride, rows], [1, cols]])

        loads = [0, 0]

        def load(eng, dst, src):
            own = int(eng is nc.gpsimd)
            eng.dma_start(dst, src).then_inc((s_w, s_wp)[own], 16)
            loads[own] += 1

        def all_loads(eng):
            eng.wait_ge(s_w, 16 * loads[0])
            eng.wait_ge(s_wp, 16 * loads[1])

        @block.sync
        def _(eng):
            xv = a["x"].rearrange("b h w c -> b (h w c)").rearrange("(g j) (p s c) -> j p g (s c)", g=G, p=LP, c=C)
            for j in range(J):
                eng.dma_start(XT[0:LP, j].rearrange("p g s c -> p g (s c)"), xv[j]).then_inc(s_x[j], 16)
            eng.wait_ge(s_z0, 1)

            def w4(u, name, off=0, cols=C, stride=C, c0=0):
                load(eng, W4[:, u, c0:c0 + cols], rep(a[name], off, C, cols, stride))
            for u in range(3):
                w4(U_Q + u, "L0_conv_w_qkv", off=C * u, stride=3 * C)
            w4(U_P, "L0_conv_w_proj")
            for u, m in ((U_A, "a"), (U_B, "b")):
                for t in range(2):
                    w4(u, f"L2_conv_W{m}{t + 1}", cols=C2, stride=C2, c0=C2 * t)
            w4(U_G, "L2_conv_Wg")
            for k, m in enumerate("ifoc"):
                w4(U_X + k, f"L3_conv_W{m}x")
                w4(U_M + k, f"L3_conv_W{m}m")
            load(eng, NB[:, 0, :], rep(a["L1_conv_in_proj_w"], C * C, C, C, C))
            load(eng, WIN[:, 0, :], rep(a["L1_conv_in_proj_w"], 0, C, C, C))
            load(eng, NB[:, 3, :], rep(a["L1_conv_out_proj_w"], 0, C, C, C))
            load(eng, NB[:, 16, 0:R], rep(a["L1_conv_dt_proj_w"], 0, C, R, R))
            for g in range(G):
                load(eng, NB[C * g:C * g + R + 2 * DS, 17, :], a["L1_conv_x_proj_w"])
            for k, m in enumerate(("w1", "w2", "wout")):
                load(eng, W8[:, k, :], rep(a["L1_conv_" + m], 0, C, 8, 8))
            load(eng, AL[:, :], rep(a["L1_conv_A_log"], 0, C, DS, DS))
            load(eng, C1[:, :], rep(a["L1_conv_conv1d_w"], 0, C, 3, 3))
            load(eng, wzraw[:, :], bass.AP(a["L2_conv_Wz"].tensor, 0, [[0, 8], [C, C2], [1, C]]))
            load(eng, wzn[:, :], a["L2_conv_Wz"])

            ov = out.rearrange("b h w c -> (b h w c)").rearrange("(r p c) -> p r c", p=112, c=C)

            def store(t, par):
                eng.wait_ge(r_o, t + 1)
                eng.dma_start(ov[:, bass.ds(t * 4, 4), :], Os[:, par]).then_inc(s_out[par], 16)
            with eng.Fori(0, H // 2) as it:
                store(it * 2, 0)
                store(it * 2 + 1, 1)
            for p_ in range(2):
                eng.wait_ge(s_out[p_], 16 * (H // 2))

        @block.gpsimd
        def _(eng):
            eng.memset(NB[:, 16:18, :], 0.0).then_inc(s_z0, 1)
            eng.memset(ident[:, :], 0.0).then_inc(s_mk, 1)
            for m in (bd, m16, m8, ones):
                eng.memset(m[:, :], 1.0).then_inc(s_mk, 1)
            eng.wait_ge(s_mk, 5)
            eng.affine_select(out=ident[:, :], in_=ident[:, :], compare_op=ALU.not_equal, fill=1.0,
                              base=0, pattern=[[-1, P]], channel_multiplier=1).then_inc(s_mk, 1)
            for m, w, n in ((bd, 32, G), (m16, 8, 16), (m8, 16, 8)):
                eng.affine_select(out=m[:, :], in_=m[:, :], compare_op=ALU.is_ge, fill=0.0,
                                  base=0, pattern=[[-w, n]], channel_multiplier=1).then_inc(s_mk, 1)
            eng.memset(half3[:, :], 0.5).then_inc(s_hf, 1)
            eng.wait_ge(s_hf, 1)
            eng.affine_select(out=half3[:, :], in_=half3[:, :], compare_op=ALU.not_equal, fill=1.0,
                              base=-3, pattern=[[0, 1]], channel_multiplier=1).then_inc(s_hf, 1)
            eng.wait_ge(s_mk, 9)
            for m, w, n in ((bd, 32, G), (m16, 8, 16), (m8, 16, 8)):
                eng.affine_select(out=m[:, :], in_=m[:, :], compare_op=ALU.is_ge, fill=0.0,
                                  base=w - 1, pattern=[[w, n]], channel_multiplier=-1).then_inc(s_mk, 1)
            with nc.allow_non_contiguous_dma(reason="small per-channel vectors"):
                def col(k, name, off=0):
                    load(eng, vec[:, k:k + 1], bass.AP(a[name].tensor, off, [[0, G], [1, C], [1, 1]]))
                for k in range(3):
                    col(V_BQ + k, "L0_conv_b_qkv", C * k)
                col(V_BP, "L0_conv_b_proj")
                col(V_CB, "L1_conv_conv1d_b")
                col(V_DTB, "L1_conv_dt_proj_b")
                col(V_D, "L1_conv_D_param")
                col(V_GA, "L1_conv_gamma")
                col(V_BE, "L1_conv_beta")
                col(V_BG, "L2_conv_bg")
                col(V_BZ, "L2_conv_bz")
                load(eng, vec[:, V_LG:V_LG + 1], bass.AP(a["L2_conv_ln2_g"].tensor, 0, [[0, 8], [1, C2], [1, 1]]))
                load(eng, lnb[:, :], bass.AP(a["L2_conv_ln2_b"].tensor, 0, [[1, C2], [1, 1]]))
                for g in range(G):
                    load(eng, DW[C * g:C * g + C, :], bass.AP(a["L1_conv_dw"].tensor, 0, [[1, C], [C, 9]]))
            for k, m in enumerate(("ba1", "ba2", "bb1", "bb2")):
                load(eng, smallr[0:1, k // 2, C2 * (k % 2):C2 * (k % 2) + C2], a["L2_conv_" + m].rearrange("(a n) -> a n", a=1))
            for k, m in enumerate("ifoc"):
                load(eng, BL[k:k + 1, :, :], bass.AP(a["L3_conv_b" + m].tensor, 0, [[0, 1], [0, G], [1, C]]))

            eng.wait_ge(s_ev, 8)
            eng.wait_ge(s_xn, J)
            for m in (xw, Qw, Vst, Pr):
                eng.memset(m[:], 0.0).then_inc(s_mk2, 1)
            eng.wait_ge(s_mk2, 4)

            def pool_att(s, par):
                nxt = not isinstance(s, int) or s + 1 < NS
                cur = not isinstance(s, int) or s >= 0
                np_ = 1 - par
                if nxt:
                    if isinstance(s, int) and s < 0:
                        eng.wait_ge(s_xn, J)
                    if not isinstance(s, int) or s >= 1:
                        eng.wait_ge(v_r, s)
                    for u in range(2):
                        ins = eng.tensor_copy(xw[:, np_, :, u, 0:WT].rearrange("p w (r c) -> p w r c", r=WS),
                                              windows(XN[:, strip(s + 1)]))
                    ins.then_inc(xw_r, 1)
                    eng.wait_ge(k_r, s + 2)
                    if not isinstance(s, int) or s >= 1:
                        eng.wait_ge(s_r, s)
                    eng.tensor_tensor(Km[:, np_], bcast(Ks[:, np_], 2, NH), bcast(bcast(mask8[:, :], 1, NW), 3, WT),
                                      ALU.mult).then_inc(km_r, 1)
                if cur:
                    for g in range(G):
                        eng.wait_ge(rec_r, 4 * s + g + 1)
                        pg = Pr[:, par, g, :, 0:WT]
                        eng.tensor_tensor(pg, pg, bcast(rc[:, g, :], 2, WT), ALU.mult).then_inc(pn_r, 1)

            for s in (-1, 0, 1, 2):
                pool_att(s, s % 2)
            with eng.Fori(0, 6) as it:
                pool_att(it * 2 + 3, 1)
                pool_att(it * 2 + 4, 0)
            pool_att(15, 1)

            eng.wait_ge(x1_r, NS)
            eng.memset(S1[:, :, 0:2], 0.0).then_inc(s1z, 1)

            def pool_ssm(i):
                for n in range(1, DS):
                    eng.wait_ge(drel, len(D_ORDER) * i + D_ORDER.index(f"C{n}") + 1)
                    if n > 1:
                        eng.wait_ge(ya_r, (DS - 1) * i + n - 1)
                    eng.tensor_tensor(YA[:, :], YA[:, :], hC[:, n % 2, :], ALU.add).then_inc(ya_r, 1)
            pool_ssm(0)
            with eng.Fori(1, J) as i:
                pool_ssm(i)

            eng.wait_ge(drel, len(D_ORDER) * J)
            for m in (Zc, XR):
                eng.memset(m[:], 0.0).then_inc(t_zz, 1)

        @block.scalar
        def _(eng):
            chain = [0]

            def link(ins):
                chain[0] += 1
                ins.then_inc(s_a, 1)
                eng.wait_ge(s_a, chain[0])

            for j in range(1, J, 2):
                eng.wait_ge(s_x[j], 16)
                eng.activation(XS[0:LP, j].rearrange("p s g c -> p g s c"), XT[0:LP, j], ACT.Copy).then_inc(s_xs[j], 1)
            for q in range(1, 7, 2):
                eng.wait_ge(s_tr, q + 1)
                evac_in(eng, q)
            all_loads(eng)
            eng.activation(AE[:, :], AL[:, :], ACT.Exp).then_inc(s_ae, 1)

            def gn(layer):
                eng.wait_ge(s_mv, layer + 1)
                if layer:
                    eng.wait_ge(s_xn, J * layer)
                link(eng.activation(lnv[:, :], mv[:, :, 1], ACT.Ln, bias=epsc[:, 0:1]))
                eng.activation(rstd[:, :], lnv[:, :], ACT.Exp, scale=-0.5).then_inc(s_rs, 1)

            gn(0)

            eng.wait_ge(s_mk2, 4)

            def act_att(s, par):
                fixed = isinstance(s, int)
                nxt = not fixed or s + 1 < NS
                cur = not fixed or 0 <= s < NS
                prv = not fixed or 1 <= s <= NS
                np_ = 1 - par
                if nxt:
                    eng.wait_ge(qk_d, s + 2)
                    if not fixed or s >= 1:
                        eng.wait_ge(s_r, s)
                    eng.activation(Qw[:, np_, :, 0:WT].rearrange("p w (r c) -> p w r c", r=WS),
                                   windows(banks[4][:, 0:ST]), ACT.Identity,
                                   bias=vec[:, V_BQS:V_BQS + 1], scale=SCALE).then_inc(q_r, 1)
                    if not fixed or s >= 1:
                        eng.wait_ge(km_r, s)
                    eng.activation(Ks[:, np_].rearrange("p w (r c) -> p w r c", r=WS),
                                   windows(banks[4][:, ST:2 * ST]), ACT.Identity,
                                   bias=vec[:, V_BK:V_BK + 1]).then_inc(k_r, 1)
                for g in range(G):
                    if prv:
                        eng.wait_ge(t_r, 4 * (s - 1) + g + 1)
                        if not fixed or 4 * (s - 1) + g >= 2:
                            eng.wait_ge(av_r, 4 * (s - 1) + g - 1)
                        eng.activation(PT[:, g % 2].rearrange("p a b q -> p (a b q)"),
                                       banks[5 + (par + 1 + g) % 2][:, :], ACT.Copy).then_inc(ring_r, 1)
                    if cur:
                        eng.wait_ge(sub_r, 4 * s + g + 1)
                        if not fixed or s >= 2:
                            eng.wait_ge(t_r, 4 * (s - 2) + g + 1)
                        eng.activation(Pr[:, par, g, :, 0:WT], Ts[:, g, :, :], ACT.Exp).then_inc(exp_r, 1)
                if nxt:
                    eng.wait_ge(v_r, s + 2)
                    if not fixed or s >= 1:
                        eng.wait_ge(av_r, 4 * s)
                    vb = banks[5 + (par + 1) % 2]
                    for u in range(2):
                        src = vb[64 * u:64 * u + 64, :].rearrange("p (m e q d) -> p m e q d", m=16, e=2, q=2)[:, :, :, u, :]
                        dst = Vst[64 * u:64 * u + 64, np_].rearrange("p w g e n -> p (w g) (e n)")
                        dst = bass.AP(dst.tensor, dst.offset + HD * u, [list(dst.ap[0]), [64, 16], [48, 2], [1, HD]])
                        eng.activation(dst, src, ACT.Copy).then_inc(ring_r, 1)

            for s in (-1, 0, 1, 2):
                act_att(s, s % 2)
            with eng.Fori(0, 6) as it:
                act_att(it * 2 + 3, 1)
                act_att(it * 2 + 4, 0)
            act_att(15, 1)
            act_att(16, 0)

            gn(1)

            eng.wait_ge(s1z, 1)

            def act_ssm(i):
                fixed = isinstance(i, int)
                first = fixed and i == 0
                U = len(USES)

                def ready(k):
                    eng.wait_ge(pe_u, U * i + k + 1)

                def at(buf):
                    return col_of(buf, i)
                ready(0)
                eng.activation(halves(at(S1)[:, 2:T + 2]), two_banks(0), ACT.Silu).then_inc(arel, 1)
                ready(1)
                eng.activation(halves(at(X2)), two_banks(1), ACT.Silu).then_inc(arel, 1)
                ready(2)
                eng.activation(halves(at(US)), two_banks(2), ACT.Silu, bias=vec[:, V_CB:V_CB + 1]).then_inc(arel, 1)
                ready(3)
                eng.activation(halves(at(ZS)), two_banks(3), ACT.Silu).then_inc(arel, 1)
                ready(4)
                if not first:
                    eng.wait_ge(sp3, i)
                eng.activation(halves(sp[:, 0, :]), two_banks(4), ACT.Abs, bias=vec[:, V_DTB:V_DTB + 1]).then_inc(arel, 1)
                eng.wait_ge(arel, len(A_ORDER) * i + 5)
                eng.activation(sp[:, 1, :], sp[:, 0, :], ACT.Exp, scale=-1.0).then_inc(sp1, 1)
                eng.wait_ge(sp1, i + 1)
                eng.wait_ge(sp2, i + 1)
                eng.activation(sp[:, 3, :], sp[:, 2, :], ACT.Ln).then_inc(sp3, 1)
                eng.wait_ge(sp3, i + 1)
                eng.activation(sp[:, 4, :], sp[:, 3, :], ACT.Exp, scale=-1.0).then_inc(sp4, 1)
                eng.wait_ge(dl_r, i + 1)
                for n in range(DS):
                    if n >= 2 or not first:
                        eng.wait_ge(sc_r, DS * i + n - 1)
                    eng.activation(dA[:, n % 2, :], DL[:, :], ACT.Exp, scale=Aneg[:, n:n + 1]).then_inc(da_r, 1)
                ready(21)
                if not first:
                    eng.wait_ge(pe_u, U * i)
                eng.activation(halves(sq[:, 0, :]), two_banks(21), ACT.Square).then_inc(arel, 1)
                ready(22)
                eng.activation(halves(sq[:, 1, :]), two_banks(22), ACT.Ln, bias=epsc[:, 0:1]).then_inc(arel, 1)
                eng.wait_ge(arel, len(A_ORDER) * i + 7)
                if not first:
                    eng.wait_ge(nt1, i)
                eng.activation(sq[:, 2, :], sq[:, 1, :], ACT.Exp, scale=-0.5).then_inc(rs_r, 1)

            act_ssm(0)
            with eng.Fori(1, J) as i:
                act_ssm(i)

            gn(2)

            for n in range(14):
                side, q = n // 7, n % 7
                eng.wait_ge(t_pr, n + 1)
                if n >= 2:
                    eng.wait_ge(t_pp, n - 1)
                bk = banks[n % 2][:, :].rearrange("p (i g t c) -> p i g t c", i=4, g=G, t=2)
                eng.activation(p1[:, n % 2].rearrange("p (i g c) -> p i g c", i=4, g=G), bk[:, :, :, 0, :],
                               ACT.Copy).then_inc(t_p1, 1)
                eng.wait_ge(t_pp, n + 1)
                eng.activation(Ab[:, side, :, 4 * q:4 * q + 4].rearrange("p m i -> p i m"),
                               pp[:, n % 2].rearrange("p (i m) -> p i m", i=4), ACT.Sigmoid).then_inc(t_sg, 1)
            for n in range(8):
                eng.wait_ge(t_g, n + 1)
                eng.activation(flat(Gt)[:, n * HT:(n + 1) * HT], banks[2 + n % 2][:, 0:HT], ACT.Sigmoid,
                               bias=vec[:, V_BG:V_BG + 1]).then_inc(t_gd, 1)
            for g in range(G):
                eng.wait_ge(t_c, g + 1)
                if g >= 2:
                    eng.wait_ge(t_v, g - 1)
                zg = Zc[:, :, C2 * g:C2 * g + C2]
                eng.activation(Zq[:, g % 2].rearrange("p (j c) -> p j c", c=C2), zg, ACT.Square).then_inc(t_q, 1)
                eng.wait_ge(t_v, g + 1)
                eng.activation(zst[:, g, 2, :], zst[:, g, 1, :], ACT.Ln, bias=epsc[:, 0:1], scale=1.0 / C2).then_inc(t_r1, 1)
                eng.wait_ge(t_r1, g + 1)
                eng.activation(zst[:, g, 3, :], zst[:, g, 2, :], ACT.Exp, scale=-0.5).then_inc(t_r2, 1)
            for n in range(4):
                eng.wait_ge(t_t, n + 1)
                m = min(4, 14 - 4 * n) * P
                eng.activation(ZT[:, 512 * n:512 * n + m], banks[4 + n % 2][:, 0:m], ACT.Copy).then_inc(t_te, 1)
            for n in range(8):
                q, par = n % 4, n // 4
                w = min(4, 14 - 4 * q)
                eng.wait_ge(t_o, n + 1)
                Yv = Y[:, :, :].rearrange("p b (i j e) -> p e b i j", i=H, e=2)[:, par]
                for jj in range(w):
                    ins = eng.activation(Yv[:, :, :, 4 * q + jj],
                                         banks[6 + n % 2][:, P * jj:P * jj + P].rearrange("p (b i) -> p b i", b=J)[:, :, 0:H],
                                         ACT.Identity, bias=vec[:, V_BZF:V_BZF + 1])
                ins.then_inc(t_y, 1)

            gn(3)

            def act_step(t, par):
                eng.wait_ge(r_z, t + 1)
                zb = banks[par]
                if not isinstance(t, int) or t >= 2:
                    eng.wait_ge(r_h, t - 1)
                eng.activation(gates[:, par].rearrange("p k n -> p (k n)"), zb[:, 0:448], ACT.Tanh).then_inc(r_g, 1)
                eng.wait_ge(r_c, t + 1)
                eng.activation(tcn[:, :], cst[:, 1 - par, :], ACT.Tanh, scale=0.5).then_inc(r_th, 1)

            act_step(0, 0)
            act_step(1, 1)
            with eng.Fori(1, H // 2) as it:
                act_step(it * 2, 0)
                act_step(it * 2 + 1, 1)

        @block.tensor
        def _(eng):
            eng.wait_ge(s_mk, 12)
            for n in range(J * SP):
                j, s = divmod(n, SP)
                if s == 0:
                    eng.wait_ge(s_xs[j], 1)
                q = n // 4
                ins = eng.transpose(banks[q][:, LP * (n % 4):LP * (n % 4) + LP], XS[0:LP, j, s].rearrange("p g c -> p (g c)"), ident[0:LP, 0:LP])
                if n % 4 == 3:
                    ins.then_inc(s_tr, 1)
            eng.wait_ge(s_v, TRB)
            for g in range(G):
                rows = slice(C * g, C * g + C)
                eng.matmul(banks[7][rows, 0:C], NB[0:R, 17, :], TB[0:R, 16, :], start=True, stop=True)
                ins = eng.matmul(banks[7][rows, C:C + 1], wzn[:, :], lnb[:, :], start=True, stop=True)
            ins.then_inc(s_wd, 1)


            def pe_att(s, par):
                fixed = isinstance(s, int)
                nxt = not fixed or s + 1 < NS
                cur = not fixed or 0 <= s < NS
                prv = not fixed or 1 <= s <= NS
                prv2 = not fixed or s >= 2
                np_ = 1 - par
                if cur:
                    eng.wait_ge(q_r, s + 1)
                    eng.wait_ge(km_r, s + 1)
                    if not fixed or s >= 1:
                        eng.wait_ge(sub_r, 4 * s)
                    for w in range(NW):
                        for g in range(G):
                            ins = eng.matmul(banks[g][64 * (w % 2):64 * (w % 2) + 64, 196 * (w // 2):196 * (w // 2) + 196],
                                             Qw[C * g:C * g + C, par, w, :],
                                             Km[C * g:C * g + C, par, w].rearrange("p h k -> p (h k)"), start=True, stop=True)
                    ins.then_inc(s_r, 1)
                if nxt:
                    if fixed and s < 0:
                        eng.wait_ge(s_xn, J)
                    else:
                        eng.wait_ge(k_r, s + 1)
                    if not fixed or s >= 3:
                        eng.wait_ge(x1_r, s - 2)
                    eng.matmul(banks[4][:, 0:ST], BD[:, U_Q, :], XN[:, strip(s + 1)], start=True, stop=True)
                    eng.matmul(banks[4][:, ST:2 * ST], BD[:, U_K, :], XN[:, strip(s + 1)], start=True, stop=True).then_inc(qk_d, 1)

                def project():
                    eng.wait_ge(ao_r, s - 1)
                    if nxt:
                        eng.wait_ge(k_r, s + 2)
                    elif s > NS:
                        eng.wait_ge(x1_r, NS - 1)
                    eng.matmul(banks[4][:, 0:ST], BD[:, U_P, :], AO[:, par, :], start=True, stop=True).then_inc(pj_r, 1)

                last = fixed and s == NS
                base = 6 * (s - 1) + 4 - (2 if last else 0)

                def transposes(g):
                    eng.wait_ge(pn_r, 4 * (s - 1) + g + 1)
                    if g == 0:
                        eng.wait_ge(ring_r, base if last else base - 2)
                    elif g == 1:
                        eng.wait_ge(ring_r, base)
                    else:
                        eng.wait_ge(ring_r, base + g - 1)
                    bk = banks[5 + (par + 1 + g) % 2]
                    for k in range(4):
                        pg = Pr[:, np_, g, 2 * k:2 * k + 2, :].rearrange("p h k -> p (h k)")
                        ins = eng.transpose(bk[:, P * k:P * k + P], pg, ident[:, :])
                    ins.then_inc(t_r, 1)

                def av(g):
                    eng.wait_ge(ring_r, base + g + 1)
                    if g == 0 and (not fixed or s >= 2):
                        eng.wait_ge(ao_r, s - 1)
                    for w in range(NW):
                        for e in range(2):
                            ins = eng.matmul(banks[7][C * g:C * g + C, WT * w:WT * w + WT], Vst[:, np_, w, g, e, :],
                                             PT[:, g % 2, w // 2, e, 64 * (w % 2):64 * (w % 2) + WT],
                                             start=(e == 0), stop=(e == 1))
                    ins.then_inc(av_r, 1)

                if prv:
                    transposes(0)
                    transposes(1)
                if prv2:
                    project()
                if prv:
                    av(0)
                    transposes(2)
                    av(1)
                    transposes(3)
                    av(2)
                if nxt:
                    eng.wait_ge(xw_r, s + 2)
                    if prv:
                        eng.wait_ge(ring_r, base + 3)
                    for w in range(NW):
                        ins = eng.matmul(banks[5 + (par + 1) % 2][:, P * w:P * w + P], xw[:, np_, w].rearrange("p u k -> p (u k)"),
                                         BD[:, U_V, :], start=True, stop=True)
                    ins.then_inc(v_r, 1)
                if prv:
                    av(3)

            for s in (-1, 0, 1, 2):
                pe_att(s, s % 2)
            with eng.Fori(0, 6) as it:
                pe_att(it * 2 + 3, 1)
                pe_att(it * 2 + 4, 0)
            for s in (15, 16, 17):
                pe_att(s, s % 2)

            def pe_ssm(i):
                fixed = isinstance(i, int)
                first = fixed and i == 0
                nd, na = len(D_ORDER), len(A_ORDER)

                def claim(k):
                    name = USES[k - 4]
                    back = 1 if k < 4 else 0
                    if first and back:
                        return
                    if name in D_ORDER:
                        eng.wait_ge(drel, nd * (i - back) + D_ORDER.index(name) + 1)
                    if name in A_ORDER:
                        eng.wait_ge(arel, na * (i - back) + A_ORDER.index(name) + 1)

                def product(k, terms):
                    claim(k)
                    for h in range(2):
                        for n, (w, rhs) in enumerate(terms):
                            ins = eng.matmul(used(k)[h][:, 0:HT], w, rhs(h), start=(n == 0), stop=(n == len(terms) - 1))
                    ins.then_inc(pe_u, 1)

                def image(h, dy, dx):
                    off = (14 * h + dy) * 30 + dx
                    v = XN[:, bass.ds(i * 900, 900)].rearrange("p (y x) -> p y x", x=30)
                    return v[:, 14 * h + dy:14 * h + dy + 14, dx:dx + W]

                def half(buf, h, shift=0):
                    return col_of(buf, i)[:, HT * h + shift:HT * h + shift + HT]

                eng.wait_ge(s_xn, J + i + 1)
                product(0, [(BD[:, U_CV + k, :], lambda h, k=k: image(h, k // 3, k % 3)) for k in range(9)])
                product(1, [(BD[:, U_X2, :], lambda h: image(h, 1, 1))])
                eng.wait_ge(arel, na * i + 1)
                product(2, [(BD[:, U_U + k, :], lambda h, k=k: half(S1, h, k)) for k in range(3)])
                product(3, [(BD[:, U_Z, :], lambda h: half(S1, h, 2))])
                eng.wait_ge(arel, na * i + 3)
                product(4, [(BD[:, U_DL, :], lambda h: half(US, h))])
                for n in range(DS):
                    product(5 + 2 * n, [(BC[:, n, :], lambda h: half(US, h))])
                    product(6 + 2 * n, [(BC[:, DS + n, :], lambda h: half(US, h))])
                eng.wait_ge(y2_r, i + 1)
                product(21, [(BD[:, U_OUT, :], lambda h: y2[:, HT * h:HT * h + HT])])
                eng.wait_ge(arel, na * i + 6)
                product(22, [(VB[:, :], lambda h: sq[:, 0, HT * h:HT * h + HT])])
                eng.wait_ge(xf_r, i + 1)
                product(23, [(BD[:, U_WO, :], lambda h: nt[:, 2, HT * h:HT * h + HT])])

            eng.wait_ge(s1z, 1)
            pe_ssm(0)
            with eng.Fori(1, J) as i:
                pe_ssm(i)

            eng.wait_ge(s_xn, 3 * J)
            for n in range(14):
                side, q = n // 7, n % 7
                if n >= 2:
                    eng.wait_ge(t_pp, n - 1)
                if n == 7:
                    eng.wait_ge(t_xr, 1)
                bk = banks[n % 2]
                eng.matmul(bk[:, :], ones[0:1, 0:P], (rowA, rowB)[side][0:1].rearrange("p a c -> p (a c)"), start=True, stop=False)
                for r in range(4):
                    i = 4 * q + r
                    ins = eng.matmul(bk[:, P * r:P * r + P], XR[:, side, i].rearrange("p b k -> p (b k)"), BD[:, U_A + side, :], start=False, stop=(r == 3))
                ins.then_inc(t_pr, 1)
            for n in range(8):
                if n >= 2:
                    eng.wait_ge(t_gd, n - 1)
                eng.matmul(banks[2 + n % 2][:, 0:HT].rearrange("p (y x) -> p y x", x=W), BD[:, U_G, :],
                           XR[:, 0, 14 * (n % 2):14 * (n % 2) + 14, n // 2, 0:W], start=True, stop=True).then_inc(t_g, 1)
            eng.wait_ge(t_sg, 14)
            for g in range(G):
                if g:
                    eng.wait_ge(t_zc, g)
                for c in range(C2):
                    for b in range(J):
                        m = C2 * g + c
                        ins = eng.matmul(banks[4 + b][32 * b:32 * b + H, H * c:H * c + H], Ab[32 * b:32 * b + H, 0, m, :],
                                         Ab[32 * b:32 * b + H, 1, m, :], start=True, stop=True)
                ins.then_inc(t_z, 1)
            for q in range(14):
                if q == 0:
                    eng.wait_ge(t_n, G)
                if q % 4 == 0 and q >= 8:
                    eng.wait_ge(t_te, q // 4 - 1)
                ins = eng.transpose(banks[4 + (q // 4) % 2][:, P * (q % 4):P * (q % 4) + P],
                                    Zc[:, 2 * q:2 * q + 2, :].rearrange("p j m -> p (j m)"), ident[:, :])
                if q % 4 == 3 or q == 13:
                    ins.then_inc(t_t, 1)
            for n in range(8):
                q, par = n % 4, n // 4
                m = min(4, 14 - 4 * q) * P
                eng.wait_ge(t_te, q + 1)
                if n >= 2:
                    eng.wait_ge(t_y, n - 1)
                eng.matmul(banks[6 + n % 2][:, 0:m], WZ[64 * par:64 * par + 64, :], ZT[64 * par:64 * par + 64, 512 * q:512 * q + m],
                           start=True, stop=True).then_inc(t_o, 1)

            eng.wait_ge(t_x3, 1)
            for n in range(28):
                q = n // 4
                if n % 4 == 0 and q >= 2:
                    eng.wait_ge(r_te, q - 1)
                ins = eng.transpose(banks[2 + q % 2][0:112, P * (n % 4):P * (n % 4) + P], X[:, 112 * n:112 * n + 112], ident[:, :])
                if n % 4 == 3:
                    ins.then_inc(r_t, 1)

            def inputs(t, par):
                zb = banks[par]
                if not isinstance(t, int) or t >= 2:
                    eng.wait_ge(r_g, t - 1)
                eng.matmul(zb[:, 0:448].rearrange("p (k n) -> p k n", k=4), BL[:, :, :].rearrange("k g c -> k (g c)"),
                           bcast(ident[0:4, 0:4], 2, 112), start=True, stop=False, skip_group_check=True)
                for k in range(4):
                    xt = XN[:, 0:N].rearrange("p (b t) -> p b t", b=J)[:, :, bass.ds(t * W, W)]
                    eng.matmul(zb[:, 112 * k:112 * k + 112].rearrange("p (b n) -> p b n", b=J), BD[:, U_X + k, :], xt, start=False, stop=False, skip_group_check=True)

            def recur(t, par, after=True):
                zb = banks[par]
                if not isinstance(t, int) or t >= 1:
                    eng.wait_ge(r_h, t)
                else:
                    eng.wait_ge(r_in, 1)
                for k in range(4):
                    ins = eng.matmul(zb[:, 112 * k:112 * k + 112], BD[:, U_M + k, :], hst[:, 1 - par, :], start=False, stop=True,
                                     skip_group_check=True)
                ins.then_inc(r_z, 1)

            def turn(t, par):
                eng.wait_ge(r_h, t + 1)
                if not isinstance(t, int) or t >= 2:
                    eng.wait_ge(r_o, t - 1)
                eng.transpose(banks[4 + par][0:112, 0:P], hst[:, par, :], ident[:, :]).then_inc(r_t, 1)

            eng.wait_ge(s_xn, 4 * J)
            inputs(0, 0)
            recur(0, 0)
            inputs(1, 1)
            recur(1, 1)
            turn(0, 0)
            inputs(2, 0)
            recur(2, 0)
            turn(1, 1)
            inputs(3, 1)
            with eng.Fori(1, H // 2 - 1) as it:
                recur(it * 2 + 1, 1)
                turn(it * 2, 0)
                inputs(it * 2 + 2, 0)
                recur(it * 2 + 2, 0)
                turn(it * 2 + 1, 1)
                inputs(it * 2 + 3, 1)
            recur(H - 1, 1)
            turn(H - 2, 0)
            turn(H - 1, 1)

        @block.vector
        def _(eng):
            chain = [0]

            def link(ins):
                chain[0] += 1
                ins.then_inc(s_v, 1)
                eng.wait_ge(s_v, chain[0])

            eng.memset(epsc[:, :], EPS).then_inc(s_ev, 1)
            for j in range(0, J, 2):
                eng.wait_ge(s_x[j], 16)
                eng.tensor_copy(XS[0:LP, j].rearrange("p s g c -> p g s c"), XT[0:LP, j]).then_inc(s_xs[j], 1)
            for q in range(0, 7, 2):
                eng.wait_ge(s_tr, q + 1)
                evac_in(eng, q)

            def gn_stats(layer):
                if layer:
                    eng.wait_ge(s_xn, J * layer)
                for j in range(J):
                    for h in range(2):
                        ins = eng.bn_stats(stats[:, j, h, :], X[:, T * j + HT * h:T * j + HT * h + HT])
                link(ins)
                for j in range(J):
                    ins = eng.bn_aggr(mv[:, j, :], stats[:, j].rearrange("p h s -> p (h s)"))
                ins.then_inc(s_mv, 1)
                eng.wait_ge(s_mv, layer + 1)

            def gn_apply(layer, dst):
                eng.wait_ge(s_rs, layer + 1)
                for j in range(J):
                    src = X[:, T * j:T * j + T]
                    d = dst(j)
                    if len(d.shape) == 3:
                        src = src.rearrange("p (y x) -> p y x", y=H)
                    eng.tensor_scalar(d, src, mv[:, j, 0:1], rstd[:, j:j + 1], ALU.subtract, ALU.mult).then_inc(s_xn, 1)

            eng.wait_ge(s_ev, 8)
            gn_stats(0)

            eng.wait_ge(s_mk, 12)
            all_loads(eng)
            eng.wait_ge(s_hf, 2)
            eng.tensor_reduce(mask8[:, :], m16[:, :].rearrange("p (g h) -> p h g", g=G), AX.X, ALU.add)
            link(eng.tensor_tensor(maskz[:, :], m8[:, 0:4], m8[:, 4:8], ALU.add))
            for k, dst in ((0, W8X[:, :]), (1, NB[:, 1, :]), (2, NB[:, 2, :])):
                ins = eng.tensor_tensor(dst.rearrange("p (h i) -> p h i", h=4), bcast(W8[:, k, :], 1, 4), bcast(mask8[:, :], 2, 8), ALU.mult)
            link(ins)
            for k in range(3):
                eng.tensor_scalar(NB[:, 4 + k, :], WIN[:, 0, :], C1[:, k:k + 1], None, ALU.mult)
            for k in range(9):
                ins = eng.tensor_scalar(NB[:, 7 + k, :], W8X[:, :], DW[:, k:k + 1], None, ALU.mult)
            link(ins)
            link(eng.transpose(TB[:, :, :].rearrange("p u c -> p (u c)"), NB[:, :, :].rearrange("p u c -> p (u c)")))
            assert chain[0] == TRB
            link(eng.tensor_reduce(omean[:, :], TB[:, 3, :], AX.X, ALU.add))
            link(eng.tensor_scalar(omean[:, :], omean[:, :], 1.0 / C, None, ALU.mult))
            link(eng.tensor_scalar(TB[:, 3, :], TB[:, 3, :], omean[:, 0:1], None, ALU.subtract))
            eng.tensor_copy(W4[:, U_Z:U_DL, :], TB[:, 0:16, :])
            eng.tensor_scalar(W4[:, U_X:U_X + 3, :], W4[:, U_X:U_X + 3, :], 0.5, None, ALU.mult)
            eng.tensor_scalar(W4[:, U_M:U_M + 3, :], W4[:, U_M:U_M + 3, :], 0.25, None, ALU.mult)
            eng.tensor_scalar(W4[:, U_M + 3, :], W4[:, U_M + 3, :], 0.5, None, ALU.mult)
            eng.tensor_scalar(BL[:, :, :], BL[:, :, :], half3[:, 0:1], None, ALU.mult)
            eng.wait_ge(s_wd, 1)
            eng.tensor_copy(W4[:, U_DL, :], banks[7][:, 0:C])
            eng.tensor_scalar(vec[:, V_BQS:V_BQS + 1], vec[:, V_BQ:V_BQ + 1], SCALE, None, ALU.mult)
            link(eng.tensor_tensor(vec[:, V_BZF:V_BZF + 1], vec[:, V_BZ:V_BZ + 1], banks[7][:, C:C + 1], ALU.add))
            eng.tensor_tensor(BD[:, :, :].rearrange("p u (g c) -> p u g c", g=G), bcast(W4[:, :, :], 2, G),
                              bcast(bcast(bd[:, :], 1, NU), 3, C), ALU.mult)
            eng.tensor_tensor(BC[:, :, :].rearrange("p n (g c) -> p n g c", g=G), bcast(bcast(TB[:, 17, R:R + 2 * DS], 2, G), 3, C),
                              bcast(bcast(bd[:, :], 1, 2 * DS), 3, C), ALU.mult)
            eng.tensor_scalar(VB[:, :].rearrange("p (g c) -> p g c", g=G), bcast(bd[:, :], 2, C), 1.0 / C, None, ALU.mult)
            link(eng.tensor_scalar(wzs[:, :], wzraw[:, :], vec[:, V_LG:V_LG + 1], None, ALU.mult))
            eng.tensor_tensor(WZ[:, :].rearrange("p (g c) -> p g c", g=G), bcast(wzs[:, :], 1, G), bcast(maskz[:, :], 2, C), ALU.mult)
            eng.tensor_copy(rowA[:, :, :], bcast(smallr[0:1, 0, :], 1, 16))
            eng.tensor_copy(rowB[:, :, :], bcast(smallr[0:1, 1, :], 1, 16))
            eng.wait_ge(s_ae, 1)
            link(eng.tensor_scalar(Aneg[:, :], AE[:, :], -1.0, None, ALU.mult))
            gn_apply(0, lambda j: XN[:, T * j:T * j + T])

            eng.wait_ge(s_mk2, 4)

            def dve_att(s, par):
                fixed = isinstance(s, int)
                cur = not fixed or 0 <= s < NS
                prv = not fixed or 1 <= s <= NS
                prv2 = not fixed or s >= 2
                np_ = 1 - par
                if cur:
                    eng.wait_ge(s_r, s + 1)
                    for g in range(G):
                        eng.tensor_reduce(mx[:, g, :], banks[g][:, 0:392].rearrange("p (m k) -> p m k", k=WT), AX.X,
                                          ALU.max).then_inc(max_r, 1)
                    for g in range(G):
                        eng.wait_ge(max_r, 4 * s + g + 1)
                        if not fixed or s >= 1:
                            eng.wait_ge(exp_r, 4 * (s - 1) + g + 1)
                        eng.tensor_tensor(Ts[:, g, :, :], banks[g][:, 0:392].rearrange("p (m k) -> p m k", k=WT),
                                          bcast(mx[:, g, :], 2, WT), ALU.subtract).then_inc(sub_r, 1)
                if prv2:
                    eng.wait_ge(pj_r, s - 1)
                    xs = X[:, strip(s - 2)]
                    eng.scalar_tensor_tensor(xs, banks[4][:, 0:ST], vec[:, V_BP:V_BP + 1], xs, ALU.add, ALU.add).then_inc(x1_r, 1)
                if cur:
                    for g in range(G):
                        eng.wait_ge(exp_r, 4 * s + g + 1)
                        if not fixed or s >= 1:
                            eng.wait_ge(pn_r, 4 * (s - 1) + g + 1)
                        eng.tensor_reduce(sm[:, g, :], Pr[:, par, g, :, 0:WT], AX.X, ALU.add).then_inc(sum_r, 1)
                    for g in range(G):
                        eng.wait_ge(sum_r, 4 * s + g + 1)
                        eng.reciprocal(rc[:, g, :], sm[:, g, :]).then_inc(rec_r, 1)
                if prv:
                    eng.wait_ge(av_r, 4 * s)
                    eng.tensor_scalar(windows(AO[:, np_, :]), banks[7][:, 0:ST].rearrange("p (w r c) -> p w r c", w=NW, r=WS),
                                      vec[:, V_BV:V_BV + 1], None, ALU.add).then_inc(ao_r, 1)

            for s in (0, 1, 2):
                dve_att(s, s % 2)
            with eng.Fori(0, 6) as it:
                dve_att(it * 2 + 3, 1)
                dve_att(it * 2 + 4, 0)
            for s in (15, 16, 17):
                dve_att(s, s % 2)

            eng.wait_ge(x1_r, NS)
            eng.memset(XN[:, :], 0.0).then_inc(s_v, 1)
            chain[0] += 1
            gn_stats(1)
            eng.wait_ge(s_v, chain[0])
            img = XN[:, :].rearrange("p (b y x) -> p b y x", b=J, y=30)
            gn_apply(1, lambda j: img[:, j, 1:29, 1:29])

            def dve_ssm(i):
                fixed = isinstance(i, int)
                first = fixed and i == 0
                U = len(USES)
                nd = len(D_ORDER)

                def ready(k):
                    eng.wait_ge(pe_u, U * i + k + 1)
                ready(4)
                eng.wait_ge(arel, len(A_ORDER) * i + 5)
                if not first:
                    eng.wait_ge(dl_r, i)
                eng.tensor_scalar(halves(mxd[:, :]), two_banks(4), vec[:, V_DTB:V_DTB + 1], 0.0, ALU.add, ALU.max).then_inc(drel, 1)
                eng.wait_ge(sp1, i + 1)
                eng.tensor_scalar(sp[:, 2, :], sp[:, 1, :], 1.0, None, ALU.add).then_inc(sp2, 1)
                eng.wait_ge(sp2, i + 1)
                eng.scalar_tensor_tensor(sp[:, 5, :], sp[:, 2, :], 1.0, sp[:, 1, :], ALU.subtract, ALU.subtract).then_inc(sp5, 1)
                eng.wait_ge(drel, nd * i + 1)
                eng.wait_ge(sp3, i + 1)
                eng.tensor_tensor(mxd[:, :], mxd[:, :], sp[:, 3, :], ALU.add).then_inc(sp6, 1)
                eng.wait_ge(sp4, i + 1)
                eng.wait_ge(sp5, i + 1)
                eng.tensor_tensor(sp[:, 6, :], sp[:, 5, :], sp[:, 4, :], ALU.mult).then_inc(sp7, 1)
                eng.wait_ge(sp6, i + 1)
                eng.wait_ge(sp7, i + 1)
                if not first:
                    eng.wait_ge(da_r, DS * i)
                eng.tensor_tensor(DL[:, :], mxd[:, :], sp[:, 6, :], ALU.subtract).then_inc(dl_r, 1)
                eng.wait_ge(dl_r, i + 1)
                eng.tensor_tensor(DU[:, :], DL[:, :], col_of(US, i), ALU.mult).then_inc(du_r, 1)
                eng.wait_ge(du_r, i + 1)

                def times_b(n):
                    ready(5 + 2 * n)
                    if n >= 2 or not first:
                        eng.wait_ge(sc_r, DS * i + n - 1)
                    eng.tensor_tensor(halves(dBu[:, n % 2, :]), halves(DU[:, :]), two_banks(5 + 2 * n), ALU.mult).then_inc(drel, 1)

                def scan(n):
                    eng.wait_ge(drel, nd * i + D_ORDER.index(f"B{n}") + 1)
                    eng.wait_ge(da_r, DS * i + n + 1)
                    if n >= 2:
                        eng.wait_ge(drel, nd * i + D_ORDER.index(f"C{n - 2}") + 1)
                    eng.tensor_tensor_scan(Hs[:, n % 2, :], dA[:, n % 2, :], dBu[:, n % 2, :], 0.0, ALU.mult, ALU.add).then_inc(sc_r, 1)

                def times_c(n):
                    ready(6 + 2 * n)
                    eng.wait_ge(sc_r, DS * i + n + 1)
                    dst = YA[:, :] if n == 0 else hC[:, n % 2, :]
                    if n >= 3:
                        eng.wait_ge(ya_r, (DS - 1) * i + n - 2)
                    ins = eng.tensor_tensor(halves(dst), halves(Hs[:, n % 2, :]), two_banks(6 + 2 * n), ALU.mult)
                    ins.then_inc(drel, 1)

                times_b(0)
                scan(0)
                for n in range(1, DS):
                    times_b(n)
                    times_c(n - 1)
                    scan(n)
                times_c(DS - 1)
                eng.wait_ge(ya_r, (DS - 1) * (i + 1))
                eng.scalar_tensor_tensor(y1[:, :], col_of(US, i), vec[:, V_D:V_D + 1], YA[:, :], ALU.mult, ALU.add).then_inc(y1_r, 1)
                eng.wait_ge(y1_r, i + 1)
                eng.tensor_tensor(y2[:, :], y1[:, :], col_of(ZS, i), ALU.mult).then_inc(y2_r, 1)
                ready(21)
                eng.wait_ge(rs_r, i + 1)
                eng.tensor_tensor(halves(nt[:, 0, :]), halves(sq[:, 2, :]), two_banks(21), ALU.mult).then_inc(drel, 1)
                eng.wait_ge(drel, nd * i + D_ORDER.index("out") + 1)
                eng.tensor_scalar(nt[:, 1, :], nt[:, 0, :], vec[:, V_GA:V_GA + 1], vec[:, V_BE:V_BE + 1], ALU.mult, ALU.add).then_inc(nt1, 1)
                eng.wait_ge(nt1, i + 1)
                eng.tensor_tensor(nt[:, 2, :], nt[:, 1, :], col_of(X2, i), ALU.mult).then_inc(xf_r, 1)
                ready(23)
                xs = X[:, bass.ds(i * T, T)]
                eng.tensor_tensor(halves(xs), halves(xs), two_banks(23), ALU.add).then_inc(drel, 1)

            dve_ssm(0)
            with eng.Fori(1, J) as i:
                dve_ssm(i)

            eng.wait_ge(drel, len(D_ORDER) * J)
            gn_stats(2)
            eng.wait_ge(t_zz, 2)
            gn_apply(2, lambda j: XR[:, 0, :, j, 0:W])
            eng.wait_ge(s_xn, 3 * J)
            for j in range(J):
                ins = eng.tensor_copy(XR[:, 1, :, j, 0:H].rearrange("p c k -> p k c"), XR[:, 0, :, j, 0:W])
            ins.then_inc(t_xr, 1)
            for n in range(14):
                eng.wait_ge(t_p1, n + 1)
                if n >= 2:
                    eng.wait_ge(t_sg, n - 1)
                bk = banks[n % 2][:, :].rearrange("p (m t c) -> p m t c", m=16, t=2)
                eng.tensor_tensor(pp[:, n % 2].rearrange("p (m c) -> p m c", m=16), p1[:, n % 2].rearrange("p (m c) -> p m c", m=16),
                                  bk[:, :, 1, :], ALU.mult).then_inc(t_pp, 1)
            for g in range(G):
                eng.wait_ge(t_z, g + 1)
                for b in range(J):
                    ins = eng.tensor_copy(Zc[32 * b:32 * b + H, :, C2 * g:C2 * g + C2].rearrange("p j c -> p c j"),
                                          banks[4 + b][32 * b:32 * b + H, 0:448].rearrange("p (c j) -> p c j", c=C2))
                ins.then_inc(t_zc, 1)
                eng.wait_ge(t_zc, g + 1)
                zg = Zc[:, :, C2 * g:C2 * g + C2]
                link(eng.tensor_reduce(zst[:, g, 0, :], zg, AX.X, ALU.add))
                link(eng.tensor_scalar(zst[:, g, 0, :], zst[:, g, 0, :], 1.0 / C2, None, ALU.mult))
                eng.tensor_tensor(zg, zg, bcast(zst[:, g, 0, :], 2, C2), ALU.subtract).then_inc(t_c, 1)
                eng.wait_ge(t_q, g + 1)
                eng.tensor_reduce(zst[:, g, 1, :], Zq[:, g % 2].rearrange("p (j c) -> p j c", c=C2), AX.X, ALU.add).then_inc(t_v, 1)
                eng.wait_ge(t_r2, g + 1)
                eng.wait_ge(t_c, g + 1)
                eng.tensor_tensor(zg, zg, bcast(zst[:, g, 3, :], 2, C2), ALU.mult).then_inc(t_n, 1)
            eng.wait_ge(t_gd, 8)
            eng.wait_ge(t_y, 8)
            link(eng.tensor_tensor(flat(Y), flat(Y), flat(Gt), ALU.mult))
            eng.tensor_tensor(X[:, :], X[:, :], flat(Y), ALU.add).then_inc(t_x3, 1)
            eng.wait_ge(t_x3, 1)

            gn_stats(3)
            gn_apply(3, lambda j: XN[:, T * j:T * j + T])
            eng.memset(hst[:, :, :], 0.0)
            eng.memset(cst[:, :, :], 0.0).then_inc(r_in, 1)
            eng.wait_ge(r_in, 1)
            Rv = Rt[:, :, :].rearrange("p (g m) c -> p m g c", g=G)
            for q in range(7):
                eng.wait_ge(r_t, q + 1)
                eng.tensor_copy(Rv[:, 4 * q:4 * q + 4], banks[2 + q % 2][0:112, :].rearrange("p (m g c) -> p m g c", m=4, g=G)).then_inc(r_te, 1)
            eng.wait_ge(r_te, 7)

            def dve_step(t, par, m):
                g = gates[:, par]
                eng.wait_ge(r_g, t + 1)
                eng.scalar_tensor_tensor(t1[:, :], g[:, 1, :], 1.0, cst[:, par, :], ALU.add, ALU.mult).then_inc(r_1, 1)
                eng.scalar_tensor_tensor(t2[:, :], g[:, 0, :], 1.0, g[:, 3, :], ALU.add, ALU.mult).then_inc(r_1, 1)
                eng.wait_ge(r_1, 2 * t + 2)
                eng.scalar_tensor_tensor(cst[:, 1 - par, :], t1[:, :], 0.5, t2[:, :], ALU.mult, ALU.add).then_inc(r_c, 1)
                eng.wait_ge(r_th, t + 1)
                eng.scalar_tensor_tensor(hst[:, par, :], g[:, 2, :], 1.0, tcn[:, :], ALU.add, ALU.mult).then_inc(r_h, 1)
                eng.wait_ge(r_t, 7 + t + 1)
                if not isinstance(t, int) or t >= 2:
                    eng.wait_ge(s_out[par], m * 16)
                eng.scalar_tensor_tensor(Os[:, par].rearrange("p g c -> p (g c)"), banks[4 + par][0:112, 0:P], 0.5,
                                         Rt[:, bass.ds(t * 4, 4), :].rearrange("p g c -> p (g c)"), ALU.mult, ALU.add).then_inc(r_o, 1)

            dve_step(0, 0, 0)
            dve_step(1, 1, 0)
            with eng.Fori(1, H // 2) as it:
                dve_step(it * 2, 0, it)
                dve_step(it * 2 + 1, 1, it)


_INS = ['x', 'L0_conv_w_qkv', 'L0_conv_b_qkv', 'L0_conv_w_proj', 'L0_conv_b_proj', 'L1_conv_w1', 'L1_conv_dw',
        'L1_conv_in_proj_w', 'L1_conv_conv1d_w', 'L1_conv_conv1d_b', 'L1_conv_x_proj_w', 'L1_conv_dt_proj_w',
        'L1_conv_dt_proj_b', 'L1_conv_A_log', 'L1_conv_D_param', 'L1_conv_out_proj_w', 'L1_conv_gamma', 'L1_conv_beta',
        'L1_conv_w2', 'L1_conv_wout', 'L2_conv_Wa1', 'L2_conv_ba1', 'L2_conv_Wa2', 'L2_conv_ba2', 'L2_conv_Wb1',
        'L2_conv_bb1', 'L2_conv_Wb2', 'L2_conv_bb2', 'L2_conv_ln2_g', 'L2_conv_ln2_b', 'L2_conv_Wg', 'L2_conv_bg',
        'L2_conv_Wz', 'L2_conv_bz', 'L3_conv_Wix', 'L3_conv_Wim', 'L3_conv_Wfx', 'L3_conv_Wfm', 'L3_conv_Wcx',
        'L3_conv_Wcm', 'L3_conv_Wox', 'L3_conv_Wom', 'L3_conv_bi', 'L3_conv_bf', 'L3_conv_bc', 'L3_conv_bo']


def kernel(**inputs):
    import concourse.bacc as _bacc
    from concourse.bass_utils import run_bass_kernel_spmd as _run

    nc = _bacc.Bacc("TRN2", target_bir_lowering=False, num_devices=1)
    arrays, aps = {}, {}
    for name in _INS:
        v = np.ascontiguousarray(inputs[name])
        arrays[f"in_{name}"] = v
        aps[name] = nc.dram_tensor(f"in_{name}", v.shape, mybir.dt.from_np(v.dtype), kind="ExternalInput").ap()
    out = nc.dram_tensor("out", (B, H, W, C), F32, kind="ExternalOutput").ap()
    build(nc, aps, out)
    r = _run(nc, [arrays], core_ids=[0])
    return r.results[0]["out"]
```

```python
import numpy as np

import concourse.bass as bass
from concourse import mybir
from contextlib import ExitStack

F32 = mybir.dt.float32
BF16 = mybir.dt.bfloat16
ALU = mybir.AluOpType
ACT = mybir.ActivationFunctionType
AX = mybir.AxisListType

P = 128
B, H, W, C = 16, 28, 28, 32
G = P // C
J = B // G
T = H * W
N = J * T
SP = 7
LP = T // SP
WS = 7
WT = WS * WS
WP = 64
NH, HD = 4, 8
NW = W // WS
ST = WS * W
NS = N // ST
R, DS = 8, 8
C2 = 16
HT = T // 2
EPS = 1e-5
SCALE = HD ** -0.5

(U_Q, U_K, U_V, U_P, U_A, U_B, U_G, U_X, U_M) = (0, 1, 2, 3, 4, 5, 6, 7, 11)
(U_Z, U_X2, U_WO, U_OUT, U_U, U_CV, U_DL, NU) = (15, 16, 17, 18, 19, 22, 31, 32)


def build(nc, a, out):
    ctx = ExitStack()
    with ctx:
        def sb(name, shape, stack=ctx, dtype=F32):
            return stack.enter_context(nc.sbuf_tensor(name, shape, dtype))

        def sem(name):
            return ctx.enter_context(nc.semaphore(name))

        X = sb("X", [P, N])
        XN = sb("XN", [P, J * 30 * 30])
        BD = sb("BD", [P, NU, P])
        WBC = sb("WBC", [P, 2, 3 * C])
        sel = sb("sel", [3 * C, DS, P], ctx, BF16)
        ident = sb("ident", [P, P])
        bd = sb("bd", [P, G])
        m16 = sb("m16", [P, 16])
        mask8 = sb("mask8", [P, NH])
        m8 = sb("m8", [P, 8])
        maskz = sb("maskz", [P, G])
        WZ = sb("WZ", [P, P])
        VB = sb("VB", [P, P])
        BL = sb("BL", [4, G, C])
        half3 = sb("half3", [4, 1])
        BAB = sb("BAB", [P, 2, C])
        epsc = sb("epsc", [P, 1])
        vec = sb("vec", [P, 16])
        (V_BQ, V_BK, V_BV, V_BP, V_CB, V_DTB, V_D, V_GA, V_BE, V_BG, V_BZ, V_LG, V_BQS, V_BZF) = range(14)
        lnb = sb("lnb", [C2, 1])
        Aneg = sb("Aneg", [P, DS])
        W4 = sb("W4", [P, NU, C])
        wzraw = sb("wzraw", [P, C])
        wzs = sb("wzs", [P, C])
        stats = sb("stats", [P, J, 2, 6])
        mv = sb("mv", [P, J, 2])
        lnv = sb("lnv", [P, J])
        rstd = sb("rstd", [P, J])

        pairs = [ctx.enter_context(nc.psum_tensor(f"pair{i}", [P, 2, 512], F32)) for i in range(4)]
        banks = [pairs[i // 2][:, i % 2, :] for i in range(8)]
        TRB = 5

        setup = ExitStack()
        NB = sb("NB", [P, 18, C], setup)
        TB = sb("TB", [P, 18, C], setup)
        W8 = sb("W8", [P, 3, 8], setup)
        W8X = sb("W8X", [P, C], setup)
        DW = sb("DW", [P, 9], setup)
        C1 = sb("C1", [P, 3], setup)
        AL = sb("AL", [P, DS], setup)
        AE = sb("AE", [P, DS], setup)
        WIN = sb("WIN", [P, 1, C], setup)
        wzn = sb("wzn", [C2, C], setup)
        omean = sb("omean", [P, 1], setup)
        raw = ExitStack()
        XT = sb("XT", [P, J, G, SP, C], raw)
        XS = sb("XS", [P, J, SP, G, C], raw)
        raw.close()

        att = ExitStack()
        xw = sb("xw", [P, 2, NW, 2, WP], att)
        Qw = sb("Qw", [P, 2, NW, WP], att)
        Ks = sb("Ks", [P, 2, NW, WT], att)
        Km = sb("Km", [P, 2, NW, NH, WT], att)
        Vst = sb("Vst", [P, 2, NW, G, 2, C], att)
        Ts = sb("Ts", [P, G, 8, WT], att)
        Pr = sb("Pr", [P, 2, G, 8, WP], att)
        PT = sb("PT", [P, 2, 2, 2, P], att)
        AO = sb("AO", [P, 2, ST], att)
        mx = sb("mx", [P, G, 8], att)
        sm = sb("sm", [P, G, 8], att)
        rc = sb("rc", [P, G, 8], att)
        att.close()
        setup.close()

        ssm = ExitStack()
        NA = 4
        S1 = sb("S1", [P, T + 2], ssm)
        US = sb("US", [P, J, T], ssm)
        ZS = sb("ZS", [P, J, T], ssm)
        X2 = sb("X2", [P, J, T], ssm)
        DL = sb("DL", [P, 2, T], ssm)
        BCf = sb("BCf", [3 * C, 2, 2, T], ssm)
        YA = sb("YA", [P, 2, T], ssm)
        DU = sb("DU", [P, T], ssm)
        dA = sb("dA", [P, NA, T], ssm)
        dBu = sb("dBu", [P, 2, T], ssm)
        Hs = sb("Hs", [P, 2, T], ssm)
        NHC = 4
        hC = sb("hC", [P, NHC, T], ssm)
        (SP_E, SP_U, SP_L, SP_W, SP_C, SP_M) = range(6)
        sp = sb("sp", [P, 6, T], ssm)
        y1 = sb("y1", [P, T], ssm)
        y2 = sb("y2", [P, T], ssm)
        cS = sb("cS", [P, T], ssm)
        sq = sb("sq", [P, T], ssm)
        lv = sb("lv", [P, T], ssm)
        rs = sb("rs", [P, T], ssm)
        nt = sb("nt", [P, 3, T], ssm)
        ssm.close()

        tri = ExitStack()
        XR = sb("XR", [P, 2, H, J, 32], tri)
        Ab = sb("Ab", [P, 2, 64, H], tri)
        p1 = sb("p1", [P, 2, 512], tri)
        pp = sb("pp", [P, 2, 256], tri)
        Zc = sb("Zc", [P, H, 64], tri)
        Zq = sb("Zq", [P, 2, 448], tri)
        zst = sb("zst", [P, 4, G, H], tri)
        ZT = sb("ZT", [P, 14 * P], tri)
        Gt = sb("Gt", [P, J, T], tri)
        Y = sb("Y", [P, J, T], tri)
        tri.close()

        rec = ExitStack()
        Rt = sb("Rt", [112, 112, C], rec)
        gates = sb("gates", [P, 2, 4, 112], rec)
        hst = sb("hst", [P, 2, 112], rec)
        cst = sb("cst", [P, 2, 112], rec)
        t1 = sb("t1", [P, 112], rec)
        t2 = sb("t2", [P, 112], rec)
        tcn = sb("tcn", [P, 112], rec)
        Os = sb("Os", [112, 2, G, C], rec)
        rec.close()

        s_x = [sem(f"s_x{j}") for j in range(J)]
        s_xs = [sem(f"s_xs{j}") for j in range(J)]
        s_w = [sem(f"s_w{k}") for k in range(3)]
        s_wp = [sem(f"s_wp{k}") for k in range(2)]
        s_z0 = sem("s_z0")
        s_mk = sem("s_mk")
        s_mk2 = sem("s_mk2")
        s_v = sem("s_v")
        s_a = sem("s_a")
        s_tr = sem("s_tr")
        s_ev = sem("s_ev")
        s_hf = sem("s_hf")
        s_ae = sem("s_ae")
        s_wd = sem("s_wd")
        s_mv = sem("s_mv")
        s_rs = sem("s_rs")
        s_xn = sem("s_xn")

        qk_d, q_r, k_r, km_r, xw_r, v_r, s_r, sub_r, exp_r, max_r, sum_r, rec_r, pn_r, t_r, ring_r, av_r, ao_r, pj_r, x1_r, = \
            [sem("a_" + n) for n in "qk q k km xw v s sub exp max sum rec pn t ring av ao pj x1".split()]
        FRONT_TAIL = "conv x2 u z delta xB xC out var wout".split()
        p_ = {n: sem("p_" + n) for n in FRONT_TAIL + ["B", "C"]}
        c_ = {n: sem("c_" + n) for n in FRONT_TAIL}
        a_rel, a_e, a_u, a_l, a_w, a_lv, a_da, a_rs = [sem("b_" + n) for n in "rel e u l w lv da rs".split()]
        v_b, v_s, v_c, v_cc, v_dl, v_du, v_y1, v_y2, v_nt1 = [sem("v_" + n) for n in "b s c cc dl du y1 y2 nt1".split()]
        g_ya, g_ml, g_cw, g_mid, g_low, g_nt0, g_nt2, s1z = [sem("g_" + n) for n in "ya ml cw mid low nt0 nt2 s1z".split()]
        t_pr, t_p1, t_pp, t_sg, t_z, t_zc, t_za, t_c, t_q, t_v, t_r1, t_r2, t_n, t_t, t_te, t_o, t_y, t_g, t_gd, t_x3, t_zz, t_xr = \
            [sem("t_" + n) for n in "pr p1 pp sg z zc za c q v r1 r2 n t te o y g gd x3 zz xr".split()]
        r_t, r_te, r_z, r_g, r_1, r_2, r_c, r_th, r_h, r_o, r_os, r_in, r_1b = \
            [sem("r_" + n) for n in "t te z g 1 2 c th h o os in 1b".split()]
        s_out = [sem("s_out0"), sem("s_out1")]

        block = ctx.enter_context(nc.Block())

        def strip(s):
            return bass.ds(s * ST, ST)

        def windows(ap):
            return ap.rearrange("p (r w c) -> p w r c", r=WS, w=NW)

        def bcast(ap, axis, n):
            ap = ap.unsqueeze(axis)
            shape = list(ap.shape)
            shape[axis] = n
            return ap.broadcast_to(shape)

        def flat(buf):
            return buf[:, :, :].rearrange("p b t -> p (b t)")

        def col_of(buf, i):
            n = buf.shape[2]
            return flat(buf)[:, bass.ds(i * n, n)]

        def two_banks(k):
            return pairs[k % 4][:, :, 0:HT]

        def evac_in(eng, q):
            n, stop = 4 * q, 4 * q + 4
            while n < stop:
                j, s = divmod(n, SP)
                m = min(stop - n, SP - s)
                src = banks[q][:, LP * (n % 4):LP * (n % 4 + m)].rearrange("p (s t) -> p s t", s=m)
                dst = X[:, T * j:T * j + T].rearrange("p (t s) -> p s t", s=SP)[:, s:s + m]
                ins = (eng.activation(dst, src, ACT.Copy) if eng is nc.scalar else eng.tensor_copy(dst, src))
                n += m
            ins.then_inc(s_ev, 1)

        def halves(ap):
            return ap.rearrange("p (h t) -> p h t", h=2)

        PAIR = dict(B=0, C=1, conv=2, u=2, delta=2, xC=2, xB=3, wout=3, out=3, var=3, z=3, x2=3)

        def result(name):
            return pairs[PAIR[name]][:, :, 0:HT]

        def take_z(eng, g, columns):
            first = 4 - 4 * (g % 2)
            for b in columns:
                dst = Zc[32 * b:32 * b + H, :, C2 * g:C2 * g + C2].rearrange("p j c -> p c j")
                src = banks[first + b][32 * b:32 * b + H, 0:448].rearrange("p (c j) -> p c j", c=C2)
                ins = eng.activation(dst, src, ACT.Copy) if eng is nc.scalar else eng.tensor_copy(dst, src)
            return ins

        def parts(i):
            return [b if 0 <= b < J else None for b in (i + 2, i + 1, i, i - 1, i - 2)]

        def upper(ap):
            return ap.bitcast(BF16).rearrange("p (t two) -> p t two", two=2)[:, :, 1]

        SSM_STEPS = range(-2, J + 2)

        def rep(dram, off, rows, cols, stride):
            return bass.AP(dram.tensor, off, [[0, G], [stride, rows], [1, cols]])

        loads = {}

        def load(eng, dst, src, stage=1):
            s = (s_wp if eng is nc.gpsimd else s_w)[stage]
            eng.dma_start(dst, src).then_inc(s, 16)
            loads[s.name] = loads.get(s.name, 0) + 1

        def col(eng, k, name, off=0, stage=1):
            load(eng, vec[:, k:k + 1], bass.AP(a[name].tensor, off, [[0, G], [1, C], [1, 1]]), stage)

        def loaded(eng, stage):
            for s in [s_w[stage]] + s_wp[stage:stage + 1]:
                eng.wait_ge(s, 16 * loads[s.name])

        @block.sync
        def _(eng):
            xv = a["x"].rearrange("b h w c -> b (h w c)").rearrange("(g j) (p s c) -> j p g (s c)", g=G, p=LP, c=C)
            for j in range(J):
                eng.dma_start(XT[0:LP, j].rearrange("p g s c -> p g (s c)"), xv[j]).then_inc(s_x[j], 16)
            eng.wait_ge(s_z0, 1)

            load(eng, W4[:, U_Q:U_V + 1, :].rearrange("p u c -> p (u c)"), rep(a["L0_conv_w_qkv"], 0, C, 3 * C, 3 * C), 0)
            load(eng, W4[:, U_P, :], rep(a["L0_conv_w_proj"], 0, C, C, C), 0)
            load(eng, NB[:, 0, :], rep(a["L1_conv_in_proj_w"], C * C, C, C, C))
            load(eng, WIN[:, 0, :], rep(a["L1_conv_in_proj_w"], 0, C, C, C))
            load(eng, NB[:, 3, :], rep(a["L1_conv_out_proj_w"], 0, C, C, C))
            load(eng, NB[:, 16, 0:R], rep(a["L1_conv_dt_proj_w"], 0, C, R, R))
            for g in range(G):
                load(eng, NB[C * g:C * g + R + 2 * DS, 17, :], a["L1_conv_x_proj_w"])
            for k, m in enumerate(("w1", "w2", "wout")):
                load(eng, W8[:, k, :], rep(a["L1_conv_" + m], 0, C, 8, 8))
            load(eng, AL[:, :], rep(a["L1_conv_A_log"], 0, C, DS, DS))
            load(eng, C1[:, :], rep(a["L1_conv_conv1d_w"], 0, C, 3, 3))
            load(eng, wzn[:, :], a["L2_conv_Wz"])

            def w4(u, name, cols=C, stride=C, c0=0):
                load(eng, W4[:, u, c0:c0 + cols], rep(a[name], 0, C, cols, stride), 2)
            for u, m in ((U_A, "a"), (U_B, "b")):
                for t in range(2):
                    w4(u, f"L2_conv_W{m}{t + 1}", cols=C2, stride=C2, c0=C2 * t)
            w4(U_G, "L2_conv_Wg")
            for k, m in enumerate("ifoc"):
                w4(U_X + k, f"L3_conv_W{m}x")
                w4(U_M + k, f"L3_conv_W{m}m")
            load(eng, wzraw[:, :], bass.AP(a["L2_conv_Wz"].tensor, 0, [[0, 8], [C, C2], [1, C]]), 2)

            with nc.allow_non_contiguous_dma(reason="small per-channel vectors"):
                col(eng, V_BG, "L2_conv_bg", stage=2)
                load(eng, vec[:, V_LG:V_LG + 1], bass.AP(a["L2_conv_ln2_g"].tensor, 0, [[0, 8], [1, C2], [1, 1]]), 2)
            for k, m in enumerate(("ba1", "ba2", "bb1", "bb2")):
                load(eng, BAB[:, k // 2, C2 * (k % 2):C2 * (k % 2) + C2], bass.AP(a["L2_conv_" + m].tensor, 0, [[0, P], [1, C2]]), 2)
            for k, m in enumerate("ifoc"):
                load(eng, BL[k:k + 1, :, :], bass.AP(a["L3_conv_b" + m].tensor, 0, [[0, 1], [0, G], [1, C]]), 2)


            ov = out.rearrange("b h w c -> (b h w c)").rearrange("(r p c) -> p r c", p=112, c=C)

            def store(t, par):
                eng.wait_ge(r_o, t + 1)
                eng.dma_start(ov[:, bass.ds(t * 4, 4), :], Os[:, par]).then_inc(s_out[par], 16)
            with eng.Fori(0, H // 2) as it:
                store(it * 2, 0)
                store(it * 2 + 1, 1)
            for p_ in range(2):
                eng.wait_ge(s_out[p_], 16 * (H // 2))

        @block.gpsimd
        def _(eng):
            eng.memset(NB[:, 16:18, :], 0.0).then_inc(s_z0, 1)
            eng.memset(ident[:, :], 0.0).then_inc(s_mk, 1)
            for m in (bd, m16, m8):
                eng.memset(m[:, :], 1.0).then_inc(s_mk, 1)
            eng.wait_ge(s_mk, 4)
            eng.affine_select(out=ident[:, :], in_=ident[:, :], compare_op=ALU.not_equal, fill=1.0,
                              base=0, pattern=[[-1, P]], channel_multiplier=1).then_inc(s_mk, 1)
            for m, w, n in ((bd, 32, G), (m16, 8, 16), (m8, 16, 8)):
                eng.affine_select(out=m[:, :], in_=m[:, :], compare_op=ALU.is_ge, fill=0.0,
                                  base=0, pattern=[[-w, n]], channel_multiplier=1).then_inc(s_mk, 1)
            eng.memset(half3[:, :], 0.5).then_inc(s_hf, 1)
            eng.wait_ge(s_hf, 1)
            eng.affine_select(out=half3[:, :], in_=half3[:, :], compare_op=ALU.not_equal, fill=1.0,
                              base=-3, pattern=[[0, 1]], channel_multiplier=1).then_inc(s_hf, 1)
            eng.wait_ge(s_mk, 8)
            for m, w, n in ((bd, 32, G), (m16, 8, 16), (m8, 16, 8)):
                eng.affine_select(out=m[:, :], in_=m[:, :], compare_op=ALU.is_ge, fill=0.0,
                                  base=w - 1, pattern=[[w, n]], channel_multiplier=-1).then_inc(s_mk, 1)
            with nc.allow_non_contiguous_dma(reason="small per-channel vectors"):
                for k in range(3):
                    col(eng, V_BQ + k, "L0_conv_b_qkv", C * k, stage=0)
                col(eng, V_BP, "L0_conv_b_proj", stage=0)
                for k, m in ((V_CB, "conv1d_b"), (V_DTB, "dt_proj_b"), (V_D, "D_param"), (V_GA, "gamma"), (V_BE, "beta")):
                    col(eng, k, "L1_conv_" + m)
                col(eng, V_BZ, "L2_conv_bz")
                load(eng, lnb[:, :], bass.AP(a["L2_conv_ln2_b"].tensor, 0, [[1, C2], [1, 1]]))
                for g in range(G):
                    load(eng, DW[C * g:C * g + C, :], bass.AP(a["L1_conv_dw"].tensor, 0, [[1, C], [C, 9]]))
            eng.wait_ge(s_ev, 8)
            for m in (xw, Qw, Vst, Pr):
                eng.memset(m[:], 0.0).then_inc(s_mk2, 1)
            eng.wait_ge(s_mk2, 4)

            def pool_att(s, par):
                nxt = not isinstance(s, int) or s + 1 < NS
                cur = not isinstance(s, int) or s >= 0
                np_ = 1 - par
                if nxt:
                    if isinstance(s, int) and s < 0:
                        eng.wait_ge(s_xn, J)
                    if not isinstance(s, int) or s >= 1:
                        eng.wait_ge(v_r, s)
                    for u in range(2):
                        ins = eng.tensor_copy(xw[:, np_, :, u, 0:WT].rearrange("p w (r c) -> p w r c", r=WS),
                                              windows(XN[:, strip(s + 1)]))
                    ins.then_inc(xw_r, 1)
                    eng.wait_ge(k_r, s + 2)
                    if not isinstance(s, int) or s >= 1:
                        eng.wait_ge(s_r, s)
                    eng.tensor_tensor(Km[:, np_], bcast(Ks[:, np_], 2, NH), bcast(bcast(mask8[:, :], 1, NW), 3, WT),
                                      ALU.mult).then_inc(km_r, 1)
                if cur:
                    for g in range(G):
                        eng.wait_ge(rec_r, 4 * s + g + 1)
                        pg = Pr[:, par, g, :, 0:WT]
                        eng.tensor_tensor(pg, pg, bcast(rc[:, g, :], 2, WT), ALU.mult).then_inc(pn_r, 1)

            for s in (-1, 0, 1, 2):
                pool_att(s, s % 2)
            with eng.Fori(0, 6) as it:
                pool_att(it * 2 + 3, 1)
                pool_att(it * 2 + 4, 0)
            pool_att(15, 1)

            eng.wait_ge(x1_r, NS)
            eng.memset(S1[:, 0:2], 0.0).then_inc(s1z, 1)

            def pool_ssm(i):
                f, k, c, m, w = parts(i)

                def add(n):
                    if c is None:
                        return
                    eng.wait_ge(v_c, DS * c + n + 1)
                    if n > 1:
                        eng.wait_ge(g_ya, (DS - 1) * c + n - 1)
                    y = YA[:, c % 2, :]
                    eng.tensor_tensor(y, y, hC[:, n % NHC, :], ALU.add).then_inc(g_ya, 1)

                def split(s, name):
                    if k is None:
                        return
                    eng.wait_ge(c_[name], k + 1)
                    two, one = BCf[0:2 * C, k % 2, s, :], BCf[0:C, k % 2, s, :]
                    eng.tensor_tensor(two, two, upper(two), ALU.subtract).then_inc(g_mid, 1)
                    eng.wait_ge(g_mid, 2 * k + s + 1)
                    eng.tensor_tensor(one, one, upper(one), ALU.subtract).then_inc(g_low, 1)

                if w is not None:
                    eng.wait_ge(v_nt1, w + 1)
                    if w:
                        eng.wait_ge(p_["wout"], w)
                    eng.tensor_tensor(nt[:, 2, :], nt[:, 1, :], X2[:, w, :], ALU.mult).then_inc(g_nt2, 1)
                split(0, "xB")
                add(1)
                split(1, "xC")
                add(2)
                add(3)
                add(4)
                if k is not None:
                    eng.wait_ge(a_l, k + 1)
                    mk = sp[:, SP_M, :]
                    eng.tensor_tensor(mk, mk, sp[:, SP_L, :], ALU.add).then_inc(g_ml, 1)
                add(5)
                if k is not None:
                    eng.wait_ge(a_w, k + 1)
                    eng.wait_ge(v_cc, k + 1)
                    eng.tensor_tensor(sp[:, SP_C, :], sp[:, SP_C, :], sp[:, SP_W, :], ALU.mult).then_inc(g_cw, 1)
                if m is not None:
                    eng.wait_ge(a_rs, m + 1)
                    if m:
                        eng.wait_ge(v_nt1, m)
                    eng.tensor_tensor(nt[:, 0, :], cS[:, :], rs[:, :], ALU.mult).then_inc(g_nt0, 1)
                add(6)
                add(7)

            for i in SSM_STEPS:
                pool_ssm(i)

            eng.wait_ge(c_["wout"], J)
            for m in (Zc, XR):
                eng.memset(m[:], 0.0).then_inc(t_zz, 1)
            for n in range(14):
                eng.wait_ge(t_p1, n + 1)
                if n >= 2:
                    eng.wait_ge(t_sg, n - 1)
                fac = p1[:, n % 2].rearrange("p (m t c) -> p m t c", m=16, t=2)
                eng.tensor_tensor(pp[:, n % 2].rearrange("p (m c) -> p m c", m=16), fac[:, :, 0, :], fac[:, :, 1, :],
                                  ALU.mult).then_inc(t_pp, 1)

        @block.scalar
        def _(eng):
            chain = [0]

            def link(ins):
                chain[0] += 1
                ins.then_inc(s_a, 1)
                eng.wait_ge(s_a, chain[0])

            for j in range(1, J, 2):
                eng.wait_ge(s_x[j], 16)
                eng.activation(XS[0:LP, j].rearrange("p s g c -> p g s c"), XT[0:LP, j], ACT.Copy).then_inc(s_xs[j], 1)
            for q in range(1, 7, 2):
                eng.wait_ge(s_tr, q + 1)
                evac_in(eng, q)
            def gn(layer):
                eng.wait_ge(s_mv, layer + 1)
                if layer:
                    eng.wait_ge(s_xn, J * layer)
                link(eng.activation(lnv[:, :], mv[:, :, 1], ACT.Ln, bias=epsc[:, 0:1]))
                eng.activation(rstd[:, :], lnv[:, :], ACT.Exp, scale=-0.5).then_inc(s_rs, 1)

            gn(0)

            loaded(eng, 0)
            eng.wait_ge(s_mk2, 4)

            def act_att(s, par):
                fixed = isinstance(s, int)
                nxt = not fixed or s + 1 < NS
                cur = not fixed or 0 <= s < NS
                prv = not fixed or 1 <= s <= NS
                np_ = 1 - par
                if nxt:
                    eng.wait_ge(qk_d, s + 2)
                    if not fixed or s >= 1:
                        eng.wait_ge(s_r, s)
                    eng.activation(Qw[:, np_, :, 0:WT].rearrange("p w (r c) -> p w r c", r=WS),
                                   windows(banks[4][:, 0:ST]), ACT.Identity,
                                   bias=vec[:, V_BQS:V_BQS + 1], scale=SCALE).then_inc(q_r, 1)
                    if not fixed or s >= 1:
                        eng.wait_ge(km_r, s)
                    eng.activation(Ks[:, np_].rearrange("p w (r c) -> p w r c", r=WS),
                                   windows(banks[4][:, ST:2 * ST]), ACT.Identity,
                                   bias=vec[:, V_BK:V_BK + 1]).then_inc(k_r, 1)
                for g in range(G):
                    if prv:
                        eng.wait_ge(t_r, 4 * (s - 1) + g + 1)
                        if not fixed or 4 * (s - 1) + g >= 2:
                            eng.wait_ge(av_r, 4 * (s - 1) + g - 1)
                        eng.activation(PT[:, g % 2].rearrange("p a b q -> p (a b q)"),
                                       banks[5 + (par + 1 + g) % 2][:, :], ACT.Copy).then_inc(ring_r, 1)
                    if cur:
                        eng.wait_ge(sub_r, 4 * s + g + 1)
                        if not fixed or s >= 2:
                            eng.wait_ge(t_r, 4 * (s - 2) + g + 1)
                        eng.activation(Pr[:, par, g, :, 0:WT], Ts[:, g, :, :], ACT.Exp).then_inc(exp_r, 1)
                if nxt:
                    eng.wait_ge(v_r, s + 2)
                    if not fixed or s >= 1:
                        eng.wait_ge(av_r, 4 * s)
                    vb = banks[5 + (par + 1) % 2]
                    for u in range(2):
                        src = vb[64 * u:64 * u + 64, :].rearrange("p (m e q d) -> p m e q d", m=16, e=2, q=2)[:, :, :, u, :]
                        dst = Vst[64 * u:64 * u + 64, np_].rearrange("p w g e n -> p (w g) (e n)")
                        dst = bass.AP(dst.tensor, dst.offset + HD * u, [list(dst.ap[0]), [64, 16], [48, 2], [1, HD]])
                        eng.activation(dst, src, ACT.Copy).then_inc(ring_r, 1)

            act_att(-1, 1)
            loaded(eng, 1)
            eng.activation(AE[:, :], AL[:, :], ACT.Exp).then_inc(s_ae, 1)
            for s in (0, 1, 2):
                act_att(s, s % 2)
            with eng.Fori(0, 6) as it:
                act_att(it * 2 + 3, 1)
                act_att(it * 2 + 4, 0)
            act_att(15, 1)
            act_att(16, 0)

            gn(1)

            eng.wait_ge(s1z, 1)

            def act_ssm(i):
                f, k, c, m, w = parts(i)
                q = None if k is None else k % 2

                def decays(*states):
                    if c is None:
                        return
                    for n in states:
                        if DS * c + n >= NA:
                            eng.wait_ge(v_s, DS * c + n - NA + 1)
                        eng.activation(dA[:, n % NA, :], DL[:, c % 2, :], ACT.Exp, scale=Aneg[:, n:n + 1]).then_inc(a_da, 1)

                if c is not None:
                    eng.wait_ge(v_dl, c + 1)
                decays(0, 1)
                if k is not None:
                    eng.wait_ge(p_["delta"], k + 1)
                    if k:
                        eng.wait_ge(v_dl, k)
                    eng.activation(halves(sp[:, SP_E, :]), result("delta"), ACT.Abs, bias=vec[:, V_DTB:V_DTB + 1])
                    eng.activation(halves(sp[:, SP_M, :]), result("delta"), ACT.Relu, bias=vec[:, V_DTB:V_DTB + 1]).then_inc(c_["delta"], 1)
                    for s, name in enumerate(("xB", "xC")):
                        eng.wait_ge(p_[name], k + 1)
                        if k >= 2:
                            eng.wait_ge(p_["BC"[s]], DS * (k - 1))
                        eng.activation(halves(BCf[:, q, s, :]), result(name)[0:3 * C], ACT.Copy).then_inc(c_[name], 1)
                if k is not None:
                    eng.wait_ge(c_["delta"], k + 1)
                    eng.activation(sp[:, SP_E, :], sp[:, SP_E, :], ACT.Exp, scale=-1.0).then_inc(a_e, 1)
                decays(2, 3)
                if k is not None:
                    eng.wait_ge(a_e, k + 1)
                    eng.activation(sp[:, SP_U, :], sp[:, SP_E, :], ACT.Identity, bias=1.0).then_inc(a_u, 1)
                if m is not None:
                    eng.wait_ge(p_["out"], m + 1)
                    if m:
                        eng.wait_ge(g_nt0, m)
                        eng.wait_ge(p_["var"], m)
                    eng.activation(halves(cS[:, :]), result("out"), ACT.Copy)
                    eng.activation(halves(sq[:, :]), result("out"), ACT.Square).then_inc(c_["out"], 1)
                decays(4, 5)
                if k is not None:
                    eng.wait_ge(a_u, k + 1)
                    eng.activation(sp[:, SP_L, :], sp[:, SP_U, :], ACT.Ln).then_inc(a_l, 1)
                if m is not None:
                    eng.wait_ge(p_["var"], m + 1)
                    eng.activation(halves(lv[:, :]), result("var"), ACT.Ln, bias=epsc[:, 0:1]).then_inc(c_["var"], 1)
                if k is not None:
                    eng.wait_ge(a_l, k + 1)
                    eng.activation(sp[:, SP_W, :], sp[:, SP_L, :], ACT.Exp, scale=-1.0).then_inc(a_w, 1)
                if m is not None:
                    eng.wait_ge(c_["var"], m + 1)
                    eng.activation(rs[:, :], lv[:, :], ACT.Exp, scale=-0.5).then_inc(a_rs, 1)
                decays(6, 7)
                if f is not None:
                    eng.wait_ge(p_["conv"], f + 1)
                    if f:
                        eng.wait_ge(p_["z"], f)
                    eng.activation(halves(S1[:, 2:T + 2]), result("conv"), ACT.Silu).then_inc(c_["conv"], 1)
                    eng.wait_ge(p_["x2"], f + 1)
                    eng.activation(halves(X2[:, f, :]), result("x2"), ACT.Silu).then_inc(c_["x2"], 1)
                    eng.wait_ge(p_["u"], f + 1)
                    eng.activation(halves(US[:, f, :]), result("u"), ACT.Silu, bias=vec[:, V_CB:V_CB + 1]).then_inc(c_["u"], 1)
                    eng.wait_ge(p_["z"], f + 1)
                    eng.activation(halves(ZS[:, f, :]), result("z"), ACT.Silu).then_inc(c_["z"], 1)

            for i in SSM_STEPS:
                act_ssm(i)

            gn(2)

            for n in range(14):
                side, q = n // 7, n % 7
                eng.wait_ge(t_pp, n + 1)
                eng.activation(Ab[:, side, :, 4 * q:4 * q + 4].rearrange("p m i -> p i m"),
                               pp[:, n % 2].rearrange("p (i m) -> p i m", i=4), ACT.Sigmoid).then_inc(t_sg, 1)
            for n in range(8):
                eng.wait_ge(t_g, n + 1)
                eng.activation(flat(Gt)[:, n * HT:(n + 1) * HT], banks[2 + n % 2][:, 0:HT], ACT.Sigmoid,
                               bias=vec[:, V_BG:V_BG + 1]).then_inc(t_gd, 1)
            for g in range(G):
                eng.wait_ge(t_z, g + 1)
                take_z(eng, g, (2, 3)).then_inc(t_za, 1)
                eng.wait_ge(t_c, g + 1)
                if g >= 2:
                    eng.wait_ge(t_v, g - 1)
                eng.activation(Zq[:, g % 2].rearrange("p (j c) -> p j c", c=C2), Zc[:, :, C2 * g:C2 * g + C2],
                               ACT.Square).then_inc(t_q, 1)
            eng.wait_ge(t_v, G)
            eng.activation(zst[:, 2], zst[:, 1], ACT.Ln, bias=epsc[:, 0:1], scale=1.0 / C2).then_inc(t_r1, 1)
            eng.wait_ge(t_r1, 1)
            eng.activation(zst[:, 3], zst[:, 2], ACT.Exp, scale=-0.5).then_inc(t_r2, 1)
            for n in range(4):
                eng.wait_ge(t_t, n + 1)
                m = min(4, 14 - 4 * n) * P
                eng.activation(ZT[:, 512 * n:512 * n + m], banks[4 + n % 2][:, 0:m], ACT.Copy).then_inc(t_te, 1)
            gn(3)

            def act_step(t, par):
                eng.wait_ge(r_z, t + 1)
                zb = banks[par]
                if not isinstance(t, int) or t >= 2:
                    eng.wait_ge(r_h, t - 1)
                eng.activation(gates[:, par].rearrange("p k n -> p (k n)"), zb[:, 0:448], ACT.Tanh).then_inc(r_g, 1)
                eng.wait_ge(r_c, t + 1)
                eng.activation(tcn[:, :], cst[:, 1 - par, :], ACT.Tanh, scale=0.5).then_inc(r_th, 1)

            act_step(0, 0)
            act_step(1, 1)
            with eng.Fori(1, H // 2) as it:
                act_step(it * 2, 0)
                act_step(it * 2 + 1, 1)

        @block.tensor
        def _(eng):
            eng.wait_ge(s_mk, 11)
            for n in range(J * SP):
                j, s = divmod(n, SP)
                if s == 0:
                    eng.wait_ge(s_xs[j], 1)
                q = n // 4
                ins = eng.transpose(banks[q][:, LP * (n % 4):LP * (n % 4) + LP], XS[0:LP, j, s].rearrange("p g c -> p (g c)"), ident[0:LP, 0:LP])
                if n % 4 == 3:
                    ins.then_inc(s_tr, 1)

            def pe_att(s, par):
                fixed = isinstance(s, int)
                nxt = not fixed or s + 1 < NS
                cur = not fixed or 0 <= s < NS
                prv = not fixed or 1 <= s <= NS
                prv2 = not fixed or s >= 2
                np_ = 1 - par
                if cur:
                    eng.wait_ge(q_r, s + 1)
                    eng.wait_ge(km_r, s + 1)
                    if not fixed or s >= 1:
                        eng.wait_ge(sub_r, 4 * s)
                    for w in range(NW):
                        for g in range(G):
                            ins = eng.matmul(banks[g][64 * (w % 2):64 * (w % 2) + 64, 196 * (w // 2):196 * (w // 2) + 196],
                                             Qw[C * g:C * g + C, par, w, :],
                                             Km[C * g:C * g + C, par, w].rearrange("p h k -> p (h k)"), start=True, stop=True)
                    ins.then_inc(s_r, 1)
                if nxt:
                    if fixed and s < 0:
                        eng.wait_ge(s_xn, J)
                    else:
                        eng.wait_ge(k_r, s + 1)
                    if not fixed or s >= 3:
                        eng.wait_ge(x1_r, s - 2)
                    eng.matmul(banks[4][:, 0:ST], BD[:, U_Q, :], XN[:, strip(s + 1)], start=True, stop=True)
                    eng.matmul(banks[4][:, ST:2 * ST], BD[:, U_K, :], XN[:, strip(s + 1)], start=True, stop=True).then_inc(qk_d, 1)

                def project():
                    eng.wait_ge(ao_r, s - 1)
                    if nxt:
                        eng.wait_ge(k_r, s + 2)
                    elif s > NS:
                        eng.wait_ge(x1_r, NS - 1)
                    eng.matmul(banks[4][:, 0:ST], BD[:, U_P, :], AO[:, par, :], start=True, stop=True).then_inc(pj_r, 1)

                last = fixed and s == NS
                base = 6 * (s - 1) + 4 - (2 if last else 0)

                def transposes(g):
                    eng.wait_ge(pn_r, 4 * (s - 1) + g + 1)
                    if g == 0:
                        eng.wait_ge(ring_r, base if last else base - 2)
                    elif g == 1:
                        eng.wait_ge(ring_r, base)
                    else:
                        eng.wait_ge(ring_r, base + g - 1)
                    bk = banks[5 + (par + 1 + g) % 2]
                    for k in range(4):
                        pg = Pr[:, np_, g, 2 * k:2 * k + 2, :].rearrange("p h k -> p (h k)")
                        ins = eng.transpose(bk[:, P * k:P * k + P], pg, ident[:, :])
                    ins.then_inc(t_r, 1)

                def av(g):
                    eng.wait_ge(ring_r, base + g + 1)
                    if g == 0 and (not fixed or s >= 2):
                        eng.wait_ge(ao_r, s - 1)
                    for w in range(NW):
                        for e in range(2):
                            ins = eng.matmul(banks[7][C * g:C * g + C, WT * w:WT * w + WT], Vst[:, np_, w, g, e, :],
                                             PT[:, g % 2, w // 2, e, 64 * (w % 2):64 * (w % 2) + WT],
                                             start=(e == 0), stop=(e == 1))
                    ins.then_inc(av_r, 1)

                if prv:
                    transposes(0)
                    transposes(1)
                if prv2:
                    project()
                if prv:
                    av(0)
                    transposes(2)
                    av(1)
                    transposes(3)
                    av(2)
                if nxt:
                    eng.wait_ge(xw_r, s + 2)
                    if prv:
                        eng.wait_ge(ring_r, base + 3)
                    for w in range(NW):
                        ins = eng.matmul(banks[5 + (par + 1) % 2][:, P * w:P * w + P], xw[:, np_, w].rearrange("p u k -> p (u k)"),
                                         BD[:, U_V, :], start=True, stop=True)
                    ins.then_inc(v_r, 1)
                if prv:
                    av(3)

            pe_att(-1, 1)
            eng.wait_ge(s_v, TRB)
            for g in range(G):
                rows = slice(C * g, C * g + C)
                eng.matmul(banks[7][rows, 0:C], NB[0:R, 17, :], TB[0:R, 16, :], start=True, stop=True)
                ins = eng.matmul(banks[7][rows, C:C + 1], wzn[:, :], lnb[:, :], start=True, stop=True)
            ins.then_inc(s_wd, 1)
            for s in (0, 1, 2):
                pe_att(s, s % 2)
            with eng.Fori(0, 6) as it:
                pe_att(it * 2 + 3, 1)
                pe_att(it * 2 + 4, 0)
            for s in (15, 16, 17):
                pe_att(s, s % 2)

            order = []

            def claim(name):
                last = [n for n in order if PAIR[n] == PAIR[name]]
                if last:
                    eng.wait_ge(c_[last[-1]], order.count(last[-1]))
                order.append(name)

            def product(name, w, rhs):
                claim(name)
                for h in range(2):
                    ins = eng.matmul(result(name)[0:w.shape[-1], h, :], w, rhs[:, HT * h:HT * h + HT], start=True, stop=True)
                ins.then_inc(p_[name], 1)

            img = XN[:, :].rearrange("p (b y x) -> p b y x", b=J, y=30)

            def pe_ssm(i):
                f, k, c, m, w = parts(i)

                def spread(name, n):
                    if c is None or n < 0:
                        return
                    s = "BC".index(name)
                    eng.wait_ge(g_low, 2 * c + s + 1)
                    eng.wait_ge((v_b, v_c)[s], DS * c + n)
                    for h in range(2):
                        ins = eng.matmul(result(name)[:, h, :], sel[:, n, :], upper(BCf[:, c % 2, s, HT * h:HT * h + HT]),
                                         start=True, stop=True)
                    ins.then_inc(p_[name], 1)

                def conv(first, last):
                    if f is None:
                        return
                    if first == 0:
                        eng.wait_ge(s_xn, J + f + 1)
                        claim("conv")
                    for n in range(first, last):
                        h, tap = divmod(n, 9)
                        y, x = 14 * h + tap // 3, tap % 3
                        ins = eng.matmul(result("conv")[:, h, :].rearrange("p (y x) -> p y x", x=W), BD[:, U_CV + tap, :],
                                         img[:, f, y:y + 14, x:x + W], start=(tap == 0), stop=(tap == 8))
                    if last == 18:
                        ins.then_inc(p_["conv"], 1)

                def inner(first, last):
                    if f is None:
                        return
                    if first == 0:
                        eng.wait_ge(c_["conv"], f + 1)
                        claim("u")
                    for n in range(first, last):
                        h, tap = divmod(n, 3)
                        ins = eng.matmul(result("u")[:, h, :], BD[:, U_U + tap, :], S1[:, HT * h + tap:HT * h + tap + HT],
                                         start=(tap == 0), stop=(tap == 2))
                    if last == 6:
                        ins.then_inc(p_["u"], 1)

                def slot(n):
                    spread("B", n)
                    spread("C", n - 1)

                slot(0)
                if k is not None:
                    eng.wait_ge(c_["u"], k + 1)
                    product("delta", BD[:, U_DL, :], US[:, k, :])
                    product("xB", WBC[:, 0, :], US[:, k, :])
                slot(1)
                if k is not None:
                    product("xC", WBC[:, 1, :], US[:, k, :])
                slot(2)
                conv(0, 2)
                if m is not None:
                    eng.wait_ge(v_y2, m + 1)
                    product("out", BD[:, U_OUT, :], y2[:, :])
                conv(2, 4)
                slot(3)
                conv(4, 6)
                if w is not None:
                    eng.wait_ge(g_nt2, w + 1)
                    product("wout", BD[:, U_WO, :], nt[:, 2, :])
                conv(6, 8)
                slot(4)
                conv(8, 12)
                if m is not None:
                    eng.wait_ge(c_["out"], m + 1)
                    product("var", VB[:, :], sq[:, :])
                slot(5)
                conv(12, 16)
                slot(6)
                conv(16, 18)
                if f is not None:
                    claim("x2")
                    for h in range(2):
                        ins = eng.matmul(result("x2")[:, h, :].rearrange("p (y x) -> p y x", x=W), BD[:, U_X2, :],
                                         img[:, f, 14 * h + 1:14 * h + 15, 1:W + 1], start=True, stop=True)
                    ins.then_inc(p_["x2"], 1)
                inner(0, 4)
                slot(7)
                inner(4, 6)
                spread("C", 7)
                if f is not None:
                    product("z", BD[:, U_Z, :], S1[:, 2:T + 2])

            eng.wait_ge(s1z, 1)
            for i in SSM_STEPS:
                pe_ssm(i)

            eng.wait_ge(s_xn, 3 * J)
            for n in range(14):
                side, q = n // 7, n % 7
                if n >= 2:
                    eng.wait_ge(t_p1, n - 1)
                if n == 7:
                    eng.wait_ge(t_xr, 1)
                bk = banks[n % 2]
                for r in range(4):
                    i = 4 * q + r
                    ins = eng.matmul(bk[:, P * r:P * r + P], XR[:, side, i].rearrange("p b k -> p (b k)"), BD[:, U_A + side, :], start=True, stop=True)
                ins.then_inc(t_pr, 1)
            for n in range(8):
                if n >= 2:
                    eng.wait_ge(t_gd, n - 1)
                eng.matmul(banks[2 + n % 2][:, 0:HT].rearrange("p (y x) -> p y x", x=W), BD[:, U_G, :],
                           XR[:, 0, 14 * (n % 2):14 * (n % 2) + 14, n // 2, 0:W], start=True, stop=True).then_inc(t_g, 1)
            eng.wait_ge(t_sg, 14)
            for g in range(G):
                if g == 1:
                    eng.wait_ge(t_gd, 8)
                if g >= 2:
                    eng.wait_ge(t_zc, g - 1)
                    eng.wait_ge(t_za, g - 1)
                first = 4 - 4 * (g % 2)
                for c in range(C2):
                    for b in range(J):
                        m = C2 * g + c
                        ins = eng.matmul(banks[first + b][32 * b:32 * b + H, H * c:H * c + H], Ab[32 * b:32 * b + H, 0, m, :],
                                         Ab[32 * b:32 * b + H, 1, m, :], start=True, stop=True)
                ins.then_inc(t_z, 1)
            for q in range(14):
                if q % 4 == 0:
                    eng.wait_ge(t_n, q // 4 + 1)
                if q % 4 == 0 and q >= 8:
                    eng.wait_ge(t_te, q // 4 - 1)
                ins = eng.transpose(banks[4 + (q // 4) % 2][:, P * (q % 4):P * (q % 4) + P],
                                    Zc[:, 2 * q:2 * q + 2, :].rearrange("p j m -> p (j m)"), ident[:, :])
                if q % 4 == 3 or q == 13:
                    ins.then_inc(t_t, 1)
            for n in range(8):
                q, par = n % 4, n // 4
                m = min(4, 14 - 4 * q) * P
                eng.wait_ge(t_te, q + 1)
                if n >= 2:
                    eng.wait_ge(t_y, n - 1)
                eng.matmul(banks[6 + n % 2][:, 0:m], WZ[64 * par:64 * par + 64, :], ZT[64 * par:64 * par + 64, 512 * q:512 * q + m],
                           start=True, stop=True).then_inc(t_o, 1)

            eng.wait_ge(t_x3, 1)
            for n in range(28):
                q = n // 4
                if n % 4 == 0 and q >= 2:
                    eng.wait_ge(r_te, q - 1)
                ins = eng.transpose(banks[2 + q % 2][0:112, P * (n % 4):P * (n % 4) + P], X[:, 112 * n:112 * n + 112], ident[:, :])
                if n % 4 == 3:
                    ins.then_inc(r_t, 1)

            def inputs(t, par):
                zb = banks[par]
                if not isinstance(t, int) or t >= 2:
                    eng.wait_ge(r_g, t - 1)
                eng.matmul(zb[:, 0:448].rearrange("p (k n) -> p k n", k=4), BL[:, :, :].rearrange("k g c -> k (g c)"),
                           bcast(ident[0:4, 0:4], 2, 112), start=True, stop=False, skip_group_check=True)
                for k in range(4):
                    xt = XN[:, 0:N].rearrange("p (b t) -> p b t", b=J)[:, :, bass.ds(t * W, W)]
                    eng.matmul(zb[:, 112 * k:112 * k + 112].rearrange("p (b n) -> p b n", b=J), BD[:, U_X + k, :], xt, start=False, stop=False, skip_group_check=True)

            def recur(t, par, after=True):
                zb = banks[par]
                if not isinstance(t, int) or t >= 1:
                    eng.wait_ge(r_h, t)
                else:
                    eng.wait_ge(r_in, 1)
                for k in range(4):
                    ins = eng.matmul(zb[:, 112 * k:112 * k + 112], BD[:, U_M + k, :], hst[:, 1 - par, :], start=False, stop=True,
                                     skip_group_check=True)
                ins.then_inc(r_z, 1)

            def turn(t, par):
                eng.wait_ge(r_h, t + 1)
                if not isinstance(t, int) or t >= 2:
                    eng.wait_ge(r_o, t - 1)
                eng.transpose(banks[4 + par][0:112, 0:P], hst[:, par, :], ident[:, :]).then_inc(r_t, 1)

            eng.wait_ge(s_xn, 4 * J)
            inputs(0, 0)
            recur(0, 0)
            inputs(1, 1)
            recur(1, 1)
            turn(0, 0)
            inputs(2, 0)
            recur(2, 0)
            turn(1, 1)
            inputs(3, 1)
            with eng.Fori(1, H // 2 - 1) as it:
                recur(it * 2 + 1, 1)
                turn(it * 2, 0)
                inputs(it * 2 + 2, 0)
                recur(it * 2 + 2, 0)
                turn(it * 2 + 1, 1)
                inputs(it * 2 + 3, 1)
            recur(H - 1, 1)
            turn(H - 2, 0)
            turn(H - 1, 1)

        @block.vector
        def _(eng):
            chain = [0]

            def link(ins):
                chain[0] += 1
                ins.then_inc(s_v, 1)
                eng.wait_ge(s_v, chain[0])

            eng.memset(epsc[:, :], EPS).then_inc(s_ev, 1)
            for j in range(0, J, 2):
                eng.wait_ge(s_x[j], 16)
                eng.tensor_copy(XS[0:LP, j].rearrange("p s g c -> p g s c"), XT[0:LP, j]).then_inc(s_xs[j], 1)
            for q in range(0, 7, 2):
                eng.wait_ge(s_tr, q + 1)
                evac_in(eng, q)

            def gn_stats(layer):
                if layer:
                    eng.wait_ge(s_xn, J * layer)
                for j in range(J):
                    for h in range(2):
                        ins = eng.bn_stats(stats[:, j, h, :], X[:, T * j + HT * h:T * j + HT * h + HT])
                link(ins)
                for j in range(J):
                    ins = eng.bn_aggr(mv[:, j, :], stats[:, j].rearrange("p h s -> p (h s)"))
                ins.then_inc(s_mv, 1)
                eng.wait_ge(s_mv, layer + 1)

            def gn_apply(layer, dst):
                eng.wait_ge(s_rs, layer + 1)
                for j in range(J):
                    src = X[:, T * j:T * j + T]
                    d = dst(j)
                    if len(d.shape) == 3:
                        src = src.rearrange("p (y x) -> p y x", y=H)
                    eng.tensor_scalar(d, src, mv[:, j, 0:1], rstd[:, j:j + 1], ALU.subtract, ALU.mult).then_inc(s_xn, 1)

            eng.wait_ge(s_ev, 8)
            gn_stats(0)

            eng.wait_ge(s_mk, 11)
            loaded(eng, 0)

            def spread_weights(u0, u1):
                return eng.tensor_tensor(BD[:, u0:u1, :].rearrange("p u (g c) -> p u g c", g=G), bcast(W4[:, u0:u1, :], 2, G),
                                         bcast(bcast(bd[:, :], 1, u1 - u0), 3, C), ALU.mult)
            eng.tensor_scalar(vec[:, V_BQS:V_BQS + 1], vec[:, V_BQ:V_BQ + 1], SCALE, None, ALU.mult)
            eng.tensor_reduce(mask8[:, :], m16[:, :].rearrange("p (g h) -> p h g", g=G), AX.X, ALU.add)
            spread_weights(U_Q, U_P + 1)
            gn_apply(0, lambda j: XN[:, T * j:T * j + T])

            loaded(eng, 1)
            eng.wait_ge(s_hf, 2)
            link(eng.tensor_tensor(maskz[:, :], m8[:, 0:4], m8[:, 4:8], ALU.add))
            for k, dst in ((0, W8X[:, :]), (1, NB[:, 1, :]), (2, NB[:, 2, :])):
                ins = eng.tensor_tensor(dst.rearrange("p (h i) -> p h i", h=4), bcast(W8[:, k, :], 1, 4), bcast(mask8[:, :], 2, 8), ALU.mult)
            link(ins)
            for k in range(3):
                eng.tensor_scalar(NB[:, 4 + k, :], WIN[:, 0, :], C1[:, k:k + 1], None, ALU.mult)
            for k in range(9):
                ins = eng.tensor_scalar(NB[:, 7 + k, :], W8X[:, :], DW[:, k:k + 1], None, ALU.mult)
            link(ins)
            link(eng.transpose(TB[:, :, :].rearrange("p u c -> p (u c)"), NB[:, :, :].rearrange("p u c -> p (u c)")))
            assert chain[0] == TRB
            link(eng.tensor_reduce(omean[:, :], TB[:, 3, :], AX.X, ALU.add))
            link(eng.tensor_scalar(omean[:, :], omean[:, :], 1.0 / C, None, ALU.mult))
            link(eng.tensor_scalar(TB[:, 3, :], TB[:, 3, :], omean[:, 0:1], None, ALU.subtract))
            eng.tensor_copy(W4[:, U_Z:U_DL, :], TB[:, 0:16, :])
            eng.wait_ge(s_wd, 1)
            eng.tensor_copy(W4[:, U_DL, :], banks[7][:, 0:C])
            link(eng.tensor_tensor(vec[:, V_BZF:V_BZF + 1], vec[:, V_BZ:V_BZ + 1], banks[7][:, C:C + 1], ALU.add))
            spread_weights(U_Z, NU)
            for s in range(2):
                for q in range(3):
                    eng.tensor_tensor(WBC[:, s, C * q:C * q + C].rearrange("p (g n) -> p g n", g=G),
                                      bcast(TB[:, 17, R + DS * s:R + DS * s + DS], 1, G), bcast(bd[:, :], 2, DS), ALU.mult)
            for q in range(3):
                rows = slice(C * q, C * q + C)
                eng.tensor_copy(sel[rows].rearrange("p n (g c) -> p n g c", g=G),
                                bcast(ident[rows, rows].rearrange("p (g n) -> p n g", g=G), 3, C))
            eng.tensor_scalar(VB[:, :].rearrange("p (g c) -> p g c", g=G), bcast(bd[:, :], 2, C), 1.0 / C, None, ALU.mult)
            eng.wait_ge(s_ae, 1)
            link(eng.tensor_scalar(Aneg[:, :], AE[:, :], -1.0, None, ALU.mult))

            eng.wait_ge(s_mk2, 4)

            def dve_att(s, par):
                fixed = isinstance(s, int)
                cur = not fixed or 0 <= s < NS
                prv = not fixed or 1 <= s <= NS
                prv2 = not fixed or s >= 2
                np_ = 1 - par
                if cur:
                    eng.wait_ge(s_r, s + 1)
                    for g in range(G):
                        eng.tensor_reduce(mx[:, g, :], banks[g][:, 0:392].rearrange("p (m k) -> p m k", k=WT), AX.X,
                                          ALU.max).then_inc(max_r, 1)
                    for g in range(G):
                        eng.wait_ge(max_r, 4 * s + g + 1)
                        if not fixed or s >= 1:
                            eng.wait_ge(exp_r, 4 * (s - 1) + g + 1)
                        eng.tensor_tensor(Ts[:, g, :, :], banks[g][:, 0:392].rearrange("p (m k) -> p m k", k=WT),
                                          bcast(mx[:, g, :], 2, WT), ALU.subtract).then_inc(sub_r, 1)
                if prv2:
                    eng.wait_ge(pj_r, s - 1)
                    xs = X[:, strip(s - 2)]
                    eng.scalar_tensor_tensor(xs, banks[4][:, 0:ST], vec[:, V_BP:V_BP + 1], xs, ALU.add, ALU.add).then_inc(x1_r, 1)
                if cur:
                    for g in range(G):
                        eng.wait_ge(exp_r, 4 * s + g + 1)
                        if not fixed or s >= 1:
                            eng.wait_ge(pn_r, 4 * (s - 1) + g + 1)
                        eng.tensor_reduce(sm[:, g, :], Pr[:, par, g, :, 0:WT], AX.X, ALU.add).then_inc(sum_r, 1)
                    for g in range(G):
                        eng.wait_ge(sum_r, 4 * s + g + 1)
                        eng.reciprocal(rc[:, g, :], sm[:, g, :]).then_inc(rec_r, 1)
                if prv:
                    eng.wait_ge(av_r, 4 * s)
                    eng.tensor_scalar(windows(AO[:, np_, :]), banks[7][:, 0:ST].rearrange("p (w r c) -> p w r c", w=NW, r=WS),
                                      vec[:, V_BV:V_BV + 1], None, ALU.add).then_inc(ao_r, 1)

            for s in (0, 1, 2):
                dve_att(s, s % 2)
            with eng.Fori(0, 6) as it:
                dve_att(it * 2 + 3, 1)
                dve_att(it * 2 + 4, 0)
            for s in (15, 16, 17):
                dve_att(s, s % 2)

            eng.wait_ge(x1_r, NS)
            eng.memset(XN[:, :], 0.0).then_inc(s_v, 1)
            chain[0] += 1
            gn_stats(1)
            eng.wait_ge(s_v, chain[0])
            img = XN[:, :].rearrange("p (b y x) -> p b y x", b=J, y=30)
            gn_apply(1, lambda j: img[:, j, 1:29, 1:29])
            loaded(eng, 2)
            eng.tensor_scalar(W4[:, U_X:U_X + 3, :], W4[:, U_X:U_X + 3, :], 0.5, None, ALU.mult)
            eng.tensor_scalar(W4[:, U_M:U_M + 3, :], W4[:, U_M:U_M + 3, :], 0.25, None, ALU.mult)
            eng.tensor_scalar(W4[:, U_M + 3, :], W4[:, U_M + 3, :], 0.5, None, ALU.mult)
            link(eng.tensor_scalar(BL[:, :, :], BL[:, :, :], half3[:, 0:1], None, ALU.mult))
            spread_weights(U_A, U_Z)
            link(eng.tensor_scalar(wzs[:, :], wzraw[:, :], vec[:, V_LG:V_LG + 1], None, ALU.mult))
            eng.tensor_tensor(WZ[:, :].rearrange("p (g c) -> p g c", g=G), bcast(wzs[:, :], 1, G), bcast(maskz[:, :], 2, C), ALU.mult)

            def dve_ssm(i):
                f, k, c, m, w = parts(i)

                def times_b(n):
                    eng.wait_ge(p_["B"], DS * c + n + 1)
                    eng.wait_ge(v_du, c + 1)
                    if DS * c + n >= 2:
                        eng.wait_ge(v_s, DS * c + n - 1)
                    eng.tensor_tensor(halves(dBu[:, n % 2, :]), halves(DU[:, :]), result("B"), ALU.mult).then_inc(v_b, 1)

                def scan(n):
                    eng.wait_ge(v_b, DS * c + n + 1)
                    eng.wait_ge(a_da, DS * c + n + 1)
                    if DS * c + n >= 2:
                        eng.wait_ge(v_c, DS * c + n - 1)
                    eng.tensor_tensor_scan(Hs[:, n % 2, :], dA[:, n % NA, :], dBu[:, n % 2, :], 0.0, ALU.mult, ALU.add).then_inc(v_s, 1)

                def times_c(n):
                    eng.wait_ge(p_["C"], DS * c + n + 1)
                    eng.wait_ge(v_s, DS * c + n + 1)
                    if n == 0:
                        dst = YA[:, c % 2, :]
                    else:
                        dst = hC[:, n % NHC, :]
                        before = (DS - 1) * c + n - NHC if n > NHC else (DS - 1) * c + min(n - NHC, 0)
                        if before > 0:
                            eng.wait_ge(g_ya, before)
                    eng.tensor_tensor(halves(dst), halves(Hs[:, n % 2, :]), result("C"), ALU.mult).then_inc(v_c, 1)

                def slot(n):
                    if c is not None:
                        times_b(n)
                        if n:
                            times_c(n - 1)
                        scan(n)

                slot(0)
                slot(1)
                if m is not None:
                    eng.wait_ge(g_ya, (DS - 1) * (m + 1))
                    if m:
                        eng.wait_ge(v_y2, m)
                    eng.scalar_tensor_tensor(y1[:, :], US[:, m, :], vec[:, V_D:V_D + 1], YA[:, m % 2, :], ALU.mult, ALU.add).then_inc(v_y1, 1)
                    eng.wait_ge(v_y1, m + 1)
                    if m:
                        eng.wait_ge(p_["out"], m)
                    eng.wait_ge(c_["z"], m + 1)
                    eng.tensor_tensor(y2[:, :], y1[:, :], ZS[:, m, :], ALU.mult).then_inc(v_y2, 1)
                slot(2)
                slot(3)
                if k is not None:
                    eng.wait_ge(a_u, k + 1)
                    eng.scalar_tensor_tensor(sp[:, SP_C, :], sp[:, SP_U, :], 1.0, sp[:, SP_E, :], ALU.subtract, ALU.subtract).then_inc(v_cc, 1)
                if w is not None:
                    eng.wait_ge(p_["wout"], w + 1)
                    xs = X[:, w * T:w * T + T]
                    eng.tensor_tensor(halves(xs), halves(xs), result("wout"), ALU.add).then_inc(c_["wout"], 1)
                slot(4)
                slot(5)
                slot(6)
                slot(7)
                if m is not None:
                    eng.wait_ge(g_nt0, m + 1)
                    if m:
                        eng.wait_ge(g_nt2, m)
                    eng.tensor_scalar(nt[:, 1, :], nt[:, 0, :], vec[:, V_GA:V_GA + 1], vec[:, V_BE:V_BE + 1], ALU.mult, ALU.add).then_inc(v_nt1, 1)
                if k is not None:
                    eng.wait_ge(g_ml, k + 1)
                    eng.wait_ge(g_cw, k + 1)
                    if k >= 2:
                        eng.wait_ge(a_da, DS * (k - 1))
                    eng.tensor_tensor(DL[:, k % 2, :], sp[:, SP_M, :], sp[:, SP_C, :], ALU.subtract).then_inc(v_dl, 1)
                if k is not None:
                    eng.wait_ge(v_dl, k + 1)
                    if k:
                        eng.wait_ge(v_b, DS * k)
                    eng.tensor_tensor(DU[:, :], DL[:, k % 2, :], US[:, k, :], ALU.mult).then_inc(v_du, 1)
                if c is not None:
                    times_c(DS - 1)

            for i in SSM_STEPS:
                dve_ssm(i)

            eng.wait_ge(c_["wout"], J)
            gn_stats(2)
            eng.wait_ge(t_zz, 2)
            gn_apply(2, lambda j: XR[:, 0, :, j, 0:W])
            eng.wait_ge(s_xn, 3 * J)
            for j in range(J):
                ins = eng.tensor_copy(XR[:, 1, :, j, 0:H].rearrange("p c k -> p k c"), XR[:, 0, :, j, 0:W])
            ins.then_inc(t_xr, 1)
            for n in range(14):
                eng.wait_ge(t_pr, n + 1)
                if n >= 2:
                    eng.wait_ge(t_pp, n - 1)
                eng.tensor_tensor(p1[:, n % 2].rearrange("p (m c) -> p m c", m=16), banks[n % 2][:, :].rearrange("p (m c) -> p m c", m=16),
                                  bcast(BAB[:, n // 7, :], 1, 16), ALU.add).then_inc(t_p1, 1)
            for s in range(G + 1):
                if s < G:
                    g = s
                    eng.wait_ge(t_z, g + 1)
                    take_z(eng, g, (0, 1)).then_inc(t_zc, 1)
                    eng.wait_ge(t_zc, g + 1)
                    eng.wait_ge(t_za, g + 1)
                    zg = Zc[:, :, C2 * g:C2 * g + C2]
                    link(eng.tensor_reduce(zst[:, 0, g, :], zg, AX.X, ALU.add))
                    link(eng.tensor_scalar(zst[:, 0, g, :], zst[:, 0, g, :], 1.0 / C2, None, ALU.mult))
                    eng.tensor_tensor(zg, zg, bcast(zst[:, 0, g, :], 2, C2), ALU.subtract).then_inc(t_c, 1)
                if s:
                    g = s - 1
                    eng.wait_ge(t_q, g + 1)
                    eng.tensor_reduce(zst[:, 1, g, :], Zq[:, g % 2].rearrange("p (j c) -> p j c", c=C2), AX.X, ALU.add).then_inc(t_v, 1)
            eng.wait_ge(t_r2, 1)
            eng.wait_ge(t_c, G)
            for q in range(4):
                cols = slice(8 * q, min(8 * q + 8, H))
                zq = Zc[:, cols, :].rearrange("p j (g c) -> p j g c", g=G)
                eng.tensor_tensor(zq, zq, bcast(zst[:, 3, :, cols].rearrange("p g j -> p j g"), 3, C2), ALU.mult).then_inc(t_n, 1)
            eng.wait_ge(t_gd, 8)
            for n in range(8):
                q, par = n % 4, n // 4
                w = min(4, 14 - 4 * q)
                eng.wait_ge(t_o, n + 1)
                src = banks[6 + n % 2][:, 0:P * w].rearrange("p (j b i) -> p j b i", j=w, b=J)[:, :, :, 0:H]
                Yv, Gv = [m[:, :, :].rearrange("p b (i j e) -> p e b i j", i=H, e=2)[:, par] for m in (Y, Gt)]
                for jj in range(w):
                    ins = eng.scalar_tensor_tensor(Yv[:, :, :, 4 * q + jj], src[:, jj], vec[:, V_BZF:V_BZF + 1],
                                                   Gv[:, :, :, 4 * q + jj], ALU.add, ALU.mult)
                ins.then_inc(t_y, 1)
            eng.wait_ge(t_y, 8)
            eng.tensor_tensor(X[:, :], X[:, :], flat(Y), ALU.add).then_inc(t_x3, 1)
            eng.wait_ge(t_x3, 1)

            gn_stats(3)
            gn_apply(3, lambda j: XN[:, T * j:T * j + T])
            eng.memset(hst[:, :, :], 0.0)
            eng.memset(cst[:, :, :], 0.0).then_inc(r_in, 1)
            eng.wait_ge(r_in, 1)
            Rv = Rt[:, :, :].rearrange("p (g m) c -> p m g c", g=G)
            for q in range(7):
                eng.wait_ge(r_t, q + 1)
                eng.tensor_copy(Rv[:, 4 * q:4 * q + 4], banks[2 + q % 2][0:112, :].rearrange("p (m g c) -> p m g c", m=4, g=G)).then_inc(r_te, 1)
            eng.wait_ge(r_te, 7)

            def dve_step(t, par, m):
                g = gates[:, par]
                eng.wait_ge(r_g, t + 1)
                eng.scalar_tensor_tensor(t1[:, :], g[:, 1, :], 1.0, cst[:, par, :], ALU.add, ALU.mult).then_inc(r_1, 1)
                eng.scalar_tensor_tensor(t2[:, :], g[:, 0, :], 1.0, g[:, 3, :], ALU.add, ALU.mult).then_inc(r_1, 1)
                eng.wait_ge(r_1, 2 * t + 2)
                eng.scalar_tensor_tensor(cst[:, 1 - par, :], t1[:, :], 0.5, t2[:, :], ALU.mult, ALU.add).then_inc(r_c, 1)
                eng.wait_ge(r_th, t + 1)
                eng.scalar_tensor_tensor(hst[:, par, :], g[:, 2, :], 1.0, tcn[:, :], ALU.add, ALU.mult).then_inc(r_h, 1)
                eng.wait_ge(r_t, 7 + t + 1)
                if not isinstance(t, int) or t >= 2:
                    eng.wait_ge(s_out[par], m * 16)
                eng.scalar_tensor_tensor(Os[:, par].rearrange("p g c -> p (g c)"), banks[4 + par][0:112, 0:P], 0.5,
                                         Rt[:, bass.ds(t * 4, 4), :].rearrange("p g c -> p (g c)"), ALU.mult, ALU.add).then_inc(r_o, 1)

            dve_step(0, 0, 0)
            dve_step(1, 1, 0)
            with eng.Fori(1, H // 2) as it:
                dve_step(it * 2, 0, it)
                dve_step(it * 2 + 1, 1, it)


_INS = ['x', 'L0_conv_w_qkv', 'L0_conv_b_qkv', 'L0_conv_w_proj', 'L0_conv_b_proj', 'L1_conv_w1', 'L1_conv_dw',
        'L1_conv_in_proj_w', 'L1_conv_conv1d_w', 'L1_conv_conv1d_b', 'L1_conv_x_proj_w', 'L1_conv_dt_proj_w',
        'L1_conv_dt_proj_b', 'L1_conv_A_log', 'L1_conv_D_param', 'L1_conv_out_proj_w', 'L1_conv_gamma', 'L1_conv_beta',
        'L1_conv_w2', 'L1_conv_wout', 'L2_conv_Wa1', 'L2_conv_ba1', 'L2_conv_Wa2', 'L2_conv_ba2', 'L2_conv_Wb1',
        'L2_conv_bb1', 'L2_conv_Wb2', 'L2_conv_bb2', 'L2_conv_ln2_g', 'L2_conv_ln2_b', 'L2_conv_Wg', 'L2_conv_bg',
        'L2_conv_Wz', 'L2_conv_bz', 'L3_conv_Wix', 'L3_conv_Wim', 'L3_conv_Wfx', 'L3_conv_Wfm', 'L3_conv_Wcx',
        'L3_conv_Wcm', 'L3_conv_Wox', 'L3_conv_Wom', 'L3_conv_bi', 'L3_conv_bf', 'L3_conv_bc', 'L3_conv_bo']


def kernel(**inputs):
    import concourse.bacc as _bacc
    from concourse.bass_utils import run_bass_kernel_spmd as _run

    nc = _bacc.Bacc("TRN2", target_bir_lowering=False, num_devices=1)
    arrays, aps = {}, {}
    for name in _INS:
        v = np.ascontiguousarray(inputs[name])
        arrays[f"in_{name}"] = v
        aps[name] = nc.dram_tensor(f"in_{name}", v.shape, mybir.dt.from_np(v.dtype), kind="ExternalInput").ap()
    out = nc.dram_tensor("out", (B, H, W, C), F32, kind="ExternalOutput").ap()
    build(nc, aps, out)
    r = _run(nc, [arrays], core_ids=[0])
    return r.results[0]["out"]
```

```python
import numpy as np

import concourse.bass as bass
from concourse import mybir
from contextlib import ExitStack

F32 = mybir.dt.float32
BF16 = mybir.dt.bfloat16
ALU = mybir.AluOpType
ACT = mybir.ActivationFunctionType
AX = mybir.AxisListType

P = 128
B, H, W, C = 16, 28, 28, 32
G = P // C
J = B // G
T = H * W
N = J * T
SP = 7
LP = T // SP
WS = 7
WT = WS * WS
WP = 64
NH, HD = 4, 8
NW = W // WS
ST = WS * W
NS = N // ST
R, DS = 8, 8
C2 = 16
HT = T // 2
EPS = 1e-5
SCALE = HD ** -0.5

(U_Q, U_K, U_V, U_P, U_A, U_B, U_G, U_X, U_M) = (0, 1, 2, 3, 4, 5, 6, 7, 11)
(U_Z, U_X2, U_WO, U_OUT, U_U, U_CV, U_DL, NU) = (15, 16, 17, 18, 19, 22, 31, 32)


def build(nc, a, out):
    ctx = ExitStack()
    with ctx:
        def sb(name, shape, stack=ctx, dtype=F32):
            return stack.enter_context(nc.sbuf_tensor(name, shape, dtype))

        def sem(name):
            return ctx.enter_context(nc.semaphore(name))

        X = sb("X", [P, N])
        XN = sb("XN", [P, J * 30 * 30])
        BD = sb("BD", [P, NU, P])
        WBC = sb("WBC", [P, 2, 3 * C])
        sel = sb("sel", [3 * C, DS, P], ctx, BF16)
        ident = sb("ident", [P, P])
        bd = sb("bd", [P, G])
        m16 = sb("m16", [P, 16])
        mask8 = sb("mask8", [P, NH])
        m8 = sb("m8", [P, 8])
        maskz = sb("maskz", [P, G])
        WZ = sb("WZ", [P, 2, P])
        VB = sb("VB", [P, P])
        BL = sb("BL", [3, G, C])
        half3 = sb("half3", [3, 1])
        BAB = sb("BAB", [P, 2, C])
        epsc = sb("epsc", [P, 1])
        vec = sb("vec", [P, 16])
        (V_BQ, V_BK, V_BV, V_BP, V_CB, V_DTB, V_D, V_GA, V_BE, V_BG, V_BZ, V_LG, V_BQS, V_BZF, V_BO) = range(15)
        lnb = sb("lnb", [C2, 1])
        Aneg = sb("Aneg", [P, DS])
        W4 = sb("W4", [P, NU, C])
        wzraw = sb("wzraw", [P, C])
        wzs = sb("wzs", [P, C])
        stats = sb("stats", [P, J, 2, 6])
        mv = sb("mv", [P, J, 2])
        lnv = sb("lnv", [P, J])
        rstd = sb("rstd", [P, J])

        pairs = [ctx.enter_context(nc.psum_tensor(f"pair{i}", [P, 2, 512], F32)) for i in range(4)]
        banks = [pairs[i // 2][:, i % 2, :] for i in range(8)]
        TRB = 5

        setup = ExitStack()
        NB = sb("NB", [P, 18, C], setup)
        TB = sb("TB", [P, 18, C], setup)
        W8 = sb("W8", [P, 3, 8], setup)
        W8X = sb("W8X", [P, C], setup)
        DW = sb("DW", [P, 9], setup)
        C1 = sb("C1", [P, 3], setup)
        AL = sb("AL", [P, DS], setup)
        AE = sb("AE", [P, DS], setup)
        WIN = sb("WIN", [P, 1, C], setup)
        wzn = sb("wzn", [C2, C], setup)
        omean = sb("omean", [P, 1], setup)
        raw = ExitStack()
        XT = sb("XT", [P, J, G, SP, C], raw)
        XS = sb("XS", [P, J, SP, G, C], raw)
        raw.close()

        att = ExitStack()
        xw = sb("xw", [P, 2, NW, 2, WP], att)
        Qw = sb("Qw", [P, 2, NW, WP], att)
        Ks = sb("Ks", [P, 2, NW, WT], att)
        Km = sb("Km", [P, 2, NW, NH, WT], att)
        Vst = sb("Vst", [P, 2, NW, G, 2, C], att)
        Ts = sb("Ts", [P, G, 8, WT], att)
        Pr = sb("Pr", [P, 2, G, 8, WP], att)
        PT = sb("PT", [P, 2, 2, 2, P], att)
        AO = sb("AO", [P, 2, ST], att)
        mx = sb("mx", [P, G, 8], att)
        sm = sb("sm", [P, G, 8], att)
        rc = sb("rc", [P, G, 8], att)
        att.close()
        setup.close()

        ssm = ExitStack()
        NA = 4
        S1 = sb("S1", [P, T + 2], ssm)
        DL = sb("DL", [P, 2, T], ssm)
        BCf = sb("BCf", [3 * C, 2, 2, T], ssm)
        dA = sb("dA", [P, NA, T], ssm)
        dBu = sb("dBu", [P, 2, T], ssm)
        Hs = sb("Hs", [P, 2, T], ssm)
        NHC = 4
        hC = sb("hC", [P, NHC, T], ssm)
        (SP_E, SP_U, SP_L, SP_W, SP_C, SP_M) = range(6)
        sp = sb("sp", [P, 6, T], ssm)
        US = sb("US", [P, J, T], ssm)
        ZS = sb("ZS", [P, J, T], ssm)
        X2 = sb("X2", [P, J, T], ssm)
        YA = sb("YA", [P, 2, T], ssm)
        DU = sb("DU", [P, T], ssm)
        y1 = sb("y1", [P, T], ssm)
        y2 = sb("y2", [P, T], ssm)
        cS = sb("cS", [P, T], ssm)
        sq = sb("sq", [P, T], ssm)
        lv = sb("lv", [P, T], ssm)
        rs = sb("rs", [P, T], ssm)
        nt = sb("nt", [P, 3, T], ssm)
        ssm.close()

        tri = ExitStack()
        XR = sb("XR", [P, 2, H, J, 32], tri)
        Zc = sb("Zc", [P, H, 64], tri)
        Ab = sb("Ab", [P, 2, 64, H], tri)
        p1 = sb("p1", [P, 4, 512], tri)
        pp = sb("pp", [P, 4, 256], tri)
        Zq = sb("Zq", [P, 2, 448], tri)
        zst = sb("zst", [P, 4, G, H], tri)
        ZT = sb("ZT", [P, 14 * P], tri)
        Gt = sb("Gt", [P, J, T], tri)
        Y = sb("Y", [P, J, T], tri)
        tri.close()

        rec = ExitStack()
        Rt = sb("Rt", [112, 112, C], rec)
        gates = sb("gates", [P, 2, 5, 112], rec)
        hst = sb("hst", [P, 2, 112], rec)
        prods = sb("prods", [P, 2, 112], rec)
        tcn = sb("tcn", [P, 112], rec)
        Os = sb("Os", [112, 2, G, C], rec)
        rec.close()

        s_x = [sem(f"s_x{j}") for j in range(J)]
        s_xs = [sem(f"s_xs{j}") for j in range(J)]
        s_w = [sem(f"s_w{k}") for k in range(3)]
        s_wp = sem("s_wp")
        s_z0 = sem("s_z0")
        s_mk = sem("s_mk")
        s_mk2 = sem("s_mk2")
        s_v = sem("s_v")
        s_a = sem("s_a")
        s_tr = sem("s_tr")
        s_ev = sem("s_ev")
        s_hf = sem("s_hf")
        s_bd = sem("s_bd")
        s_ae = sem("s_ae")
        s_wd = sem("s_wd")
        s_mv = sem("s_mv")
        s_rs = sem("s_rs")
        s_xn = sem("s_xn")

        def sems(names):
            return [sem(n) for n in names.split()]

        qk_d, v_r, s_r, t_r, av_r, pj_r, q_r, k_r, exp_r, ring_r = sems("qk_d v_r s_r t_r av_r pj_r q_r k_r exp_r ring_r")
        xw_r, km_r, pn_r, max_r, sub_r, sum_r, rec_r, ao_r, x1_r = sems("xw_r km_r pn_r max_r sub_r sum_r rec_r ao_r x1_r")
        PRODUCTS = "conv x2 u z delta xB xC out var wout".split()
        p_ = {n: sem("p_" + n) for n in PRODUCTS + ["B", "C"]}
        c_ = {n: sem("c_" + n) for n in PRODUCTS}
        a_e, a_u, a_l, a_w, a_da, a_rs = sems("a_e a_u a_l a_w a_da a_rs")
        v_b, v_s, v_c, v_cc, v_dl, v_du, v_y1, v_y2, v_nt1 = sems("v_b v_s v_c v_cc v_dl v_du v_y1 v_y2 v_nt1")
        g_ya, g_ml, g_cw, g_mid, g_low, g_nt0, g_nt2, s1z = sems("g_ya g_ml g_cw g_mid g_low g_nt0 g_nt2 s1z")
        t_pr, t_g, t_z, t_t, t_o, t_sg, t_gd, t_za, t_q, t_r1, t_r2 = sems("t_pr t_g t_z t_t t_o t_sg t_gd t_za t_q t_r1 t_r2")
        t_te, t_xr, t_p1, t_zc, t_c, t_v, t_n, t_y, t_x3, t_pp, t_zz = sems("t_te t_xr t_p1 t_zc t_c t_v t_n t_y t_x3 t_pp t_zz")
        r_z, r_zo, r_t, r_x, r_g, r_go, r_th = sems("r_z r_zo r_t r_x r_g r_go r_th")
        r_in, r_1, r_c, r_h, r_te, r_o = sems("r_in r_1 r_c r_h r_te r_o")
        s_out = [sem("s_out0"), sem("s_out1")]

        block = ctx.enter_context(nc.Block())

        def strip(s):
            return bass.ds(s * ST, ST)

        def windows(ap):
            return ap.rearrange("p (r w c) -> p w r c", r=WS, w=NW)

        def bcast(ap, axis, n):
            ap = ap.unsqueeze(axis)
            shape = list(ap.shape)
            shape[axis] = n
            return ap.broadcast_to(shape)

        def flat(buf):
            return buf[:, :, :].rearrange("p b t -> p (b t)")

        def evac_in(eng, q):
            n, stop = 4 * q, 4 * q + 4
            while n < stop:
                j, s = divmod(n, SP)
                m = min(stop - n, SP - s)
                src = banks[q][:, LP * (n % 4):LP * (n % 4 + m)].rearrange("p (s t) -> p s t", s=m)
                dst = X[:, T * j:T * j + T].rearrange("p (t s) -> p s t", s=SP)[:, s:s + m]
                ins = (eng.activation(dst, src, ACT.Copy) if eng is nc.scalar else eng.tensor_copy(dst, src))
                n += m
            ins.then_inc(s_ev, 1)

        def halves(ap):
            return ap.rearrange("p (h t) -> p h t", h=2)

        PAIR = dict(B=0, C=1, conv=2, u=2, delta=2, xC=2, xB=3, wout=3, out=3, var=3, z=3, x2=3)

        def result(name):
            return pairs[PAIR[name]][:, :, 0:HT]

        FACTORS = (0, 1, 4, 5)
        LAST = (6, 7, 2, 3)

        def take_z(eng, g, columns):
            first = 4 - 4 * (g % 2)
            for b in columns:
                dst = Zc[32 * b:32 * b + H, :, C2 * g:C2 * g + C2].rearrange("p j c -> p c j")
                src = banks[first + b][32 * b:32 * b + H, 0:448].rearrange("p (c j) -> p c j", c=C2)
                ins = eng.activation(dst, src, ACT.Copy) if eng is nc.scalar else eng.tensor_copy(dst, src)
            return ins

        def parts(i):
            return [b if 0 <= b < J else None for b in (i + 2, i + 1, i, i - 1, i - 2)]

        def upper(ap):
            return ap.bitcast(BF16).rearrange("p (t two) -> p t two", two=2)[:, :, 1]

        SSM_STEPS = range(-2, J + 2)

        def rep(dram, off, rows, cols, stride):
            return bass.AP(dram.tensor, off, [[0, G], [stride, rows], [1, cols]])

        loads = {}

        def load(eng, dst, src, stage=1):
            s = s_wp if eng is nc.gpsimd else s_w[stage]
            eng.dma_start(dst, src).then_inc(s, 16)
            loads[s.name] = loads.get(s.name, 0) + 1

        def col(eng, k, name, off=0, stage=1):
            load(eng, vec[:, k:k + 1], bass.AP(a[name].tensor, off, [[0, G], [1, C], [1, 1]]), stage)

        def loaded(eng, stage):
            for s in (s_w[stage], s_wp)[0:2 - min(stage, 1)]:
                eng.wait_ge(s, 16 * loads[s.name])

        @block.sync
        def _(eng):
            xv = a["x"].rearrange("b h w c -> b (h w c)").rearrange("(g j) (p s c) -> j p g (s c)", g=G, p=LP, c=C)
            for j in range(J):
                eng.dma_start(XT[0:LP, j].rearrange("p g s c -> p g (s c)"), xv[j]).then_inc(s_x[j], 16)
            eng.wait_ge(s_z0, 1)

            load(eng, W4[:, U_Q:U_V + 1, :].rearrange("p u c -> p (u c)"), rep(a["L0_conv_w_qkv"], 0, C, 3 * C, 3 * C), 0)
            load(eng, W4[:, U_P, :], rep(a["L0_conv_w_proj"], 0, C, C, C), 0)
            load(eng, NB[:, 0, :], rep(a["L1_conv_in_proj_w"], C * C, C, C, C))
            load(eng, WIN[:, 0, :], rep(a["L1_conv_in_proj_w"], 0, C, C, C))
            load(eng, NB[:, 3, :], rep(a["L1_conv_out_proj_w"], 0, C, C, C))
            load(eng, NB[:, 16, 0:R], rep(a["L1_conv_dt_proj_w"], 0, C, R, R))
            for g in range(G):
                load(eng, NB[C * g:C * g + R + 2 * DS, 17, :], a["L1_conv_x_proj_w"])
            for k, m in enumerate(("w1", "w2", "wout")):
                load(eng, W8[:, k, :], rep(a["L1_conv_" + m], 0, C, 8, 8))
            load(eng, AL[:, :], rep(a["L1_conv_A_log"], 0, C, DS, DS))
            load(eng, C1[:, :], rep(a["L1_conv_conv1d_w"], 0, C, 3, 3))
            load(eng, wzn[:, :], a["L2_conv_Wz"])
            with nc.allow_non_contiguous_dma(reason="small per-channel vectors"):
                for k, m in ((V_CB, "conv1d_b"), (V_DTB, "dt_proj_b"), (V_D, "D_param"), (V_GA, "gamma"), (V_BE, "beta")):
                    col(eng, k, "L1_conv_" + m)
                col(eng, V_BZ, "L2_conv_bz")
                load(eng, lnb[:, :], bass.AP(a["L2_conv_ln2_b"].tensor, 0, [[1, C2], [1, 1]]))
                for g in range(G):
                    load(eng, DW[C * g:C * g + C, :], bass.AP(a["L1_conv_dw"].tensor, 0, [[1, C], [C, 9]]))

            def w4(u, name, cols=C, stride=C, c0=0):
                load(eng, W4[:, u, c0:c0 + cols], rep(a[name], 0, C, cols, stride), 2)
            for u, m in ((U_A, "a"), (U_B, "b")):
                for t in range(2):
                    w4(u, f"L2_conv_W{m}{t + 1}", cols=C2, stride=C2, c0=C2 * t)
            w4(U_G, "L2_conv_Wg")
            for k, m in enumerate("oifc"):
                w4(U_X + k, f"L3_conv_W{m}x")
                w4(U_M + k, f"L3_conv_W{m}m")
            load(eng, wzraw[:, :], bass.AP(a["L2_conv_Wz"].tensor, 0, [[0, 8], [C, C2], [1, C]]), 2)

            with nc.allow_non_contiguous_dma(reason="small per-channel vectors"):
                col(eng, V_BG, "L2_conv_bg", stage=2)
                col(eng, V_BO, "L3_conv_bo", stage=2)
                load(eng, vec[:, V_LG:V_LG + 1], bass.AP(a["L2_conv_ln2_g"].tensor, 0, [[0, 8], [1, C2], [1, 1]]), 2)
            for k, m in enumerate(("ba1", "ba2", "bb1", "bb2")):
                load(eng, BAB[:, k // 2, C2 * (k % 2):C2 * (k % 2) + C2], bass.AP(a["L2_conv_" + m].tensor, 0, [[0, P], [1, C2]]), 2)
            for k, m in enumerate("ifc"):
                load(eng, BL[k:k + 1, :, :], bass.AP(a["L3_conv_b" + m].tensor, 0, [[0, 1], [0, G], [1, C]]), 2)


            ov = out.rearrange("b h w c -> (b h w c)").rearrange("(r p c) -> p r c", p=112, c=C)

            def store(t, par):
                eng.wait_ge(r_o, t + 1)
                eng.dma_start(ov[:, bass.ds(t * 4, 4), :], Os[:, par]).then_inc(s_out[par], 16)
            with eng.Fori(0, H // 2) as it:
                store(it * 2, 0)
                store(it * 2 + 1, 1)
            for p_ in range(2):
                eng.wait_ge(s_out[p_], 16 * (H // 2))

        @block.gpsimd
        def _(eng):
            eng.memset(NB[:, 16:18, :], 0.0).then_inc(s_z0, 1)
            eng.memset(ident[:, :], 0.0).then_inc(s_mk, 1)
            for m in (bd, m16, m8):
                eng.memset(m[:, :], 1.0).then_inc(s_mk, 1)
            eng.wait_ge(s_mk, 4)
            eng.affine_select(out=ident[:, :], in_=ident[:, :], compare_op=ALU.not_equal, fill=1.0,
                              base=0, pattern=[[-1, P]], channel_multiplier=1).then_inc(s_mk, 1)
            for m, w, n in ((bd, 32, G), (m16, 8, 16), (m8, 16, 8)):
                eng.affine_select(out=m[:, :], in_=m[:, :], compare_op=ALU.is_ge, fill=0.0,
                                  base=0, pattern=[[-w, n]], channel_multiplier=1).then_inc(s_mk, 1)
            eng.memset(half3[:, :], 0.5).then_inc(s_hf, 1)
            eng.wait_ge(s_hf, 1)
            eng.affine_select(out=half3[:, :], in_=half3[:, :], compare_op=ALU.not_equal, fill=1.0,
                              base=-2, pattern=[[0, 1]], channel_multiplier=1).then_inc(s_hf, 1)
            eng.wait_ge(s_mk, 8)
            for m, w, n in ((bd, 32, G), (m16, 8, 16), (m8, 16, 8)):
                eng.affine_select(out=m[:, :], in_=m[:, :], compare_op=ALU.is_ge, fill=0.0,
                                  base=w - 1, pattern=[[w, n]], channel_multiplier=-1).then_inc(s_mk, 1)
            with nc.allow_non_contiguous_dma(reason="small per-channel vectors"):
                for k in range(3):
                    col(eng, V_BQ + k, "L0_conv_b_qkv", C * k, stage=0)
                col(eng, V_BP, "L0_conv_b_proj", stage=0)
            eng.wait_ge(s_ev, 8)
            for m in (xw, Qw, Vst, Pr):
                eng.memset(m[:], 0.0).then_inc(s_mk2, 1)
            eng.wait_ge(s_mk2, 1)

            def pool_att(s, par):
                nxt = not isinstance(s, int) or s + 1 < NS
                cur = not isinstance(s, int) or s >= 0
                np_ = 1 - par
                if nxt:
                    if isinstance(s, int) and s < 0:
                        eng.wait_ge(s_xn, J)
                    if not isinstance(s, int) or s >= 1:
                        eng.wait_ge(v_r, s)
                    for u in range(2):
                        ins = eng.tensor_copy(xw[:, np_, :, u, 0:WT].rearrange("p w (r c) -> p w r c", r=WS),
                                              windows(XN[:, strip(s + 1)]))
                    ins.then_inc(xw_r, 1)
                    eng.wait_ge(k_r, s + 2)
                    if not isinstance(s, int) or s >= 1:
                        eng.wait_ge(s_r, 2 * s)
                    eng.tensor_tensor(Km[:, np_], bcast(Ks[:, np_], 2, NH), bcast(bcast(mask8[:, :], 1, NW), 3, WT),
                                      ALU.mult).then_inc(km_r, 1)
                if cur:
                    for g in range(G):
                        eng.wait_ge(rec_r, 4 * s + g + 1)
                        pg = Pr[:, par, g, :, 0:WT]
                        eng.tensor_tensor(pg, pg, bcast(rc[:, g, :], 2, WT), ALU.mult).then_inc(pn_r, 1)

            for s in (-1, 0, 1, 2):
                pool_att(s, s % 2)
            with eng.Fori(0, 6) as it:
                pool_att(it * 2 + 3, 1)
                pool_att(it * 2 + 4, 0)
            pool_att(15, 1)
            eng.wait_ge(v_r, NS)
            eng.memset(XN[:, :], 0.0).then_inc(s_bd, 1)

            eng.wait_ge(x1_r, NS)
            eng.memset(S1[:, 0:2], 0.0).then_inc(s1z, 1)

            def pool_ssm(i):
                f, k, c, m, w = parts(i)

                def add(n):
                    if c is None:
                        return
                    eng.wait_ge(v_c, DS * c + n + 1)
                    if n > 1:
                        eng.wait_ge(g_ya, (DS - 1) * c + n - 1)
                    y = YA[:, c % 2, :]
                    eng.tensor_tensor(y, y, hC[:, n % NHC, :], ALU.add).then_inc(g_ya, 1)

                def split(s, name):
                    if k is None:
                        return
                    eng.wait_ge(c_[name], k + 1)
                    two, one = BCf[0:2 * C, k % 2, s, :], BCf[0:C, k % 2, s, :]
                    eng.tensor_tensor(two, two, upper(two), ALU.subtract).then_inc(g_mid, 1)
                    eng.wait_ge(g_mid, 2 * k + s + 1)
                    eng.tensor_tensor(one, one, upper(one), ALU.subtract).then_inc(g_low, 1)

                if w is not None and w < J - 1:
                    eng.wait_ge(v_nt1, w + 1)
                    if w:
                        eng.wait_ge(p_["wout"], w)
                    eng.tensor_tensor(nt[:, 2, :], nt[:, 1, :], X2[:, w, :], ALU.mult).then_inc(g_nt2, 1)
                if i == J:
                    eng.wait_ge(v_c, DS * J)
                    for buf in (Zc, XR):
                        eng.memset(buf[:], 0.0).then_inc(t_zz, 1)
                split(0, "xB")
                add(1)
                split(1, "xC")
                add(2)
                add(3)
                add(4)
                if k is not None:
                    eng.wait_ge(a_l, k + 1)
                    mk = sp[:, SP_M, :]
                    eng.tensor_tensor(mk, mk, sp[:, SP_L, :], ALU.add).then_inc(g_ml, 1)
                add(5)
                if k is not None:
                    eng.wait_ge(a_w, k + 1)
                    eng.wait_ge(v_cc, k + 1)
                    eng.tensor_tensor(sp[:, SP_C, :], sp[:, SP_C, :], sp[:, SP_W, :], ALU.mult).then_inc(g_cw, 1)
                if m is not None and m < J - 1:
                    eng.wait_ge(a_rs, m + 1)
                    if m:
                        eng.wait_ge(v_nt1, m)
                    eng.tensor_tensor(nt[:, 0, :], cS[:, :], rs[:, :], ALU.mult).then_inc(g_nt0, 1)
                add(6)
                add(7)

            for i in SSM_STEPS:
                pool_ssm(i)

            for n in range(14):
                eng.wait_ge(t_p1, n + 1)
                if n >= 4:
                    eng.wait_ge(t_sg, n - 3)
                fac = p1[:, n % 4].rearrange("p (m t c) -> p m t c", m=16, t=2)
                eng.tensor_tensor(pp[:, n % 4].rearrange("p (m c) -> p m c", m=16), fac[:, :, 0, :], fac[:, :, 1, :],
                                  ALU.mult).then_inc(t_pp, 1)

        @block.scalar
        def _(eng):
            chain = [0]

            def link(ins):
                chain[0] += 1
                ins.then_inc(s_a, 1)
                eng.wait_ge(s_a, chain[0])

            for j in range(1, J, 2):
                eng.wait_ge(s_x[j], 16)
                eng.activation(XS[0:LP, j].rearrange("p s g c -> p g s c"), XT[0:LP, j], ACT.Copy).then_inc(s_xs[j], 1)
            for q in range(1, 7, 2):
                eng.wait_ge(s_tr, q + 1)
                evac_in(eng, q)
            def gn(layer):
                eng.wait_ge(s_mv, layer + 1)
                if layer:
                    eng.wait_ge(s_xn, J * layer)
                link(eng.activation(lnv[:, :], mv[:, :, 1], ACT.Ln, bias=epsc[:, 0:1]))
                eng.activation(rstd[:, :], lnv[:, :], ACT.Exp, scale=-0.5).then_inc(s_rs, 1)

            gn(0)

            loaded(eng, 0)
            eng.wait_ge(s_mk2, 2)

            def act_att(s, par):
                fixed = isinstance(s, int)
                nxt = not fixed or s + 1 < NS
                cur = not fixed or 0 <= s < NS
                prv = not fixed or 1 <= s <= NS
                np_ = 1 - par
                if nxt:
                    eng.wait_ge(qk_d, s + 2)
                    if not fixed or s >= 1:
                        eng.wait_ge(s_r, 2 * s)
                    eng.activation(Qw[:, np_, :, 0:WT].rearrange("p w (r c) -> p w r c", r=WS),
                                   windows(banks[4][:, 0:ST]), ACT.Identity,
                                   bias=vec[:, V_BQS:V_BQS + 1], scale=SCALE).then_inc(q_r, 1)
                    if not fixed or s >= 1:
                        eng.wait_ge(km_r, s)
                    eng.activation(Ks[:, np_].rearrange("p w (r c) -> p w r c", r=WS),
                                   windows(banks[4][:, ST:2 * ST]), ACT.Identity,
                                   bias=vec[:, V_BK:V_BK + 1]).then_inc(k_r, 1)
                for g in range(G):
                    if prv:
                        eng.wait_ge(t_r, 4 * (s - 1) + g + 1)
                        if not fixed or 4 * (s - 1) + g >= 2:
                            eng.wait_ge(av_r, 4 * (s - 1) + g - 1)
                        eng.activation(PT[:, g % 2].rearrange("p a b q -> p (a b q)"),
                                       banks[5 + (par + 1 + g) % 2][:, :], ACT.Copy).then_inc(ring_r, 1)
                    if cur:
                        eng.wait_ge(sub_r, 4 * s + g + 1)
                        if not fixed or s >= 2:
                            eng.wait_ge(t_r, 4 * (s - 2) + g + 1)
                        eng.activation(Pr[:, par, g, :, 0:WT], Ts[:, g, :, :], ACT.Exp).then_inc(exp_r, 1)
                if nxt:
                    eng.wait_ge(v_r, s + 2)
                    if not fixed or s >= 1:
                        eng.wait_ge(av_r, 4 * s)
                    if fixed and s < 0:
                        eng.wait_ge(s_mk2, 3)
                    vb = banks[5 + (par + 1) % 2]
                    for u in range(2):
                        src = vb[64 * u:64 * u + 64, :].rearrange("p (m e q d) -> p m e q d", m=16, e=2, q=2)[:, :, :, u, :]
                        dst = Vst[64 * u:64 * u + 64, np_].rearrange("p w g e n -> p (w g) (e n)")
                        dst = bass.AP(dst.tensor, dst.offset + HD * u, [list(dst.ap[0]), [64, 16], [48, 2], [1, HD]])
                        eng.activation(dst, src, ACT.Copy).then_inc(ring_r, 1)

            act_att(-1, 1)
            eng.wait_ge(s_mk2, 4)
            loaded(eng, 1)
            eng.activation(AE[:, :], AL[:, :], ACT.Exp).then_inc(s_ae, 1)
            for s in (0, 1, 2):
                act_att(s, s % 2)
            with eng.Fori(0, 6) as it:
                act_att(it * 2 + 3, 1)
                act_att(it * 2 + 4, 0)
            act_att(15, 1)
            act_att(16, 0)

            gn(1)

            eng.wait_ge(s1z, 1)

            def act_ssm(i):
                f, k, c, m, w = parts(i)
                q = None if k is None else k % 2

                def decays(*states):
                    if c is None:
                        return
                    for n in states:
                        if DS * c + n >= NA:
                            eng.wait_ge(v_s, DS * c + n - NA + 1)
                        eng.activation(dA[:, n % NA, :], DL[:, c % 2, :], ACT.Exp, scale=Aneg[:, n:n + 1]).then_inc(a_da, 1)

                if c is not None:
                    eng.wait_ge(v_dl, c + 1)
                decays(0, 1)
                if k is not None:
                    eng.wait_ge(p_["delta"], k + 1)
                    if k:
                        eng.wait_ge(v_dl, k)
                    eng.activation(halves(sp[:, SP_E, :]), result("delta"), ACT.Abs, bias=vec[:, V_DTB:V_DTB + 1])
                    eng.activation(halves(sp[:, SP_M, :]), result("delta"), ACT.Relu, bias=vec[:, V_DTB:V_DTB + 1]).then_inc(c_["delta"], 1)
                    for s, name in enumerate(("xB", "xC")):
                        eng.wait_ge(p_[name], k + 1)
                        if k >= 2:
                            eng.wait_ge(p_["BC"[s]], DS * (k - 1))
                        eng.activation(halves(BCf[:, q, s, :]), result(name)[0:3 * C], ACT.Copy).then_inc(c_[name], 1)
                if k is not None:
                    eng.wait_ge(c_["delta"], k + 1)
                    eng.activation(sp[:, SP_E, :], sp[:, SP_E, :], ACT.Exp, scale=-1.0).then_inc(a_e, 1)
                decays(2, 3)
                if k is not None:
                    eng.wait_ge(a_e, k + 1)
                    eng.activation(sp[:, SP_U, :], sp[:, SP_E, :], ACT.Identity, bias=1.0).then_inc(a_u, 1)
                if m is not None:
                    eng.wait_ge(p_["out"], m + 1)
                    if m:
                        eng.wait_ge(g_nt0, m)
                        eng.wait_ge(p_["var"], m)
                    eng.activation(halves(cS[:, :]), result("out"), ACT.Copy)
                    eng.activation(halves(sq[:, :]), result("out"), ACT.Square).then_inc(c_["out"], 1)
                decays(4, 5)
                if k is not None:
                    eng.wait_ge(a_u, k + 1)
                    eng.activation(sp[:, SP_L, :], sp[:, SP_U, :], ACT.Ln).then_inc(a_l, 1)
                if m is not None:
                    eng.wait_ge(p_["var"], m + 1)
                    eng.activation(halves(lv[:, :]), result("var"), ACT.Ln, bias=epsc[:, 0:1]).then_inc(c_["var"], 1)
                if k is not None:
                    eng.wait_ge(a_l, k + 1)
                    eng.activation(sp[:, SP_W, :], sp[:, SP_L, :], ACT.Exp, scale=-1.0).then_inc(a_w, 1)
                if m is not None:
                    eng.wait_ge(c_["var"], m + 1)
                    eng.activation(rs[:, :], lv[:, :], ACT.Exp, scale=-0.5).then_inc(a_rs, 1)
                decays(6, 7)
                if f is not None:
                    eng.wait_ge(p_["conv"], f + 1)
                    if f:
                        eng.wait_ge(p_["z"], f)
                    eng.activation(halves(S1[:, 2:T + 2]), result("conv"), ACT.Silu).then_inc(c_["conv"], 1)
                    eng.wait_ge(p_["x2"], f + 1)
                    eng.activation(halves(X2[:, f, :]), result("x2"), ACT.Silu).then_inc(c_["x2"], 1)
                    eng.wait_ge(p_["u"], f + 1)
                    eng.activation(halves(US[:, f, :]), result("u"), ACT.Silu, bias=vec[:, V_CB:V_CB + 1]).then_inc(c_["u"], 1)
                    eng.wait_ge(p_["z"], f + 1)
                    eng.activation(halves(ZS[:, f, :]), result("z"), ACT.Silu).then_inc(c_["z"], 1)

            for i in SSM_STEPS:
                act_ssm(i)

            gn(2)

            for j in range(J):
                eng.wait_ge(s_xn, 2 * J + j + 1)
                ins = eng.activation(XR[:, 1, :, j, 0:H].rearrange("p c k -> p k c"), XR[:, 0, :, j, 0:W], ACT.Copy)
            ins.then_inc(t_xr, 1)
            for n in range(14):
                side, q = n // 7, n % 7
                eng.wait_ge(t_pp, n + 1)
                eng.activation(Ab[:, side, :, 4 * q:4 * q + 4].rearrange("p m i -> p i m"),
                               pp[:, n % 4].rearrange("p (i m) -> p i m", i=4), ACT.Sigmoid).then_inc(t_sg, 1)
                if 3 <= n < 11:
                    m = n - 3
                    eng.wait_ge(t_g, m + 1)
                    eng.activation(flat(Gt)[:, m * HT:(m + 1) * HT], banks[2 + m % 2][:, 0:HT], ACT.Sigmoid,
                                   bias=vec[:, V_BG:V_BG + 1]).then_inc(t_gd, 1)
            for g in range(G):
                eng.wait_ge(t_z, g + 1)
                take_z(eng, g, (1, 2, 3)).then_inc(t_za, 1)
                eng.wait_ge(t_c, g + 1)
                if g >= 2:
                    eng.wait_ge(t_v, g - 1)
                eng.activation(Zq[:, g % 2].rearrange("p (j c) -> p j c", c=C2), Zc[:, :, C2 * g:C2 * g + C2],
                               ACT.Square).then_inc(t_q, 1)
            eng.wait_ge(t_v, G)
            eng.activation(zst[:, 2], zst[:, 1], ACT.Ln, bias=epsc[:, 0:1], scale=1.0 / C2).then_inc(t_r1, 1)
            eng.wait_ge(t_r1, 1)
            eng.activation(zst[:, 3], zst[:, 2], ACT.Exp, scale=-0.5).then_inc(t_r2, 1)
            for n in range(4):
                eng.wait_ge(t_t, n + 1)
                m = min(4, 14 - 4 * n) * P
                eng.activation(ZT[:, 512 * n:512 * n + m], banks[4 + n % 2][:, 0:m], ACT.Copy).then_inc(t_te, 1)
            gn(3)

            def act_step(t, par):
                eng.wait_ge(r_z, t + 1)
                if not isinstance(t, int) or t >= 2:
                    eng.wait_ge(r_h, t - 1)
                eng.activation(gates[:, par, 1:4].rearrange("p k n -> p (k n)"), banks[par][:, 0:336], ACT.Tanh).then_inc(r_g, 1)
                eng.wait_ge(r_zo, t + 1)
                eng.activation(gates[:, par, 0, :], banks[6 + par][:, 0:112], ACT.Tanh, bias=vec[:, V_BO:V_BO + 1]).then_inc(r_go, 1)
                eng.wait_ge(r_c, t + 1)
                eng.activation(tcn[:, :], gates[:, 1 - par, 4, :], ACT.Tanh, scale=0.5).then_inc(r_th, 1)

            act_step(0, 0)
            act_step(1, 1)
            with eng.Fori(1, H // 2) as it:
                act_step(it * 2, 0)
                act_step(it * 2 + 1, 1)

        @block.tensor
        def _(eng):
            eng.wait_ge(s_mk, 11)
            for n in range(J * SP):
                j, s = divmod(n, SP)
                if s == 0:
                    eng.wait_ge(s_xs[j], 1)
                q = n // 4
                ins = eng.transpose(banks[q][:, LP * (n % 4):LP * (n % 4) + LP], XS[0:LP, j, s].rearrange("p g c -> p (g c)"),
                                    ident[0:LP, 0:LP])
                if n % 4 == 3:
                    ins.then_inc(s_tr, 1)

            def pe_att(s, par):
                fixed = isinstance(s, int)
                nxt = not fixed or s + 1 < NS
                cur = not fixed or 0 <= s < NS
                prv = not fixed or 1 <= s <= NS
                prv2 = not fixed or s >= 2
                np_ = 1 - par
                def scores(part):
                    if not cur:
                        return
                    if part == 0:
                        eng.wait_ge(q_r, s + 1)
                        eng.wait_ge(km_r, s + 1)
                    if not fixed or s >= 1:
                        eng.wait_ge(sub_r, 4 * s - 2 + 2 * part)
                    for pair in range(NW // 2):
                        for e in range(2):
                            for g in (2 * part, 2 * part + 1):
                                half = (g + e) % 2
                                ins = eng.matmul(banks[g][64 * half:64 * half + 64, 196 * pair:196 * pair + 196],
                                                 Qw[C * g:C * g + C, par, 2 * pair + half, :],
                                                 Km[C * g:C * g + C, par, 2 * pair + half].rearrange("p h k -> p (h k)"),
                                                 start=True, stop=True)
                    ins.then_inc(s_r, 1)

                scores(0)
                if nxt:
                    if fixed and s < 0:
                        eng.wait_ge(s_xn, J)
                    else:
                        eng.wait_ge(k_r, s + 1)
                    if not fixed or s >= 3:
                        eng.wait_ge(x1_r, s - 2)
                    eng.matmul(banks[4][:, 0:ST], BD[:, U_Q, :], XN[:, strip(s + 1)], start=True, stop=True)
                    eng.matmul(banks[4][:, ST:2 * ST], BD[:, U_K, :], XN[:, strip(s + 1)], start=True, stop=True).then_inc(qk_d, 1)

                def project():
                    eng.wait_ge(ao_r, s - 1)
                    if nxt:
                        eng.wait_ge(k_r, s + 2)
                    elif s > NS:
                        eng.wait_ge(x1_r, NS - 1)
                    eng.matmul(banks[4][:, 0:ST], BD[:, U_P, :], AO[:, par, :], start=True, stop=True).then_inc(pj_r, 1)

                last = fixed and s == NS
                base = 6 * (s - 1) + 4 - (2 if last else 0)

                def transposes(g):
                    eng.wait_ge(pn_r, 4 * (s - 1) + g + 1)
                    if g == 0:
                        eng.wait_ge(ring_r, base if last else base - 2)
                    elif g == 1:
                        eng.wait_ge(ring_r, base)
                    else:
                        eng.wait_ge(ring_r, base + g - 1)
                    bk = banks[5 + (par + 1 + g) % 2]
                    for k in range(4):
                        pg = Pr[:, np_, g, 2 * k:2 * k + 2, :].rearrange("p h k -> p (h k)")
                        ins = eng.transpose(bk[:, P * k:P * k + P], pg, ident[:, :])
                    ins.then_inc(t_r, 1)

                def av(g):
                    eng.wait_ge(ring_r, base + g + 1)
                    if g == 0 and (not fixed or s >= 2):
                        eng.wait_ge(ao_r, s - 1)
                    for w in range(NW):
                        for e in range(2):
                            ins = eng.matmul(banks[7][C * g:C * g + C, WT * w:WT * w + WT], Vst[:, np_, w, g, e, :],
                                             PT[:, g % 2, w // 2, e, 64 * (w % 2):64 * (w % 2) + WT],
                                             start=(e == 0), stop=(e == 1))
                    ins.then_inc(av_r, 1)

                if prv:
                    transposes(0)
                    transposes(1)
                scores(1)
                if prv2:
                    project()
                if prv:
                    av(0)
                    transposes(2)
                    av(1)
                    transposes(3)
                    av(2)
                if fixed and s < 0:
                    eng.wait_ge(s_v, TRB)
                    for g in range(G):
                        rows = slice(C * g, C * g + C)
                        eng.matmul(banks[7][rows, 0:C], NB[0:R, 17, :], TB[0:R, 16, :], start=True, stop=True)
                        ins = eng.matmul(banks[7][rows, C:C + 1], wzn[:, :], lnb[:, :], start=True, stop=True)
                    ins.then_inc(s_wd, 1)
                if nxt:
                    eng.wait_ge(xw_r, s + 2)
                    if prv:
                        eng.wait_ge(ring_r, base + 3)
                    for w in range(NW):
                        ins = eng.matmul(banks[5 + (par + 1) % 2][:, P * w:P * w + P], xw[:, np_, w].rearrange("p u k -> p (u k)"),
                                         BD[:, U_V, :], start=True, stop=True)
                    ins.then_inc(v_r, 1)
                if prv:
                    av(3)

            pe_att(-1, 1)
            for s in (0, 1, 2):
                pe_att(s, s % 2)
            with eng.Fori(0, 6) as it:
                pe_att(it * 2 + 3, 1)
                pe_att(it * 2 + 4, 0)
            for s in (15, 16, 17):
                pe_att(s, s % 2)

            order = []

            def claim(name):
                last = [n for n in order if PAIR[n] == PAIR[name]]
                if last:
                    eng.wait_ge(c_[last[-1]], order.count(last[-1]))
                order.append(name)

            def product(name, w, rhs):
                claim(name)
                for h in range(2):
                    ins = eng.matmul(result(name)[0:w.shape[-1], h, :], w, rhs[:, HT * h:HT * h + HT], start=True, stop=True)
                ins.then_inc(p_[name], 1)

            img = XN[:, :].rearrange("p (b y x) -> p b y x", b=J, y=30)

            def pe_ssm(i):
                f, k, c, m, w = parts(i)

                def spread(name, n):
                    if c is None or n < 0:
                        return
                    s = "BC".index(name)
                    eng.wait_ge(g_low, 2 * c + s + 1)
                    eng.wait_ge((v_b, v_c)[s], DS * c + n)
                    for h in range(2):
                        ins = eng.matmul(result(name)[:, h, :], sel[:, n, :], upper(BCf[:, c % 2, s, HT * h:HT * h + HT]),
                                         start=True, stop=True)
                    ins.then_inc(p_[name], 1)

                def conv(first, last):
                    if f is None:
                        return
                    if first == 0:
                        eng.wait_ge(s_xn, J + f + 1)
                        claim("conv")
                    for n in range(first, last):
                        h, tap = divmod(n, 9)
                        y, x = 14 * h + tap // 3, tap % 3
                        ins = eng.matmul(result("conv")[:, h, :].rearrange("p (y x) -> p y x", x=W), BD[:, U_CV + tap, :],
                                         img[:, f, y:y + 14, x:x + W], start=(tap == 0), stop=(tap == 8))
                    if last == 18:
                        ins.then_inc(p_["conv"], 1)

                def inner(first, last):
                    if f is None:
                        return
                    if first == 0:
                        eng.wait_ge(c_["conv"], f + 1)
                        claim("u")
                    for n in range(first, last):
                        h, tap = divmod(n, 3)
                        ins = eng.matmul(result("u")[:, h, :], BD[:, U_U + tap, :], S1[:, HT * h + tap:HT * h + tap + HT],
                                         start=(tap == 0), stop=(tap == 2))
                    if last == 6:
                        ins.then_inc(p_["u"], 1)

                def slot(n):
                    spread("B", n)
                    spread("C", n - 1)

                slot(0)
                if k is not None:
                    eng.wait_ge(c_["u"], k + 1)
                    product("delta", BD[:, U_DL, :], US[:, k, :])
                    product("xB", WBC[:, 0, :], US[:, k, :])
                slot(1)
                if k is not None:
                    product("xC", WBC[:, 1, :], US[:, k, :])
                slot(2)
                conv(0, 2)
                if m is not None:
                    eng.wait_ge(v_y2, m + 1)
                    product("out", BD[:, U_OUT, :], y2[:, :])
                conv(2, 4)
                slot(3)
                conv(4, 6)
                if w is not None:
                    eng.wait_ge(g_nt2, w + 1)
                    product("wout", BD[:, U_WO, :], nt[:, 2, :])
                conv(6, 8)
                slot(4)
                conv(8, 12)
                if m is not None:
                    eng.wait_ge(c_["out"], m + 1)
                    product("var", VB[:, :], sq[:, :])
                slot(5)
                conv(12, 16)
                slot(6)
                conv(16, 18)
                if f is not None:
                    claim("x2")
                    for h in range(2):
                        ins = eng.matmul(result("x2")[:, h, :].rearrange("p (y x) -> p y x", x=W), BD[:, U_X2, :],
                                         img[:, f, 14 * h + 1:14 * h + 15, 1:W + 1], start=True, stop=True)
                    ins.then_inc(p_["x2"], 1)
                inner(0, 4)
                slot(7)
                inner(4, 6)
                spread("C", 7)
                if f is not None:
                    product("z", BD[:, U_Z, :], S1[:, 2:T + 2])

            eng.wait_ge(s1z, 1)
            for i in SSM_STEPS:
                pe_ssm(i)

            eng.wait_ge(s_xn, 3 * J)
            for n in range(14):
                side, q = n // 7, n % 7
                if n >= 4:
                    eng.wait_ge(t_p1, n - 3)
                if n == 7:
                    eng.wait_ge(t_xr, 1)
                bk = banks[FACTORS[n % 4]]
                for r in range(4):
                    i = 4 * q + r
                    ins = eng.matmul(bk[:, P * r:P * r + P], XR[:, side, i].rearrange("p b k -> p (b k)"),
                                     BD[:, U_A + side, :], start=True, stop=True)
                ins.then_inc(t_pr, 1)
                if 3 <= n < 11:
                    m = n - 3
                    if m >= 2:
                        eng.wait_ge(t_gd, m - 1)
                    eng.matmul(banks[2 + m % 2][:, 0:HT].rearrange("p (y x) -> p y x", x=W), BD[:, U_G, :],
                               XR[:, 0, 14 * (m % 2):14 * (m % 2) + 14, m // 2, 0:W], start=True, stop=True).then_inc(t_g, 1)
            eng.wait_ge(t_sg, 14)
            for g in range(G):
                if g == 1:
                    eng.wait_ge(t_gd, 8)
                if g >= 2:
                    eng.wait_ge(t_zc, g - 1)
                    eng.wait_ge(t_za, g - 1)
                first = 4 - 4 * (g % 2)
                for c in range(C2):
                    for b in range(J):
                        m = C2 * g + c
                        ins = eng.matmul(banks[first + b][32 * b:32 * b + H, H * c:H * c + H], Ab[32 * b:32 * b + H, 0, m, :],
                                         Ab[32 * b:32 * b + H, 1, m, :], start=True, stop=True)
                ins.then_inc(t_z, 1)
            for q in range(14):
                if q % 4 == 0:
                    eng.wait_ge(t_n, q // 4 + 1)
                if q % 4 == 0 and q >= 8:
                    eng.wait_ge(t_te, q // 4 - 1)
                ins = eng.transpose(banks[4 + (q // 4) % 2][:, P * (q % 4):P * (q % 4) + P],
                                    Zc[:, 2 * q:2 * q + 2, :].rearrange("p j m -> p (j m)"), ident[:, :])
                if q % 4 == 3 or q == 13:
                    ins.then_inc(t_t, 1)
            for n in range(8):
                q, par = n % 4, n // 4
                m = min(4, 14 - 4 * q) * P
                eng.wait_ge(t_te, q + 1)
                if n >= 4:
                    eng.wait_ge(t_y, n - 3)
                eng.matmul(banks[LAST[n % 4]][:, 0:m], WZ[:, par, :], ZT[:, 512 * q:512 * q + m],
                           start=True, stop=True).then_inc(t_o, 1)

            def residual(q):
                if q >= 2:
                    eng.wait_ge(r_te, q - 1)
                for k in range(4):
                    ins = eng.transpose(banks[2 + q % 2][0:112, P * k:P * k + P], X[:, 112 * (4 * q + k):112 * (4 * q + k) + 112], ident[:, :])
                ins.then_inc(r_x, 1)

            def biases(t, par):
                if not isinstance(t, int) or t >= 2:
                    eng.wait_ge(r_g, t - 1)
                eng.matmul(banks[par][:, 0:336].rearrange("p (k n) -> p k n", k=3), BL[:, :, :].rearrange("k g c -> k (g c)"),
                           bcast(ident[0:3, 0:3], 2, 112), start=True, stop=False, skip_group_check=True)

            def inputs(t, par):
                if not isinstance(t, int) or t >= 2:
                    biases(t, par)
                zb = banks[par]
                xt = XN[:, 0:N].rearrange("p (b t) -> p b t", b=J)[:, :, bass.ds(t * W, W)]
                if not isinstance(t, int) or t >= 2:
                    eng.wait_ge(r_go, t - 1)
                for k in range(1, 4):
                    eng.matmul(zb[:, 112 * k - 112:112 * k].rearrange("p (b n) -> p b n", b=J), BD[:, U_X + k, :], xt,
                               start=False, stop=False, skip_group_check=True)
                eng.matmul(banks[6 + par][:, 0:112].rearrange("p (b n) -> p b n", b=J), BD[:, U_X, :], xt,
                           start=True, stop=False, skip_group_check=True)

            def recur(t, par):
                zb = banks[par]
                if not isinstance(t, int) or t >= 1:
                    eng.wait_ge(r_h, t)
                else:
                    eng.wait_ge(r_in, 1)
                for k in range(1, 4):
                    ins = eng.matmul(zb[:, 112 * k - 112:112 * k], BD[:, U_M + k, :], hst[:, 1 - par, :], start=False, stop=True,
                                     skip_group_check=True)
                ins.then_inc(r_z, 1)
                eng.matmul(banks[6 + par][:, 0:112], BD[:, U_M, :], hst[:, 1 - par, :], start=False, stop=True,
                           skip_group_check=True).then_inc(r_zo, 1)

            def turn(t, par):
                eng.wait_ge(r_h, t + 1)
                if not isinstance(t, int) or t >= 2:
                    eng.wait_ge(r_o, t - 1)
                eng.transpose(banks[4 + par][0:112, 0:P], hst[:, par, :], ident[:, :]).then_inc(r_t, 1)

            biases(0, 0)
            biases(1, 1)
            eng.wait_ge(s_xn, 4 * J)
            inputs(0, 0)
            recur(0, 0)
            residual(0)
            inputs(1, 1)
            for t in range(1, 7):
                recur(t, t % 2)
                residual(t)
                turn(t - 1, 1 - t % 2)
                inputs(t + 1, 1 - t % 2)
            with eng.Fori(3, H // 2 - 1) as it:
                recur(it * 2 + 1, 1)
                turn(it * 2, 0)
                inputs(it * 2 + 2, 0)
                recur(it * 2 + 2, 0)
                turn(it * 2 + 1, 1)
                inputs(it * 2 + 3, 1)
            recur(H - 1, 1)
            turn(H - 2, 0)
            turn(H - 1, 1)

        @block.vector
        def _(eng):
            chain = [0]

            def link(ins):
                chain[0] += 1
                ins.then_inc(s_v, 1)
                eng.wait_ge(s_v, chain[0])

            eng.memset(epsc[:, :], EPS).then_inc(s_ev, 1)
            for j in range(0, J, 2):
                eng.wait_ge(s_x[j], 16)
                eng.tensor_copy(XS[0:LP, j].rearrange("p s g c -> p g s c"), XT[0:LP, j]).then_inc(s_xs[j], 1)
            for q in range(0, 7, 2):
                eng.wait_ge(s_tr, q + 1)
                evac_in(eng, q)

            def column_stats(j):
                for h in range(2):
                    ins = eng.bn_stats(stats[:, j, h, :], X[:, T * j + HT * h:T * j + HT * h + HT])
                return ins

            def gn_stats(layer, first=0):
                if layer:
                    eng.wait_ge(s_xn, J * layer)
                for j in range(first, J):
                    ins = column_stats(j)
                link(ins)
                for j in range(J):
                    ins = eng.bn_aggr(mv[:, j, :], stats[:, j].rearrange("p h s -> p (h s)"))
                ins.then_inc(s_mv, 1)
                eng.wait_ge(s_mv, layer + 1)

            def gn_apply(layer, dst):
                eng.wait_ge(s_rs, layer + 1)
                for j in range(J):
                    src = X[:, T * j:T * j + T]
                    d = dst(j)
                    if len(d.shape) == 3:
                        src = src.rearrange("p (y x) -> p y x", y=H)
                    eng.tensor_scalar(d, src, mv[:, j, 0:1], rstd[:, j:j + 1], ALU.subtract, ALU.mult).then_inc(s_xn, 1)

            eng.wait_ge(s_ev, 8)
            gn_stats(0)

            eng.wait_ge(s_mk, 11)
            loaded(eng, 0)

            def spread_weights(u0, u1):
                return eng.tensor_tensor(BD[:, u0:u1, :].rearrange("p u (g c) -> p u g c", g=G), bcast(W4[:, u0:u1, :], 2, G),
                                         bcast(bcast(bd[:, :], 1, u1 - u0), 3, C), ALU.mult)
            eng.tensor_scalar(vec[:, V_BQS:V_BQS + 1], vec[:, V_BQ:V_BQ + 1], SCALE, None, ALU.mult)
            eng.tensor_reduce(mask8[:, :], m16[:, :].rearrange("p (g h) -> p h g", g=G), AX.X, ALU.add)
            spread_weights(U_Q, U_P + 1)
            gn_apply(0, lambda j: XN[:, T * j:T * j + T])

            loaded(eng, 1)
            eng.wait_ge(s_hf, 2)
            link(eng.tensor_tensor(maskz[:, :], m8[:, 0:4], m8[:, 4:8], ALU.add))
            for k, dst in ((0, W8X[:, :]), (1, NB[:, 1, :]), (2, NB[:, 2, :])):
                ins = eng.tensor_tensor(dst.rearrange("p (h i) -> p h i", h=4), bcast(W8[:, k, :], 1, 4), bcast(mask8[:, :], 2, 8), ALU.mult)
            link(ins)
            for k in range(3):
                eng.tensor_scalar(NB[:, 4 + k, :], WIN[:, 0, :], C1[:, k:k + 1], None, ALU.mult)
            for k in range(9):
                ins = eng.tensor_scalar(NB[:, 7 + k, :], W8X[:, :], DW[:, k:k + 1], None, ALU.mult)
            link(ins)
            link(eng.transpose(TB[:, :, :].rearrange("p u c -> p (u c)"), NB[:, :, :].rearrange("p u c -> p (u c)")))
            assert chain[0] == TRB
            link(eng.tensor_reduce(omean[:, :], TB[:, 3, :], AX.X, ALU.add))
            link(eng.tensor_scalar(omean[:, :], omean[:, :], 1.0 / C, None, ALU.mult))
            link(eng.tensor_scalar(TB[:, 3, :], TB[:, 3, :], omean[:, 0:1], None, ALU.subtract))
            eng.tensor_copy(W4[:, U_Z:U_DL, :], TB[:, 0:16, :])
            eng.wait_ge(s_wd, 1)
            eng.tensor_copy(W4[:, U_DL, :], banks[7][:, 0:C])
            link(eng.tensor_tensor(vec[:, V_BZF:V_BZF + 1], vec[:, V_BZ:V_BZ + 1], banks[7][:, C:C + 1], ALU.add))
            spread_weights(U_Z, NU)
            for s in range(2):
                for q in range(3):
                    eng.tensor_tensor(WBC[:, s, C * q:C * q + C].rearrange("p (g n) -> p g n", g=G),
                                      bcast(TB[:, 17, R + DS * s:R + DS * s + DS], 1, G), bcast(bd[:, :], 2, DS), ALU.mult)
            for q in range(3):
                rows = slice(C * q, C * q + C)
                eng.tensor_copy(sel[rows].rearrange("p n (g c) -> p n g c", g=G),
                                bcast(ident[rows, rows].rearrange("p (g n) -> p n g", g=G), 3, C))
            eng.tensor_scalar(VB[:, :].rearrange("p (g c) -> p g c", g=G), bcast(bd[:, :], 2, C), 1.0 / C, None, ALU.mult)
            eng.wait_ge(s_ae, 1)
            link(eng.tensor_scalar(Aneg[:, :], AE[:, :], -1.0, None, ALU.mult))

            eng.wait_ge(s_mk2, 4)

            def dve_att(s, par):
                fixed = isinstance(s, int)
                cur = not fixed or 0 <= s < NS
                prv = not fixed or 1 <= s <= NS
                prv2 = not fixed or s >= 2
                np_ = 1 - par
                if cur:
                    for part in range(2):
                        groups = (2 * part, 2 * part + 1)
                        eng.wait_ge(s_r, 2 * s + part + 1)
                        for g in groups:
                            eng.tensor_reduce(mx[:, g, :], banks[g][:, 0:392].rearrange("p (m k) -> p m k", k=WT), AX.X,
                                              ALU.max).then_inc(max_r, 1)
                        for g in groups:
                            eng.wait_ge(max_r, 4 * s + g + 1)
                            if not fixed or s >= 1:
                                eng.wait_ge(exp_r, 4 * (s - 1) + g + 1)
                            eng.tensor_tensor(Ts[:, g, :, :], banks[g][:, 0:392].rearrange("p (m k) -> p m k", k=WT),
                                              bcast(mx[:, g, :], 2, WT), ALU.subtract).then_inc(sub_r, 1)
                if prv2:
                    eng.wait_ge(pj_r, s - 1)
                    xs = X[:, strip(s - 2)]
                    eng.scalar_tensor_tensor(xs, banks[4][:, 0:ST], vec[:, V_BP:V_BP + 1], xs, ALU.add, ALU.add).then_inc(x1_r, 1)
                if cur:
                    for g in range(G):
                        eng.wait_ge(exp_r, 4 * s + g + 1)
                        if not fixed or s >= 1:
                            eng.wait_ge(pn_r, 4 * (s - 1) + g + 1)
                        eng.tensor_reduce(sm[:, g, :], Pr[:, par, g, :, 0:WT], AX.X, ALU.add).then_inc(sum_r, 1)
                    for g in range(G):
                        eng.wait_ge(sum_r, 4 * s + g + 1)
                        eng.reciprocal(rc[:, g, :], sm[:, g, :]).then_inc(rec_r, 1)
                if prv:
                    eng.wait_ge(av_r, 4 * s)
                    eng.tensor_scalar(windows(AO[:, np_, :]), banks[7][:, 0:ST].rearrange("p (w r c) -> p w r c", w=NW, r=WS),
                                      vec[:, V_BV:V_BV + 1], None, ALU.add).then_inc(ao_r, 1)

            for s in (0, 1, 2):
                dve_att(s, s % 2)
            with eng.Fori(0, 6) as it:
                dve_att(it * 2 + 3, 1)
                dve_att(it * 2 + 4, 0)
            for s in (15, 16, 17):
                dve_att(s, s % 2)
                if s < 17:
                    for j in ((0, 1), (2,))[s - 15]:
                        eng.wait_ge(x1_r, NS // J * (j + 1))
                        column_stats(j)

            eng.wait_ge(x1_r, NS)
            gn_stats(1, first=J - 1)
            eng.wait_ge(s_bd, 1)
            img = XN[:, :].rearrange("p (b y x) -> p b y x", b=J, y=30)
            gn_apply(1, lambda j: img[:, j, 1:29, 1:29])
            loaded(eng, 2)
            eng.tensor_scalar(W4[:, U_X:U_X + 3, :], W4[:, U_X:U_X + 3, :], 0.5, None, ALU.mult)
            eng.tensor_scalar(W4[:, U_M:U_M + 3, :], W4[:, U_M:U_M + 3, :], 0.25, None, ALU.mult)
            eng.tensor_scalar(W4[:, U_M + 3, :], W4[:, U_M + 3, :], 0.5, None, ALU.mult)
            eng.tensor_scalar(vec[:, V_BO:V_BO + 1], vec[:, V_BO:V_BO + 1], 0.5, None, ALU.mult)
            link(eng.tensor_scalar(BL[:, :, :], BL[:, :, :], half3[:, 0:1], None, ALU.mult))
            spread_weights(U_A, U_Z)
            eng.memset(WZ[:, :, :], 0.0)
            link(eng.tensor_scalar(wzs[:, :], wzraw[:, :], vec[:, V_LG:V_LG + 1], None, ALU.mult))
            for par in range(2):
                rows = slice(64 * par, 64 * par + 64)
                eng.tensor_tensor(WZ[rows, par].rearrange("p (g c) -> p g c", g=G), bcast(wzs[rows], 1, G), bcast(maskz[rows], 2, C), ALU.mult)

            def dve_ssm(i):
                f, k, c, m, w = parts(i)

                def times_b(n):
                    eng.wait_ge(p_["B"], DS * c + n + 1)
                    eng.wait_ge(v_du, c + 1)
                    if DS * c + n >= 2:
                        eng.wait_ge(v_s, DS * c + n - 1)
                    eng.tensor_tensor(halves(dBu[:, n % 2, :]), halves(DU[:, :]), result("B"), ALU.mult).then_inc(v_b, 1)

                def scan(n):
                    eng.wait_ge(v_b, DS * c + n + 1)
                    eng.wait_ge(a_da, DS * c + n + 1)
                    if DS * c + n >= 2:
                        eng.wait_ge(v_c, DS * c + n - 1)
                    eng.tensor_tensor_scan(Hs[:, n % 2, :], dA[:, n % NA, :], dBu[:, n % 2, :], 0.0, ALU.mult, ALU.add).then_inc(v_s, 1)

                def times_c(n):
                    eng.wait_ge(p_["C"], DS * c + n + 1)
                    eng.wait_ge(v_s, DS * c + n + 1)
                    if n == 0:
                        dst = YA[:, c % 2, :]
                    else:
                        dst = hC[:, n % NHC, :]
                        before = (DS - 1) * c + n - NHC if n > NHC else (DS - 1) * c + min(n - NHC, 0)
                        if before > 0:
                            eng.wait_ge(g_ya, before)
                    eng.tensor_tensor(halves(dst), halves(Hs[:, n % 2, :]), result("C"), ALU.mult).then_inc(v_c, 1)

                def slot(n):
                    if c is not None:
                        times_b(n)
                        if n:
                            times_c(n - 1)
                        scan(n)

                if w is not None:
                    if w == J - 1:
                        eng.wait_ge(c_["wout"], J - 1)
                        for j in range(J - 1):
                            column_stats(j)
                    if w == J - 1:
                        eng.wait_ge(a_rs, J)
                        eng.tensor_tensor(nt[:, 0, :], cS[:, :], rs[:, :], ALU.mult).then_inc(g_nt0, 1)
                    eng.wait_ge(g_nt0, w + 1)
                    if w:
                        eng.wait_ge(g_nt2, w)
                    eng.tensor_scalar(nt[:, 1, :], nt[:, 0, :], vec[:, V_GA:V_GA + 1], vec[:, V_BE:V_BE + 1],
                                      ALU.mult, ALU.add).then_inc(v_nt1, 1)
                    if w == J - 1:
                        eng.wait_ge(v_nt1, J)
                        eng.wait_ge(p_["wout"], J - 1)
                        eng.tensor_tensor(nt[:, 2, :], nt[:, 1, :], X2[:, J - 1, :], ALU.mult).then_inc(g_nt2, 1)
                slot(0)
                slot(1)
                if m is not None:
                    eng.wait_ge(g_ya, (DS - 1) * (m + 1))
                    if m:
                        eng.wait_ge(v_y2, m)
                    eng.scalar_tensor_tensor(y1[:, :], US[:, m, :], vec[:, V_D:V_D + 1], YA[:, m % 2, :], ALU.mult, ALU.add).then_inc(v_y1, 1)
                    eng.wait_ge(v_y1, m + 1)
                    if m:
                        eng.wait_ge(p_["out"], m)
                    eng.wait_ge(c_["z"], m + 1)
                    eng.tensor_tensor(y2[:, :], y1[:, :], ZS[:, m, :], ALU.mult).then_inc(v_y2, 1)
                slot(2)
                slot(3)
                if k is not None:
                    eng.wait_ge(a_u, k + 1)
                    eng.scalar_tensor_tensor(sp[:, SP_C, :], sp[:, SP_U, :], 1.0, sp[:, SP_E, :], ALU.subtract, ALU.subtract).then_inc(v_cc, 1)
                if w is not None:
                    eng.wait_ge(p_["wout"], w + 1)
                    xs = X[:, w * T:w * T + T]
                    eng.tensor_tensor(halves(xs), halves(xs), result("wout"), ALU.add).then_inc(c_["wout"], 1)
                slot(4)
                slot(5)
                slot(6)
                slot(7)
                if k is not None:
                    eng.wait_ge(g_ml, k + 1)
                    eng.wait_ge(g_cw, k + 1)
                    if k >= 2:
                        eng.wait_ge(a_da, DS * (k - 1))
                    eng.tensor_tensor(DL[:, k % 2, :], sp[:, SP_M, :], sp[:, SP_C, :], ALU.subtract).then_inc(v_dl, 1)
                if k is not None:
                    eng.wait_ge(v_dl, k + 1)
                    if k:
                        eng.wait_ge(v_b, DS * k)
                    eng.tensor_tensor(DU[:, :], DL[:, k % 2, :], US[:, k, :], ALU.mult).then_inc(v_du, 1)
                if c is not None:
                    times_c(DS - 1)

            for i in SSM_STEPS:
                dve_ssm(i)

            eng.wait_ge(c_["wout"], J)
            gn_stats(2, first=J - 1)
            eng.wait_ge(t_zz, 2)
            gn_apply(2, lambda j: XR[:, 0, :, j, 0:W])
            for n in range(14):
                eng.wait_ge(t_pr, n + 1)
                if n >= 4:
                    eng.wait_ge(t_pp, n - 3)
                eng.tensor_tensor(p1[:, n % 4].rearrange("p (m c) -> p m c", m=16), banks[FACTORS[n % 4]][:, :].rearrange("p (m c) -> p m c", m=16),
                                  bcast(BAB[:, n // 7, :], 1, 16), ALU.add).then_inc(t_p1, 1)
            for s in range(G + 1):
                if s < G:
                    g = s
                    eng.wait_ge(t_z, g + 1)
                    take_z(eng, g, (0,)).then_inc(t_zc, 1)
                    eng.wait_ge(t_zc, g + 1)
                    eng.wait_ge(t_za, g + 1)
                    zg = Zc[:, :, C2 * g:C2 * g + C2]
                    link(eng.tensor_reduce(zst[:, 0, g, :], zg, AX.X, ALU.add))
                    eng.scalar_tensor_tensor(zg, bcast(zst[:, 0, g, :], 2, C2), -1.0 / C2, zg, ALU.mult, ALU.add).then_inc(t_c, 1)
                if s:
                    g = s - 1
                    eng.wait_ge(t_q, g + 1)
                    eng.tensor_reduce(zst[:, 1, g, :], Zq[:, g % 2].rearrange("p (j c) -> p j c", c=C2), AX.X, ALU.add).then_inc(t_v, 1)
            eng.wait_ge(t_r2, 1)
            eng.wait_ge(t_c, G)
            for q in range(4):
                cols = slice(8 * q, min(8 * q + 8, H))
                zq = Zc[:, cols, :].rearrange("p j (g c) -> p j g c", g=G)
                eng.tensor_tensor(zq, zq, bcast(zst[:, 3, :, cols].rearrange("p g j -> p j g"), 3, C2), ALU.mult).then_inc(t_n, 1)
            eng.wait_ge(t_gd, 8)
            for n in range(8):
                q, par = n % 4, n // 4
                w = min(4, 14 - 4 * q)
                eng.wait_ge(t_o, n + 1)
                src = banks[LAST[n % 4]][:, 0:P * w].rearrange("p (j b i) -> p j b i", j=w, b=J)[:, :, :, 0:H]
                Yv, Gv = [m[:, :, :].rearrange("p b (i j e) -> p e b i j", i=H, e=2)[:, par] for m in (Y, Gt)]
                js = slice(4 * q, 4 * q + w)
                Yj, Gj = [m[:, :, :, js].rearrange("p b i j -> p j b i") for m in (Yv, Gv)]
                eng.scalar_tensor_tensor(Yj, src, vec[:, V_BZF:V_BZF + 1], Gj, ALU.add, ALU.mult).then_inc(t_y, 1)
            eng.memset(hst[:, :, :], 0.0)
            eng.memset(gates[:, 0, 4, :], 0.0).then_inc(r_in, 1)
            eng.wait_ge(t_y, 8)
            for j in range(J):
                xs = X[:, T * j:T * j + T]
                eng.tensor_tensor(xs, xs, Y[:, j, :], ALU.add).then_inc(t_x3, 1)
                if j:
                    eng.wait_ge(t_x3, j)
                    column_stats(j - 1)
            eng.wait_ge(t_x3, J)

            gn_stats(3, first=J - 1)
            gn_apply(3, lambda j: XN[:, T * j:T * j + T])
            eng.wait_ge(r_in, 1)
            Rv = Rt[:, :, :].rearrange("p (g m) c -> p m g c", g=G)

            def output(t, par):
                eng.wait_ge(r_t, t + 1)
                if isinstance(t, int) and t < 7:
                    eng.wait_ge(r_te, t + 1)
                if not isinstance(t, int) or t >= 2:
                    eng.wait_ge(s_out[par], (t - par) * 8)
                eng.scalar_tensor_tensor(Os[:, par].rearrange("p g c -> p (g c)"), banks[4 + par][0:112, 0:P], 0.5,
                                         Rt[:, bass.ds(t * 4, 4), :].rearrange("p g c -> p (g c)"), ALU.mult, ALU.add).then_inc(r_o, 1)

            def dve_step(t, par):
                eng.wait_ge(r_g, t + 1)
                eng.scalar_tensor_tensor(prods[:, :, :], gates[:, par, 1:3, :], 1.0, gates[:, par, 3:5, :],
                                         ALU.add, ALU.mult).then_inc(r_1, 1)
                eng.wait_ge(r_1, t + 1)
                eng.scalar_tensor_tensor(gates[:, 1 - par, 4, :], prods[:, 1, :], 0.5, prods[:, 0, :],
                                         ALU.mult, ALU.add).then_inc(r_c, 1)
                if not isinstance(t, int) or t >= 1:
                    output(t - 1, 1 - par)
                eng.wait_ge(r_go, t + 1)
                eng.wait_ge(r_th, t + 1)
                eng.scalar_tensor_tensor(hst[:, par, :], gates[:, par, 0, :], 1.0, tcn[:, :], ALU.add, ALU.mult).then_inc(r_h, 1)

            for t in range(8):
                dve_step(t, t % 2)
                if t < 7:
                    eng.wait_ge(r_x, t + 1)
                    eng.tensor_copy(Rv[:, 4 * t:4 * t + 4], banks[2 + t % 2][0:112, :].rearrange("p (m g c) -> p m g c", m=4, g=G)).then_inc(r_te, 1)
            with eng.Fori(4, H // 2) as it:
                dve_step(it * 2, 0)
                dve_step(it * 2 + 1, 1)
            output(H - 1, 1)


_INS = ['x', 'L0_conv_w_qkv', 'L0_conv_b_qkv', 'L0_conv_w_proj', 'L0_conv_b_proj', 'L1_conv_w1', 'L1_conv_dw',
        'L1_conv_in_proj_w', 'L1_conv_conv1d_w', 'L1_conv_conv1d_b', 'L1_conv_x_proj_w', 'L1_conv_dt_proj_w',
        'L1_conv_dt_proj_b', 'L1_conv_A_log', 'L1_conv_D_param', 'L1_conv_out_proj_w', 'L1_conv_gamma', 'L1_conv_beta',
        'L1_conv_w2', 'L1_conv_wout', 'L2_conv_Wa1', 'L2_conv_ba1', 'L2_conv_Wa2', 'L2_conv_ba2', 'L2_conv_Wb1',
        'L2_conv_bb1', 'L2_conv_Wb2', 'L2_conv_bb2', 'L2_conv_ln2_g', 'L2_conv_ln2_b', 'L2_conv_Wg', 'L2_conv_bg',
        'L2_conv_Wz', 'L2_conv_bz', 'L3_conv_Wix', 'L3_conv_Wim', 'L3_conv_Wfx', 'L3_conv_Wfm', 'L3_conv_Wcx',
        'L3_conv_Wcm', 'L3_conv_Wox', 'L3_conv_Wom', 'L3_conv_bi', 'L3_conv_bf', 'L3_conv_bc', 'L3_conv_bo']


def kernel(**inputs):
    import concourse.bacc as _bacc
    from concourse.bass_utils import run_bass_kernel_spmd as _run

    nc = _bacc.Bacc("TRN2", target_bir_lowering=False, num_devices=1)
    arrays, aps = {}, {}
    for name in _INS:
        v = np.ascontiguousarray(inputs[name])
        arrays[f"in_{name}"] = v
        aps[name] = nc.dram_tensor(f"in_{name}", v.shape, mybir.dt.from_np(v.dtype), kind="ExternalInput").ap()
    out = nc.dram_tensor("out", (B, H, W, C), F32, kind="ExternalOutput").ap()
    build(nc, aps, out)
    r = _run(nc, [arrays], core_ids=[0])
    return r.results[0]["out"]
```
